# Optimizing a Trainium2 kernel written in Bass

```python
import numpy as np
import jax
import jax.numpy as jnp

def _softmax(x, axis=-1):
    return jax.nn.softmax(x, axis=axis)

def _gelu(x):
    return jax.nn.gelu(x, approximate=True)

def _silu(x):
    return jax.nn.silu(x)

def _sigmoid(x):
    return jax.nn.sigmoid(x)

def _layernorm(x, axis=-1, eps=1e-05):
    m = jnp.mean(x, axis=axis, keepdims=True)
    v = jnp.var(x, axis=axis, keepdims=True)
    return (x - m) / jnp.sqrt(v + eps)

def _scatter_add(tgt, idx, src, axis=0):
    return tgt.at[idx].add(src)

def _segment_sum(src, seg, n):
    return jax.ops.segment_sum(src, seg, n)
kernel_name = 'mk_decoder_postln_d4_seqx_r8_95af0c'

def setup_inputs(seed: int=0):
    np.random.seed(seed)
    _w = jnp.asarray

    def _rec_inputs():
        import jax
        import jax.numpy as jnp
        _rk = jax.random.key(seed)
        x = -0.0005146 + 1 * jax.random.normal(jax.random.fold_in(_rk, 1), (16, 128, 128), jnp.float32)
        _lenS = 128 - jax.random.randint(jax.random.fold_in(_rk, 7), (16,), 0, max(1, 128 // 4) + 1, jnp.int32)
        _lenS2 = 120 - jax.random.randint(jax.random.fold_in(_rk, 8), (16,), 0, max(1, 120 // 4) + 1, jnp.int32)
        _ctx_768P = jax.random.normal(jax.random.fold_in(_rk, 11), (16, 16, 96), jnp.float32)
        _ctx_768c = jax.random.dirichlet(jax.random.fold_in(_rk, 511), 0.3 * jnp.ones((16,), jnp.float32), (16, 120))
        _ctx_768t = jnp.einsum('bsk,bkd->bsd', _ctx_768c, _ctx_768P)
        _ctx_768t = _ctx_768t * jax.lax.rsqrt(jnp.mean(jnp.square(_ctx_768t)) + 1e-12) * 0.953939
        ctx_768 = -0.00040386 + 0.999972 * (_ctx_768t + 0.3 * jax.random.normal(jax.random.fold_in(_rk, 611), (16, 120, 96), jnp.float32))
        _validS = jnp.arange(128)[None, :] < _lenS[:, None]
        _validS2 = jnp.arange(120)[None, :] < _lenS2[:, None]
        _causal = jnp.tril(jnp.ones((128, 128), dtype=bool))
        mask_BxS2_bk0 = jnp.logical_not(jnp.broadcast_to(_validS2[:, :], (16, 120)))
        mask_BxS_bf1 = jnp.ones((16, 128), dtype=bool)
        mask_BxS2_bf1 = jnp.ones((16, 120), dtype=bool)
        return (x, ctx_768, mask_BxS2_bk0, mask_BxS_bf1, mask_BxS2_bf1)
    x, ctx_768, mask_BxS2_bk0, mask_BxS_bf1, mask_BxS2_bf1 = _rec_inputs()

    def _L0_attn_setup():
        import jax, jax.numpy as jnp
        import numpy as np
        DIM = 128
        H = 16
        D = DIM // H
        CS = 64
        SCALE = D ** (-0.5)
        key = jax.random.key(seed)
        k1, k2, k3 = jax.random.split(key, 3)
        B, N = (4, 512)
        x = jax.random.normal(k1, (B, N, DIM), dtype=jnp.float32)
        W_qkv = jax.random.normal(k2, (DIM, 3 * DIM), dtype=jnp.float32) * DIM ** (-0.5)
        W_out = jax.random.normal(k3, (DIM, DIM), dtype=jnp.float32) * DIM ** (-0.5)
        return {'x': x, 'W_qkv': W_qkv, 'W_out': W_out}
    _L0_attn_all = _L0_attn_setup()
    _L0_attn_in = {k: v for k, v in _L0_attn_all.items() if k in ('W_qkv', 'W_out')}
    del _L0_attn_all

    def _L0_xattn_setup():
        import jax, jax.numpy as jnp
        import numpy as np
        DIM_IN, DIM_LAT, DIM_HEAD = (96, 128, 64)
        INNER = max(DIM_LAT, DIM_IN)
        HEADS = INNER // DIM_HEAD
        SCALE = DIM_HEAD ** (-0.5)
        RMS_EPS = 1e-08
        LN_EPS = 1e-05

        def layernorm(x, g, b):
            mu = jnp.mean(x, axis=-1, keepdims=True)
            var = jnp.mean((x - mu) ** 2, axis=-1, keepdims=True)
            return (x - mu) * jax.lax.rsqrt(var + LN_EPS) * g + b

        def rmsnorm(x, gamma):
            norm = jnp.sqrt(jnp.sum(x * x, axis=-1, keepdims=True)) * x.shape[-1] ** (-0.5)
            return x / jnp.maximum(norm, RMS_EPS) * gamma
        key = jax.random.key(seed)
        ks = jax.random.split(key, 12)
        b, n, m = (4, 512, 64)
        x = jax.random.normal(ks[0], (b, n, DIM_IN), jnp.float32)
        latents = jax.random.normal(ks[1], (b, m, DIM_LAT), jnp.float32)
        mask = jax.random.randint(ks[2], (b, n), 0, 2).astype(bool)
        s = lambda k, sh, fan: jax.random.normal(k, sh, jnp.float32) * fan ** (-0.5)
        return {'x': x, 'latents': latents, 'mask': mask, 'ln_x_g': jnp.ones((DIM_IN,), jnp.float32), 'ln_x_b': jnp.zeros((DIM_IN,), jnp.float32), 'ln_l_g': jnp.ones((DIM_LAT,), jnp.float32), 'ln_l_b': jnp.zeros((DIM_LAT,), jnp.float32), 'qn_g': jnp.ones((DIM_HEAD,), jnp.float32), 'kn_g': jnp.ones((DIM_HEAD,), jnp.float32), 'Wq': s(ks[3], (INNER, DIM_LAT), DIM_LAT), 'Wkv': s(ks[4], (2 * INNER, DIM_IN), DIM_IN), 'Wlkv': s(ks[5], (2 * INNER, DIM_LAT), DIM_LAT), 'Wo': s(ks[6], (DIM_LAT, INNER), INNER), 'bo': jnp.zeros((DIM_LAT,), jnp.float32)}
    _L0_xattn_all = _L0_xattn_setup()
    _L0_xattn_in = {k: v for k, v in _L0_xattn_all.items() if k in ('ln_x_g', 'ln_x_b', 'ln_l_g', 'ln_l_b', 'qn_g', 'kn_g', 'Wq', 'Wkv', 'Wlkv', 'Wo', 'bo')}
    del _L0_xattn_all

    def _L0_ffn_setup():
        import jax, jax.numpy as jnp
        import numpy as np
        DIM = 128
        DEPTH = 6
        HEADS = 16
        DIM_HEAD = 64
        WINDOW = 32
        INNER = HEADS * DIM_HEAD
        DIM_INNER = int(DIM * 4 * 2 / 3)
        QK_SCALE = 8.0

        def shift_tokens(t):
            a, s = jnp.split(t, 2, -1)
            s = jnp.pad(s, ((0, 0), (1, 0), (0, 0)))[:, :-1]
            return jnp.concatenate([a, s], -1)

        def l2norm(t):
            return t / jnp.maximum(jnp.linalg.norm(t, axis=-1, keepdims=True), 1e-12)

        def rotate_half(x):
            x1, x2 = jnp.split(x, 2, -1)
            return jnp.concatenate([-x2, x1], -1)

        def rotary_tables(n):
            half = jnp.arange(0, DIM_HEAD, 2, dtype=jnp.float32)
            inv_freq = 1.0 / 10000.0 ** (half / DIM_HEAD)
            t = jnp.arange(n, dtype=jnp.float32)
            freqs = t[:, None] * inv_freq[None, :]
            freqs = jnp.concatenate([freqs, freqs], -1)
            base_scale = (half + 0.4 * DIM_HEAD) / (1.4 * DIM_HEAD)
            power = (t - n // 2) / (WINDOW // 2)
            scale = base_scale[None, :] ** power[:, None]
            scale = jnp.concatenate([scale, scale], -1)
            return (freqs, scale)

        def local_attention(q, k, v):
            b, h, n, d = q.shape
            w = WINDOW
            nw = n // w
            bq = q.reshape(b, h, nw, w, d)
            bk = k.reshape(b, h, nw, w, d)
            bv = v.reshape(b, h, nw, w, d)

            def look(t):
                p = jnp.pad(t, ((0, 0), (0, 0), (1, 0), (0, 0), (0, 0)))
                return jnp.concatenate([p[:, :, :nw], p[:, :, 1:]], axis=3)
            bk2, bv2 = (look(bk), look(bv))
            seq = jnp.arange(n).reshape(nw, w)
            seq_p = jnp.pad(seq, ((1, 0), (0, 0)), constant_values=-1)
            jt = jnp.concatenate([seq_p[:nw], seq_p[1:]], axis=1)
            it = seq[:, :, None]
            jb = jt[:, None, :]
            mask = (it < jb) | (it > jb + w) | (jb == -1)
            sim = jnp.einsum('bhwie,bhwje->bhwij', bq, bk2) * QK_SCALE
            sim = jnp.where(mask, -jnp.finfo(sim.dtype).max, sim)
            attn = jax.nn.softmax(sim, -1)
            out = jnp.einsum('bhwij,bhwje->bhwie', attn, bv2)
            return out.reshape(b, h, n, d)

        def attn_layer(x, Wqkv, qs, ksc, Wo):
            b, n, _ = x.shape
            qkv = x @ Wqkv
            q, k, v = jnp.split(qkv, 3, -1)
            sh = lambda t: t.reshape(b, n, HEADS, DIM_HEAD).transpose(0, 2, 1, 3)
            q, k, v = (sh(q), sh(k), sh(v))
            q = l2norm(q) * qs
            k = l2norm(k) * ksc
            freqs, scale = rotary_tables(n)
            cos, sin = (jnp.cos(freqs), jnp.sin(freqs))
            q = q * cos * scale + rotate_half(q) * sin * scale
            inv = 1.0 / scale
            k = k * cos * inv + rotate_half(k) * sin * inv
            out = local_attention(q, k, v)
            out = out.transpose(0, 2, 1, 3).reshape(b, n, INNER)
            return out @ Wo

        def ffn_layer(x, g, bln, W1, b1, W2, b2):
            mu = x.mean(-1, keepdims=True)
            var = ((x - mu) ** 2).mean(-1, keepdims=True)
            xn = (x - mu) / jnp.sqrt(var + 1e-05) * g + bln
            hg = xn @ W1 + b1
            a, gate = jnp.split(hg, 2, -1)
            return a * jax.nn.gelu(gate, approximate=False) @ W2 + b2
        key = jax.random.key(seed)
        ks = jax.random.split(key, 8)
        B, N = (2, 256)
        init = lambda k, shape: jax.random.normal(k, shape, jnp.float32) * 0.02
        return {'x': jax.random.normal(ks[0], (B, N, DIM), jnp.float32), 'Wqkv': init(ks[1], (DEPTH, DIM, 3 * INNER)), 'q_scale': jnp.ones((DEPTH, DIM_HEAD), jnp.float32), 'k_scale': jnp.ones((DEPTH, DIM_HEAD), jnp.float32), 'Wo': init(ks[2], (DEPTH, INNER, DIM)), 'ln_g': jnp.ones((DEPTH, DIM), jnp.float32), 'ln_b': jnp.zeros((DEPTH, DIM), jnp.float32), 'W1': init(ks[3], (DEPTH, DIM, 2 * DIM_INNER)), 'b1': jnp.zeros((DEPTH, 2 * DIM_INNER), jnp.float32), 'W2': init(ks[4], (DEPTH, DIM_INNER, DIM)), 'b2': jnp.zeros((DEPTH, DIM), jnp.float32)}
    _L0_ffn_all = _L0_ffn_setup()
    _L0_ffn_in = {k: v for k, v in _L0_ffn_all.items() if k in ('Wqkv', 'q_scale', 'k_scale', 'Wo', 'ln_g', 'ln_b', 'W1', 'b1', 'W2', 'b2')}
    del _L0_ffn_all

    def _L1_attn_setup():
        import jax, jax.numpy as jnp
        import numpy as np
        B, L, D, N = (4, 256, 128, 16)

        def _layernorm(x, g, b, eps=1e-05):
            mu = jnp.mean(x, axis=-1, keepdims=True)
            var = jnp.mean(jnp.square(x - mu), axis=-1, keepdims=True)
            return (x - mu) * jax.lax.rsqrt(var + eps) * g + b

        def _silu(x):
            return x * jax.nn.sigmoid(x)

        def _depthwise_conv(x, w):
            xc = x.transpose(0, 2, 1)
            y = jax.lax.conv_general_dilated(xc, w, window_strides=(1,), padding=[(1, 1)], feature_group_count=xc.shape[1], dimension_numbers=('NCH', 'OIH', 'NCH'))
            return y.transpose(0, 2, 1)

        def _selective_scan(u, A_log, D_skip, W_dt, b_dt, W_B, W_C):
            A = -jnp.exp(A_log)
            dt = jax.nn.softplus(u @ W_dt + b_dt)
            Bt = u @ W_B
            Ct = u @ W_C

            def step(h, inp):
                dt_t, B_t, C_t, u_t = inp
                dA = jnp.exp(dt_t[..., None] * A)
                h = dA * h + (dt_t * u_t)[..., None] * B_t[:, None, :]
                y = jnp.einsum('bdn,bn->bd', h, C_t)
                return (h, y)
            h0 = jnp.zeros((u.shape[0], u.shape[2], A.shape[1]), u.dtype)
            xs = (dt.transpose(1, 0, 2), Bt.transpose(1, 0, 2), Ct.transpose(1, 0, 2), u.transpose(1, 0, 2))
            _, ys = jax.lax.scan(step, h0, xs)
            return ys.transpose(1, 0, 2) + u * D_skip
        key = jax.random.key(seed)
        ks = jax.random.split(key, 12)
        s = 1.0 / np.sqrt(D)
        inp = {'x': jax.random.normal(ks[0], (B, L, D), jnp.float32), 'ln_g': jnp.ones((D,), jnp.float32), 'ln_b': jnp.zeros((D,), jnp.float32), 'w1_w': jax.random.normal(ks[1], (D, D), jnp.float32) * s, 'w1_b': jnp.zeros((D,), jnp.float32), 'v1_w': jax.random.normal(ks[2], (D, D), jnp.float32) * s, 'v1_b': jnp.zeros((D,), jnp.float32), 'w2_w': jax.random.normal(ks[3], (D, D), jnp.float32) * s, 'w2_b': jnp.zeros((D,), jnp.float32), 'conv_w': jax.random.normal(ks[4], (D, 1, 3), jnp.float32) * (1.0 / np.sqrt(3.0)), 'A_log': jnp.log(jnp.broadcast_to(jnp.arange(1, N + 1, dtype=jnp.float32), (D, N))), 'D_skip': jnp.ones((D,), jnp.float32), 'W_dt': jax.random.normal(ks[5], (D, D), jnp.float32) * (s * 0.1), 'b_dt': jnp.full((D,), -4.0, jnp.float32), 'W_B': jax.random.normal(ks[6], (D, N), jnp.float32) * s, 'W_C': jax.random.normal(ks[7], (D, N), jnp.float32) * s}
        return inp
    _L1_attn_all = _L1_attn_setup()
    _L1_attn_in = {k: v for k, v in _L1_attn_all.items() if k in ('ln_g', 'ln_b', 'w1_w', 'w1_b', 'v1_w', 'v1_b', 'w2_w', 'w2_b', 'conv_w', 'A_log', 'D_skip', 'W_dt', 'b_dt', 'W_B', 'W_C')}
    del _L1_attn_all

    def _L1_xattn_setup():
        import jax, jax.numpy as jnp
        import numpy as np
        EMBED_DIM = 128
        HIDDEN_DIM = 128
        NUM_HEADS = 16
        CONTEXT_DIM = 96
        HEAD_DIM = EMBED_DIM // NUM_HEADS
        SCALE = HEAD_DIM ** (-0.5)

        def _split_heads(x):
            b, n, _ = x.shape
            return x.reshape(b, n, NUM_HEADS, -1).transpose(0, 2, 1, 3)
        key = jax.random.key(seed)
        ks = jax.random.split(key, 7)
        B, N, M = (4, 512, 128)
        tokens = jax.random.normal(ks[0], (B, N, HIDDEN_DIM), dtype=jnp.float32)
        context = jax.random.normal(ks[1], (B, M, CONTEXT_DIM), dtype=jnp.float32)
        Wq = jax.random.normal(ks[2], (HIDDEN_DIM, EMBED_DIM), dtype=jnp.float32) * HIDDEN_DIM ** (-0.5)
        Wk = jax.random.normal(ks[3], (CONTEXT_DIM, EMBED_DIM), dtype=jnp.float32) * CONTEXT_DIM ** (-0.5)
        Wv = jax.random.normal(ks[4], (CONTEXT_DIM, HIDDEN_DIM), dtype=jnp.float32) * CONTEXT_DIM ** (-0.5)
        Wo = jax.random.normal(ks[5], (HIDDEN_DIM, HIDDEN_DIM), dtype=jnp.float32) * HIDDEN_DIM ** (-0.5)
        bo = jax.random.normal(ks[6], (HIDDEN_DIM,), dtype=jnp.float32) * 0.01
        return {'tokens': tokens, 'context': context, 'Wq': Wq, 'Wk': Wk, 'Wv': Wv, 'Wo': Wo, 'bo': bo}
    _L1_xattn_all = _L1_xattn_setup()
    _L1_xattn_in = {k: v for k, v in _L1_xattn_all.items() if k in ('Wq', 'Wk', 'Wv', 'Wo', 'bo')}
    del _L1_xattn_all

    def _L1_ffn_setup():
        import jax, jax.numpy as jnp
        import numpy as np
        H = 8
        QD = 32
        HALF = QD // 2
        DIMS = (32, 32)
        TOPK = 16
        DTK = 4
        EPS_BN = 1e-05
        EPS_NORM = 1e-12

        def _l2norm(x):
            n = jnp.linalg.norm(x, axis=-1, keepdims=True)
            return x / jnp.maximum(n, EPS_NORM)
        key = jax.random.key(seed)
        ks = jax.random.split(key, 6)
        B, S, D, O, E = (2, 64, 128, 128, 128)
        hidden_states = jax.random.normal(ks[0], (B, S, D), jnp.float32)
        Wq = jax.random.normal(ks[1], (D, H * QD), jnp.float32) * 0.02
        bq = jnp.zeros((H * QD,), jnp.float32)
        bn_gamma = jnp.ones((QD,), jnp.float32)
        bn_beta = jnp.zeros((QD,), jnp.float32)
        sub_key0 = jax.random.normal(ks[2], (DIMS[0], HALF), jnp.float32) * 0.02
        sub_key1 = jax.random.normal(ks[3], (DIMS[1], HALF), jnp.float32) * 0.02
        expert_down = jax.random.normal(ks[4], (E, D), jnp.float32) * 0.02
        expert_up = jax.random.normal(ks[5], (E, O), jnp.float32) * 0.02
        return {'hidden_states': hidden_states, 'Wq': Wq, 'bq': bq, 'bn_gamma': bn_gamma, 'bn_beta': bn_beta, 'sub_key0': sub_key0, 'sub_key1': sub_key1, 'expert_down': expert_down, 'expert_up': expert_up}
    _L1_ffn_all = _L1_ffn_setup()
    _L1_ffn_in = {k: v for k, v in _L1_ffn_all.items() if k in ('Wq', 'bq', 'bn_gamma', 'bn_beta', 'sub_key0', 'sub_key1', 'expert_down', 'expert_up')}
    del _L1_ffn_all

    def _L2_attn_setup():
        import jax, jax.numpy as jnp
        import numpy as np
        D_MODEL = 128
        D_STATE = 64
        D_CONV = 4
        EXPAND = 2
        DT_RANK = D_MODEL // 16
        D_INNER = EXPAND * D_MODEL
        BATCH, T = (2, 256)
        D_PROJ = 2 * D_INNER + 2 * D_STATE + DT_RANK

        def _reference_tuple_inner(x, in_proj_w, conv_w, conv_b, A_log, D_param, dt_proj_w, dt_proj_b, out_proj_w):
            Bsz = x.shape[0]
            proj = jnp.einsum('btd,pd->btp', x, in_proj_w)
            x_inner = proj[..., :D_INNER]
            z = proj[..., D_INNER:2 * D_INNER]
            B_param = proj[..., 2 * D_INNER:2 * D_INNER + D_STATE]
            C_param = proj[..., 2 * D_INNER + D_STATE:2 * D_INNER + 2 * D_STATE]
            delta_raw = proj[..., -DT_RANK:]
            xc = jax.lax.conv_general_dilated(x_inner.transpose(0, 2, 1), conv_w, (1,), [(D_CONV - 1, 0)], feature_group_count=D_INNER, dimension_numbers=('NCH', 'OIH', 'NCH'))
            xc = jax.nn.silu((xc + conv_b[None, :, None]).transpose(0, 2, 1))
            delta = jax.nn.softplus(jnp.einsum('btr,ir->bti', delta_raw, dt_proj_w) + dt_proj_b)
            A = -jnp.exp(A_log)
            h0 = jnp.zeros((Bsz, D_INNER, D_STATE), x.dtype)

            def step(h, inp):
                d_t, b_t, c_t, xc_t = inp
                dA = jnp.exp(A[None, None, :] * d_t[..., None])
                h = dA * h + d_t[..., None] * b_t[:, None, :] * xc_t[..., None]
                y = jnp.einsum('bis,bs->bi', h, c_t)
                return (h, y)
            hT, ys = jax.lax.scan(step, h0, (delta.transpose(1, 0, 2), B_param.transpose(1, 0, 2), C_param.transpose(1, 0, 2), xc.transpose(1, 0, 2)))
            y = ys.transpose(1, 0, 2) + D_param * xc
            out = jnp.einsum('bti,di->btd', y * jax.nn.silu(z), out_proj_w)
            return (out, hT)
        key = jax.random.key(seed)
        ks = jax.random.split(key, 7)
        g = lambda k, shape, s=1.0: jax.random.normal(k, shape, jnp.float32) * s
        return {'x': g(ks[0], (BATCH, T, D_MODEL)), 'in_proj_w': g(ks[1], (D_PROJ, D_MODEL), 0.02), 'conv_w': g(ks[2], (D_INNER, 1, D_CONV), 0.1), 'conv_b': jnp.zeros((D_INNER,), jnp.float32), 'A_log': g(ks[3], (D_STATE,)), 'D_param': jnp.ones((D_INNER,), jnp.float32), 'dt_proj_w': g(ks[4], (D_INNER, DT_RANK), 0.05), 'dt_proj_b': jnp.zeros((D_INNER,), jnp.float32), 'out_proj_w': g(ks[5], (D_MODEL, D_INNER), 0.02)}
    _L2_attn_all = _L2_attn_setup()
    _L2_attn_in = {k: v for k, v in _L2_attn_all.items() if k in ('in_proj_w', 'conv_w', 'conv_b', 'A_log', 'D_param', 'dt_proj_w', 'dt_proj_b', 'out_proj_w')}
    del _L2_attn_all

    def _L2_xattn_setup():
        import jax, jax.numpy as jnp
        import numpy as np
        HEADS = 16
        DIM_HEAD = 64
        SCALE = DIM_HEAD ** (-0.5)
        QUERY_DIM = 128
        CONTEXT_DIM = 96
        INNER_DIM = HEADS * DIM_HEAD
        key = jax.random.key(seed)
        ks = jax.random.split(key, 7)
        B, Nq, Nk = (8, 512, 77)
        x = jax.random.normal(ks[0], (B, Nq, QUERY_DIM), dtype=jnp.float32)
        context = jax.random.normal(ks[1], (B, Nk, CONTEXT_DIM), dtype=jnp.float32)
        Wq = jax.random.normal(ks[2], (QUERY_DIM, INNER_DIM), dtype=jnp.float32) * QUERY_DIM ** (-0.5)
        Wk = jax.random.normal(ks[3], (CONTEXT_DIM, INNER_DIM), dtype=jnp.float32) * CONTEXT_DIM ** (-0.5)
        Wv = jax.random.normal(ks[4], (CONTEXT_DIM, INNER_DIM), dtype=jnp.float32) * CONTEXT_DIM ** (-0.5)
        Wo = jax.random.normal(ks[5], (INNER_DIM, QUERY_DIM), dtype=jnp.float32) * INNER_DIM ** (-0.5)
        bo = jnp.zeros((QUERY_DIM,), dtype=jnp.float32)
        return {'x': x, 'context': context, 'Wq': Wq, 'Wk': Wk, 'Wv': Wv, 'Wo': Wo, 'bo': bo}
    _L2_xattn_all = _L2_xattn_setup()
    _L2_xattn_in = {k: v for k, v in _L2_xattn_all.items() if k in ('Wq', 'Wk', 'Wv', 'Wo', 'bo')}
    del _L2_xattn_all

    def _L2_ffn_setup():
        import jax, jax.numpy as jnp
        import numpy as np
        D = 128
        H = 128
        E = 8
        K = 2
        I = 2 * 128
        ROUTE_SCALE = 1.0
        key = jax.random.key(seed)
        ks = jax.random.split(key, 12)
        s = lambda *sh: 1.0 / np.sqrt(sh[-1])
        return {'x': jax.random.normal(ks[0], (1, 256, D), jnp.float32), 'gate_w': jax.random.normal(ks[1], (E, D), jnp.float32) * s(E, D), 'w1': jax.random.normal(ks[2], (E, H, D), jnp.float32) * s(H, D), 'b1': jax.random.normal(ks[3], (E, H), jnp.float32) * 0.01, 'w2': jax.random.normal(ks[4], (E, D, H), jnp.float32) * s(D, H), 'b2': jax.random.normal(ks[5], (E, D), jnp.float32) * 0.01, 'w3': jax.random.normal(ks[6], (E, H, D), jnp.float32) * s(H, D), 'b3': jax.random.normal(ks[7], (E, H), jnp.float32) * 0.01, 'sw1': jax.random.normal(ks[8], (I, D), jnp.float32) * s(I, D), 'sw2': jax.random.normal(ks[9], (I, D), jnp.float32) * s(I, D), 'sw3': jax.random.normal(ks[10], (D, I), jnp.float32) * s(D, I)}
    _L2_ffn_all = _L2_ffn_setup()
    _L2_ffn_in = {k: v for k, v in _L2_ffn_all.items() if k in ('gate_w', 'w1', 'b1', 'w2', 'b2', 'w3', 'b3', 'sw1', 'sw2', 'sw3')}
    del _L2_ffn_all

    def _L3_attn_setup():
        import jax, jax.numpy as jnp
        import numpy as np
        B, S, H, NH, P = (1, 256, 128, 16, 2)
        D = H // NH
        SCALE = 1.0 / np.sqrt(D).astype(np.float32)

        def _lin(x, W, b):
            return x @ W + b

        def _split_heads(x):
            return x.reshape(*x.shape[:-2], x.shape[-2], NH, D).swapaxes(-3, -2)

        def _merge_heads(x):
            return x.swapaxes(-3, -2).reshape(*x.shape[:-3], x.shape[-2], H)
        key = jax.random.key(seed)
        ks = jax.random.split(key, 20)
        w = lambda k, i, o: jax.random.normal(k, (i, o), jnp.float32) * 0.02
        inp = {'hidden_states': jax.random.normal(ks[0], (B, S, H), jnp.float32), 'past_states': jax.random.normal(ks[1], (P, B, S, H), jnp.float32), 'Wq': w(ks[2], H, H), 'bq': jnp.zeros((H,), jnp.float32), 'Wk': w(ks[3], H, H), 'bk': jnp.zeros((H,), jnp.float32), 'Wv': w(ks[4], H, H), 'bv': jnp.zeros((H,), jnp.float32), 'Wo': w(ks[5], H, H), 'bo': jnp.zeros((H,), jnp.float32), 'Wrq': w(ks[6], H, H), 'brq': jnp.zeros((H,), jnp.float32), 'Wrk': w(ks[7], H, H), 'brk': jnp.zeros((H,), jnp.float32), 'Wrv': w(ks[8], H, H), 'brv': jnp.zeros((H,), jnp.float32), 'Wg': w(ks[9], 2 * H, H), 'bg': jnp.zeros((H,), jnp.float32)}
        return inp
    _L3_attn_all = _L3_attn_setup()
    _L3_attn_in = {k: v for k, v in _L3_attn_all.items() if k in ('past_states', 'Wq', 'bq', 'Wk', 'bk', 'Wv', 'bv', 'Wo', 'bo', 'Wrq', 'brq', 'Wrk', 'brk', 'Wrv', 'brv', 'Wg', 'bg')}
    del _L3_attn_all

    def _L3_xattn_setup():
        import jax, jax.numpy as jnp
        import numpy as np
        B, T, DT, G, DV = (16, 64, 128, 72, 96)
        H, DH = (4, 32)
        INNER = H * DH
        HID = 4 * DT
        N_STATE = 64
        K_TOP = 32

        def layernorm(x, g, b, eps=1e-05):
            m = x.mean(-1, keepdims=True)
            v = x.var(-1, keepdims=True)
            return (x - m) * jax.lax.rsqrt(v + eps) * g + b

        def s4d(x, log_dt, A_re, A_im, C_re, C_im, D_skip):
            Bb, L, D = x.shape
            dt = jnp.exp(log_dt)
            A = A_re + 1j * A_im
            C = C_re + 1j * C_im
            dtA = dt[:, None] * A
            dC = C * (jnp.exp(dtA) - 1.0) / A
            powers = jnp.exp(dtA[:, :, None] * jnp.arange(L))
            K = 2.0 * jnp.einsum('dn,dnl->dl', dC, powers).real
            n = 2 * L
            Kf = jnp.fft.rfft(K, n=n, axis=-1)
            xf = jnp.fft.rfft(x, n=n, axis=1)
            y = jnp.fft.irfft(xf * Kf.T[None], n=n, axis=1)[:, :L]
            return y + x * D_skip
        key = jax.random.key(seed)
        ks = jax.random.split(key, 16)
        s = 0.02
        inp = {'x_text': jax.random.normal(ks[0], (B, T, DT), jnp.float32), 'x_vision': jax.random.normal(ks[1], (B, G, DV), jnp.float32), 'text_mask': jnp.ones((B, T), bool), 'vision_mask': jnp.ones((B, G), bool), 'Wq': jax.random.normal(ks[2], (DT, INNER), jnp.float32) * s, 'Wk': jax.random.normal(ks[3], (DV, INNER), jnp.float32) * s, 'Wv': jax.random.normal(ks[4], (DV, DT), jnp.float32) * s, 'W_film_in': jax.random.normal(ks[5], (DT, 2 * DT), jnp.float32) * s, 'b_film_in': jnp.zeros((2 * DT,), jnp.float32), 'W_film_out': jax.random.normal(ks[6], (DT, 2 * DT), jnp.float32) * s, 'b_film_out': jnp.zeros((2 * DT,), jnp.float32), 'g_norm_in': jnp.ones((DT,), jnp.float32), 'b_norm_in': jnp.zeros((DT,), jnp.float32), 'g_norm_out': jnp.ones((DT,), jnp.float32), 'b_norm_out': jnp.zeros((DT,), jnp.float32), 'g_ffn': jnp.ones((DT,), jnp.float32), 'b_ffn': jnp.zeros((DT,), jnp.float32), 'W1': jax.random.normal(ks[7], (DT, HID), jnp.float32) * s, 'b1': jnp.zeros((HID,), jnp.float32), 'W2': jax.random.normal(ks[8], (HID, DT), jnp.float32) * s, 'b2': jnp.zeros((DT,), jnp.float32), 'log_dt': jnp.log(0.001) + jax.random.uniform(ks[9], (DT,), jnp.float32) * (jnp.log(0.1) - jnp.log(0.001)), 'A_re': -0.5 * jnp.ones((DT, N_STATE), jnp.float32), 'A_im': jnp.tile(jnp.pi * jnp.arange(N_STATE, dtype=jnp.float32), (DT, 1)), 'C_re': jax.random.normal(ks[10], (DT, N_STATE), jnp.float32) * 0.5 ** 0.5, 'C_im': jax.random.normal(ks[11], (DT, N_STATE), jnp.float32) * 0.5 ** 0.5, 'D_skip': jax.random.normal(ks[12], (DT,), jnp.float32), 'mod_gate': jnp.array(0.5, jnp.float32)}
        return inp
    _L3_xattn_all = _L3_xattn_setup()
    _L3_xattn_in = {k: v for k, v in _L3_xattn_all.items() if k in ('Wq', 'Wk', 'Wv', 'W_film_in', 'b_film_in', 'W_film_out', 'b_film_out', 'g_norm_in', 'b_norm_in', 'g_norm_out', 'b_norm_out', 'g_ffn', 'b_ffn', 'W1', 'b1', 'W2', 'b2', 'log_dt', 'A_re', 'A_im', 'C_re', 'C_im', 'D_skip', 'mod_gate')}
    del _L3_xattn_all

    def _L3_ffn_setup():
        import jax, jax.numpy as jnp
        import numpy as np
        B, S, D = (2, 64, 128)
        E, K, I = (16, 8, 128)
        I_SH = 128
        ROUTE_SCALE = 2.826
        key = jax.random.key(seed)
        ks = jax.random.split(key, 8)
        s = 0.02
        return {'x': jax.random.normal(ks[0], (B, S, D), dtype=jnp.float32), 'gate_w': jax.random.normal(ks[1], (E, D), dtype=jnp.float32) * s, 'expert_bias': jnp.zeros((E,), dtype=jnp.float32), 'w_gate': jax.random.normal(ks[2], (E, I, D), dtype=jnp.float32) * s, 'w_up': jax.random.normal(ks[3], (E, I, D), dtype=jnp.float32) * s, 'w_down': jax.random.normal(ks[4], (E, D, I), dtype=jnp.float32) * s, 'shared_gate_w': jax.random.normal(ks[5], (I_SH, D), dtype=jnp.float32) * s, 'shared_up_w': jax.random.normal(ks[6], (I_SH, D), dtype=jnp.float32) * s, 'shared_down_w': jax.random.normal(ks[7], (D, I_SH), dtype=jnp.float32) * s}
    _L3_ffn_all = _L3_ffn_setup()
    _L3_ffn_in = {k: v for k, v in _L3_ffn_all.items() if k in ('gate_w', 'expert_bias', 'w_gate', 'w_up', 'w_down', 'shared_gate_w', 'shared_up_w', 'shared_down_w')}
    del _L3_ffn_all
    return {'x': x, 'ctx_768': ctx_768, 'mask_BxS2_bk0': mask_BxS2_bk0, 'mask_BxS_bf1': mask_BxS_bf1, 'mask_BxS2_bf1': mask_BxS2_bf1, 'L0_attn_W_qkv': _L0_attn_in['W_qkv'], 'L0_attn_W_out': _L0_attn_in['W_out'], 'L0_xattn_ln_x_g': _L0_xattn_in['ln_x_g'], 'L0_xattn_ln_x_b': _L0_xattn_in['ln_x_b'], 'L0_xattn_ln_l_g': _L0_xattn_in['ln_l_g'], 'L0_xattn_ln_l_b': _L0_xattn_in['ln_l_b'], 'L0_xattn_qn_g': _L0_xattn_in['qn_g'], 'L0_xattn_kn_g': _L0_xattn_in['kn_g'], 'L0_xattn_Wq': _L0_xattn_in['Wq'], 'L0_xattn_Wkv': _L0_xattn_in['Wkv'], 'L0_xattn_Wlkv': _L0_xattn_in['Wlkv'], 'L0_xattn_Wo': _L0_xattn_in['Wo'], 'L0_xattn_bo': _L0_xattn_in['bo'], 'L0_ffn_Wqkv': _L0_ffn_in['Wqkv'], 'L0_ffn_q_scale': _L0_ffn_in['q_scale'], 'L0_ffn_k_scale': _L0_ffn_in['k_scale'], 'L0_ffn_Wo': _L0_ffn_in['Wo'], 'L0_ffn_ln_g': _L0_ffn_in['ln_g'], 'L0_ffn_ln_b': _L0_ffn_in['ln_b'], 'L0_ffn_W1': _L0_ffn_in['W1'], 'L0_ffn_b1': _L0_ffn_in['b1'], 'L0_ffn_W2': _L0_ffn_in['W2'], 'L0_ffn_b2': _L0_ffn_in['b2'], 'L1_attn_ln_g': _L1_attn_in['ln_g'], 'L1_attn_ln_b': _L1_attn_in['ln_b'], 'L1_attn_w1_w': _L1_attn_in['w1_w'], 'L1_attn_w1_b': _L1_attn_in['w1_b'], 'L1_attn_v1_w': _L1_attn_in['v1_w'], 'L1_attn_v1_b': _L1_attn_in['v1_b'], 'L1_attn_w2_w': _L1_attn_in['w2_w'], 'L1_attn_w2_b': _L1_attn_in['w2_b'], 'L1_attn_conv_w': _L1_attn_in['conv_w'], 'L1_attn_A_log': _L1_attn_in['A_log'], 'L1_attn_D_skip': _L1_attn_in['D_skip'], 'L1_attn_W_dt': _L1_attn_in['W_dt'], 'L1_attn_b_dt': _L1_attn_in['b_dt'], 'L1_attn_W_B': _L1_attn_in['W_B'], 'L1_attn_W_C': _L1_attn_in['W_C'], 'L1_xattn_Wq': _L1_xattn_in['Wq'], 'L1_xattn_Wk': _L1_xattn_in['Wk'], 'L1_xattn_Wv': _L1_xattn_in['Wv'], 'L1_xattn_Wo': _L1_xattn_in['Wo'], 'L1_xattn_bo': _L1_xattn_in['bo'], 'L1_ffn_Wq': _L1_ffn_in['Wq'], 'L1_ffn_bq': _L1_ffn_in['bq'], 'L1_ffn_bn_gamma': _L1_ffn_in['bn_gamma'], 'L1_ffn_bn_beta': _L1_ffn_in['bn_beta'], 'L1_ffn_sub_key0': _L1_ffn_in['sub_key0'], 'L1_ffn_sub_key1': _L1_ffn_in['sub_key1'], 'L1_ffn_expert_down': _L1_ffn_in['expert_down'], 'L1_ffn_expert_up': _L1_ffn_in['expert_up'], 'L2_attn_in_proj_w': _L2_attn_in['in_proj_w'], 'L2_attn_conv_w': _L2_attn_in['conv_w'], 'L2_attn_conv_b': _L2_attn_in['conv_b'], 'L2_attn_A_log': _L2_attn_in['A_log'], 'L2_attn_D_param': _L2_attn_in['D_param'], 'L2_attn_dt_proj_w': _L2_attn_in['dt_proj_w'], 'L2_attn_dt_proj_b': _L2_attn_in['dt_proj_b'], 'L2_attn_out_proj_w': _L2_attn_in['out_proj_w'], 'L2_xattn_Wq': _L2_xattn_in['Wq'], 'L2_xattn_Wk': _L2_xattn_in['Wk'], 'L2_xattn_Wv': _L2_xattn_in['Wv'], 'L2_xattn_Wo': _L2_xattn_in['Wo'], 'L2_xattn_bo': _L2_xattn_in['bo'], 'L2_ffn_gate_w': _L2_ffn_in['gate_w'], 'L2_ffn_w1': _L2_ffn_in['w1'], 'L2_ffn_b1': _L2_ffn_in['b1'], 'L2_ffn_w2': _L2_ffn_in['w2'], 'L2_ffn_b2': _L2_ffn_in['b2'], 'L2_ffn_w3': _L2_ffn_in['w3'], 'L2_ffn_b3': _L2_ffn_in['b3'], 'L2_ffn_sw1': _L2_ffn_in['sw1'], 'L2_ffn_sw2': _L2_ffn_in['sw2'], 'L2_ffn_sw3': _L2_ffn_in['sw3'], 'L3_attn_past_states': _L3_attn_in['past_states'], 'L3_attn_Wq': _L3_attn_in['Wq'], 'L3_attn_bq': _L3_attn_in['bq'], 'L3_attn_Wk': _L3_attn_in['Wk'], 'L3_attn_bk': _L3_attn_in['bk'], 'L3_attn_Wv': _L3_attn_in['Wv'], 'L3_attn_bv': _L3_attn_in['bv'], 'L3_attn_Wo': _L3_attn_in['Wo'], 'L3_attn_bo': _L3_attn_in['bo'], 'L3_attn_Wrq': _L3_attn_in['Wrq'], 'L3_attn_brq': _L3_attn_in['brq'], 'L3_attn_Wrk': _L3_attn_in['Wrk'], 'L3_attn_brk': _L3_attn_in['brk'], 'L3_attn_Wrv': _L3_attn_in['Wrv'], 'L3_attn_brv': _L3_attn_in['brv'], 'L3_attn_Wg': _L3_attn_in['Wg'], 'L3_attn_bg': _L3_attn_in['bg'], 'L3_xattn_Wq': _L3_xattn_in['Wq'], 'L3_xattn_Wk': _L3_xattn_in['Wk'], 'L3_xattn_Wv': _L3_xattn_in['Wv'], 'L3_xattn_W_film_in': _L3_xattn_in['W_film_in'], 'L3_xattn_b_film_in': _L3_xattn_in['b_film_in'], 'L3_xattn_W_film_out': _L3_xattn_in['W_film_out'], 'L3_xattn_b_film_out': _L3_xattn_in['b_film_out'], 'L3_xattn_g_norm_in': _L3_xattn_in['g_norm_in'], 'L3_xattn_b_norm_in': _L3_xattn_in['b_norm_in'], 'L3_xattn_g_norm_out': _L3_xattn_in['g_norm_out'], 'L3_xattn_b_norm_out': _L3_xattn_in['b_norm_out'], 'L3_xattn_g_ffn': _L3_xattn_in['g_ffn'], 'L3_xattn_b_ffn': _L3_xattn_in['b_ffn'], 'L3_xattn_W1': _L3_xattn_in['W1'], 'L3_xattn_b1': _L3_xattn_in['b1'], 'L3_xattn_W2': _L3_xattn_in['W2'], 'L3_xattn_b2': _L3_xattn_in['b2'], 'L3_xattn_log_dt': _L3_xattn_in['log_dt'], 'L3_xattn_A_re': _L3_xattn_in['A_re'], 'L3_xattn_A_im': _L3_xattn_in['A_im'], 'L3_xattn_C_re': _L3_xattn_in['C_re'], 'L3_xattn_C_im': _L3_xattn_in['C_im'], 'L3_xattn_D_skip': _L3_xattn_in['D_skip'], 'L3_xattn_mod_gate': _L3_xattn_in['mod_gate'], 'L3_ffn_gate_w': _L3_ffn_in['gate_w'], 'L3_ffn_expert_bias': _L3_ffn_in['expert_bias'], 'L3_ffn_w_gate': _L3_ffn_in['w_gate'], 'L3_ffn_w_up': _L3_ffn_in['w_up'], 'L3_ffn_w_down': _L3_ffn_in['w_down'], 'L3_ffn_shared_gate_w': _L3_ffn_in['shared_gate_w'], 'L3_ffn_shared_up_w': _L3_ffn_in['shared_up_w'], 'L3_ffn_shared_down_w': _L3_ffn_in['shared_down_w']}

def reference(x, ctx_768, mask_BxS2_bk0, mask_BxS_bf1, mask_BxS2_bf1, L0_attn_W_qkv, L0_attn_W_out, L0_xattn_ln_x_g, L0_xattn_ln_x_b, L0_xattn_ln_l_g, L0_xattn_ln_l_b, L0_xattn_qn_g, L0_xattn_kn_g, L0_xattn_Wq, L0_xattn_Wkv, L0_xattn_Wlkv, L0_xattn_Wo, L0_xattn_bo, L0_ffn_Wqkv, L0_ffn_q_scale, L0_ffn_k_scale, L0_ffn_Wo, L0_ffn_ln_g, L0_ffn_ln_b, L0_ffn_W1, L0_ffn_b1, L0_ffn_W2, L0_ffn_b2, L1_attn_ln_g, L1_attn_ln_b, L1_attn_w1_w, L1_attn_w1_b, L1_attn_v1_w, L1_attn_v1_b, L1_attn_w2_w, L1_attn_w2_b, L1_attn_conv_w, L1_attn_A_log, L1_attn_D_skip, L1_attn_W_dt, L1_attn_b_dt, L1_attn_W_B, L1_attn_W_C, L1_xattn_Wq, L1_xattn_Wk, L1_xattn_Wv, L1_xattn_Wo, L1_xattn_bo, L1_ffn_Wq, L1_ffn_bq, L1_ffn_bn_gamma, L1_ffn_bn_beta, L1_ffn_sub_key0, L1_ffn_sub_key1, L1_ffn_expert_down, L1_ffn_expert_up, L2_attn_in_proj_w, L2_attn_conv_w, L2_attn_conv_b, L2_attn_A_log, L2_attn_D_param, L2_attn_dt_proj_w, L2_attn_dt_proj_b, L2_attn_out_proj_w, L2_xattn_Wq, L2_xattn_Wk, L2_xattn_Wv, L2_xattn_Wo, L2_xattn_bo, L2_ffn_gate_w, L2_ffn_w1, L2_ffn_b1, L2_ffn_w2, L2_ffn_b2, L2_ffn_w3, L2_ffn_b3, L2_ffn_sw1, L2_ffn_sw2, L2_ffn_sw3, L3_attn_past_states, L3_attn_Wq, L3_attn_bq, L3_attn_Wk, L3_attn_bk, L3_attn_Wv, L3_attn_bv, L3_attn_Wo, L3_attn_bo, L3_attn_Wrq, L3_attn_brq, L3_attn_Wrk, L3_attn_brk, L3_attn_Wrv, L3_attn_brv, L3_attn_Wg, L3_attn_bg, L3_xattn_Wq, L3_xattn_Wk, L3_xattn_Wv, L3_xattn_W_film_in, L3_xattn_b_film_in, L3_xattn_W_film_out, L3_xattn_b_film_out, L3_xattn_g_norm_in, L3_xattn_b_norm_in, L3_xattn_g_norm_out, L3_xattn_b_norm_out, L3_xattn_g_ffn, L3_xattn_b_ffn, L3_xattn_W1, L3_xattn_b1, L3_xattn_W2, L3_xattn_b2, L3_xattn_log_dt, L3_xattn_A_re, L3_xattn_A_im, L3_xattn_C_re, L3_xattn_C_im, L3_xattn_D_skip, L3_xattn_mod_gate, L3_ffn_gate_w, L3_ffn_expert_bias, L3_ffn_w_gate, L3_ffn_w_up, L3_ffn_w_down, L3_ffn_shared_gate_w, L3_ffn_shared_up_w, L3_ffn_shared_down_w):
    import jax
    import jax.numpy as jnp

    def _L0_attn_ref(x, W_qkv, W_out):
        import jax, jax.numpy as jnp
        import numpy as np
        DIM = 128
        H = 16
        D = DIM // H
        CS = 64
        SCALE = D ** (-0.5)
        B, N, C = x.shape
        qkv = (x @ W_qkv).reshape(B, N, 3, H, D)
        qkv = jnp.transpose(qkv, (2, 0, 3, 1, 4))
        q, k, v = (qkv[0], qkv[1], qkv[2])
        nc = N // CS
        q = q.reshape(B, H, nc, CS, D)
        k = k.reshape(B, H, nc, CS, D)
        v = v.reshape(B, H, nc, CS, D)
        attn = jnp.einsum('bhcqd,bhckd->bhcqk', q, k) * SCALE
        mask = jnp.triu(jnp.ones((CS, CS), dtype=bool), k=1)
        attn = jnp.where(mask, jnp.float32(-65000.0), attn)
        attn = jax.nn.softmax(attn, axis=-1)
        out_local = jnp.einsum('bhcqk,bhckd->bhcqd', attn, v)
        chunk_k = k.mean(axis=3)
        chunk_v = v.mean(axis=3)
        cum_k = jnp.cumsum(chunk_k, axis=2)
        cum_v = jnp.cumsum(chunk_v, axis=2)
        zeros = jnp.zeros((B, H, 1, D), dtype=x.dtype)
        cum_k = jnp.concatenate([zeros, cum_k[:, :, :-1]], axis=2)
        cum_v = jnp.concatenate([zeros, cum_v[:, :, :-1]], axis=2)
        cross = jax.nn.sigmoid(jnp.einsum('bhcsd,bhcd->bhcs', q, cum_k) * SCALE)
        out = out_local + cross[..., None] * cum_v[:, :, :, None, :] * 0.5
        out = out.reshape(B, H, N, D)
        out = jnp.transpose(out, (0, 2, 1, 3)).reshape(B, N, C)
        return out @ W_out

    def _L0_xattn_ref(x, latents, mask, ln_x_g, ln_x_b, ln_l_g, ln_l_b, qn_g, kn_g, Wq, Wkv, Wlkv, Wo, bo):
        import jax, jax.numpy as jnp
        import numpy as np
        DIM_IN, DIM_LAT, DIM_HEAD = (96, 128, 64)
        INNER = max(DIM_LAT, DIM_IN)
        HEADS = INNER // DIM_HEAD
        SCALE = DIM_HEAD ** (-0.5)
        RMS_EPS = 1e-08
        LN_EPS = 1e-05

        def layernorm(x, g, b):
            mu = jnp.mean(x, axis=-1, keepdims=True)
            var = jnp.mean((x - mu) ** 2, axis=-1, keepdims=True)
            return (x - mu) * jax.lax.rsqrt(var + LN_EPS) * g + b

        def rmsnorm(x, gamma):
            norm = jnp.sqrt(jnp.sum(x * x, axis=-1, keepdims=True)) * x.shape[-1] ** (-0.5)
            return x / jnp.maximum(norm, RMS_EPS) * gamma
        b, n, _ = x.shape
        m = latents.shape[1]
        xn = layernorm(x, ln_x_g, ln_x_b)
        ln = layernorm(latents, ln_l_g, ln_l_b)
        q = ln @ Wq.T
        kv = jnp.concatenate([xn @ Wkv.T, ln @ Wlkv.T], axis=1)
        k, v = (kv[..., :INNER], kv[..., INNER:])
        split_heads = lambda t: t.reshape(t.shape[0], t.shape[1], HEADS, DIM_HEAD).transpose(0, 2, 1, 3)
        q, k, v = (split_heads(q), split_heads(k), split_heads(v))
        qn = rmsnorm(q, qn_g) * SCALE
        kn = rmsnorm(k, kn_g)
        attn = jnp.einsum('bhid,bhjd->bhij', qn, kn)
        full_mask = jnp.pad(mask, ((0, 0), (0, m)), constant_values=True)
        attn = jnp.where(full_mask[:, None, None, :], attn, -jnp.finfo(attn.dtype).max)
        attn = jax.nn.softmax(attn, axis=-1)
        out = jnp.einsum('bhij,bhjd->bhid', attn, v)
        out = out.transpose(0, 2, 1, 3).reshape(b, m, INNER)
        return out @ Wo.T + bo

    def _L0_ffn_ref(x, Wqkv, q_scale, k_scale, Wo, ln_g, ln_b, W1, b1, W2, b2):
        import jax, jax.numpy as jnp
        import numpy as np
        DIM = 128
        DEPTH = 6
        HEADS = 16
        DIM_HEAD = 64
        WINDOW = 32
        INNER = HEADS * DIM_HEAD
        DIM_INNER = int(DIM * 4 * 2 / 3)
        QK_SCALE = 8.0

        def shift_tokens(t):
            a, s = jnp.split(t, 2, -1)
            s = jnp.pad(s, ((0, 0), (1, 0), (0, 0)))[:, :-1]
            return jnp.concatenate([a, s], -1)

        def l2norm(t):
            return t / jnp.maximum(jnp.linalg.norm(t, axis=-1, keepdims=True), 1e-12)

        def rotate_half(x):
            x1, x2 = jnp.split(x, 2, -1)
            return jnp.concatenate([-x2, x1], -1)

        def rotary_tables(n):
            half = jnp.arange(0, DIM_HEAD, 2, dtype=jnp.float32)
            inv_freq = 1.0 / 10000.0 ** (half / DIM_HEAD)
            t = jnp.arange(n, dtype=jnp.float32)
            freqs = t[:, None] * inv_freq[None, :]
            freqs = jnp.concatenate([freqs, freqs], -1)
            base_scale = (half + 0.4 * DIM_HEAD) / (1.4 * DIM_HEAD)
            power = (t - n // 2) / (WINDOW // 2)
            scale = base_scale[None, :] ** power[:, None]
            scale = jnp.concatenate([scale, scale], -1)
            return (freqs, scale)

        def local_attention(q, k, v):
            b, h, n, d = q.shape
            w = WINDOW
            nw = n // w
            bq = q.reshape(b, h, nw, w, d)
            bk = k.reshape(b, h, nw, w, d)
            bv = v.reshape(b, h, nw, w, d)

            def look(t):
                p = jnp.pad(t, ((0, 0), (0, 0), (1, 0), (0, 0), (0, 0)))
                return jnp.concatenate([p[:, :, :nw], p[:, :, 1:]], axis=3)
            bk2, bv2 = (look(bk), look(bv))
            seq = jnp.arange(n).reshape(nw, w)
            seq_p = jnp.pad(seq, ((1, 0), (0, 0)), constant_values=-1)
            jt = jnp.concatenate([seq_p[:nw], seq_p[1:]], axis=1)
            it = seq[:, :, None]
            jb = jt[:, None, :]
            mask = (it < jb) | (it > jb + w) | (jb == -1)
            sim = jnp.einsum('bhwie,bhwje->bhwij', bq, bk2) * QK_SCALE
            sim = jnp.where(mask, -jnp.finfo(sim.dtype).max, sim)
            attn = jax.nn.softmax(sim, -1)
            out = jnp.einsum('bhwij,bhwje->bhwie', attn, bv2)
            return out.reshape(b, h, n, d)

        def attn_layer(x, Wqkv, qs, ksc, Wo):
            b, n, _ = x.shape
            qkv = x @ Wqkv
            q, k, v = jnp.split(qkv, 3, -1)
            sh = lambda t: t.reshape(b, n, HEADS, DIM_HEAD).transpose(0, 2, 1, 3)
            q, k, v = (sh(q), sh(k), sh(v))
            q = l2norm(q) * qs
            k = l2norm(k) * ksc
            freqs, scale = rotary_tables(n)
            cos, sin = (jnp.cos(freqs), jnp.sin(freqs))
            q = q * cos * scale + rotate_half(q) * sin * scale
            inv = 1.0 / scale
            k = k * cos * inv + rotate_half(k) * sin * inv
            out = local_attention(q, k, v)
            out = out.transpose(0, 2, 1, 3).reshape(b, n, INNER)
            return out @ Wo

        def ffn_layer(x, g, bln, W1, b1, W2, b2):
            mu = x.mean(-1, keepdims=True)
            var = ((x - mu) ** 2).mean(-1, keepdims=True)
            xn = (x - mu) / jnp.sqrt(var + 1e-05) * g + bln
            hg = xn @ W1 + b1
            a, gate = jnp.split(hg, 2, -1)
            return a * jax.nn.gelu(gate, approximate=False) @ W2 + b2
        for i in range(DEPTH):
            x = attn_layer(shift_tokens(x), Wqkv[i], q_scale[i], k_scale[i], Wo[i]) + x
            x = ffn_layer(shift_tokens(x), ln_g[i], ln_b[i], W1[i], b1[i], W2[i], b2[i]) + x
        return x

    def _L1_attn_ref(x, ln_g, ln_b, w1_w, w1_b, v1_w, v1_b, w2_w, w2_b, conv_w, A_log, D_skip, W_dt, b_dt, W_B, W_C):
        import jax, jax.numpy as jnp
        import numpy as np
        B, L, D, N = (4, 256, 128, 16)

        def _layernorm(x, g, b, eps=1e-05):
            mu = jnp.mean(x, axis=-1, keepdims=True)
            var = jnp.mean(jnp.square(x - mu), axis=-1, keepdims=True)
            return (x - mu) * jax.lax.rsqrt(var + eps) * g + b

        def _silu(x):
            return x * jax.nn.sigmoid(x)

        def _depthwise_conv(x, w):
            xc = x.transpose(0, 2, 1)
            y = jax.lax.conv_general_dilated(xc, w, window_strides=(1,), padding=[(1, 1)], feature_group_count=xc.shape[1], dimension_numbers=('NCH', 'OIH', 'NCH'))
            return y.transpose(0, 2, 1)

        def _selective_scan(u, A_log, D_skip, W_dt, b_dt, W_B, W_C):
            A = -jnp.exp(A_log)
            dt = jax.nn.softplus(u @ W_dt + b_dt)
            Bt = u @ W_B
            Ct = u @ W_C

            def step(h, inp):
                dt_t, B_t, C_t, u_t = inp
                dA = jnp.exp(dt_t[..., None] * A)
                h = dA * h + (dt_t * u_t)[..., None] * B_t[:, None, :]
                y = jnp.einsum('bdn,bn->bd', h, C_t)
                return (h, y)
            h0 = jnp.zeros((u.shape[0], u.shape[2], A.shape[1]), u.dtype)
            xs = (dt.transpose(1, 0, 2), Bt.transpose(1, 0, 2), Ct.transpose(1, 0, 2), u.transpose(1, 0, 2))
            _, ys = jax.lax.scan(step, h0, xs)
            return ys.transpose(1, 0, 2) + u * D_skip
        x_norm = _layernorm(x, ln_g, ln_b)
        x1 = x_norm @ w1_w + w1_b
        x_conv = _silu(_depthwise_conv(x1, conv_w))
        x_ssm = _selective_scan(x_conv, A_log, D_skip, W_dt, b_dt, W_B, W_C)
        v = _silu(x_norm @ v1_w + v1_b)
        return x_ssm * v @ w2_w + w2_b

    def _L1_xattn_ref(tokens, context, Wq, Wk, Wv, Wo, bo):
        import jax, jax.numpy as jnp
        import numpy as np
        EMBED_DIM = 128
        HIDDEN_DIM = 128
        NUM_HEADS = 16
        CONTEXT_DIM = 96
        HEAD_DIM = EMBED_DIM // NUM_HEADS
        SCALE = HEAD_DIM ** (-0.5)

        def _split_heads(x):
            b, n, _ = x.shape
            return x.reshape(b, n, NUM_HEADS, -1).transpose(0, 2, 1, 3)
        Q = _split_heads(tokens @ Wq)
        K = _split_heads(context @ Wk)
        V = _split_heads(context @ Wv)
        scores = jnp.einsum('bhnd,bhmd->bhnm', Q, K) * SCALE
        attn = jax.nn.softmax(scores, axis=-1)
        out = jnp.einsum('bhnm,bhmd->bhnd', attn, V)
        b, h, n, d = out.shape
        out = out.transpose(0, 2, 1, 3).reshape(b, n, h * d)
        return out @ Wo + bo

    def _L1_ffn_ref(hidden_states, Wq, bq, bn_gamma, bn_beta, sub_key0, sub_key1, expert_down, expert_up):
        import jax, jax.numpy as jnp
        import numpy as np
        H = 8
        QD = 32
        HALF = QD // 2
        DIMS = (32, 32)
        TOPK = 16
        DTK = 4
        EPS_BN = 1e-05
        EPS_NORM = 1e-12

        def _l2norm(x):
            n = jnp.linalg.norm(x, axis=-1, keepdims=True)
            return x / jnp.maximum(n, EPS_NORM)
        B, S, D = hidden_states.shape
        q = (hidden_states @ Wq + bq).reshape(B, S, H, QD)
        mean = q.mean(axis=(0, 1, 2))
        var = q.var(axis=(0, 1, 2))
        q = (q - mean) / jnp.sqrt(var + EPS_BN) * bn_gamma + bn_beta
        q0 = _l2norm(q[..., :HALF])
        q1 = _l2norm(q[..., HALF:])
        k0 = _l2norm(sub_key0)
        k1 = _l2norm(sub_key1)
        s0 = jnp.einsum('bshq,kq->bshk', q0, k0)
        s1 = jnp.einsum('bshq,kq->bshk', q1, k1)
        ts0, ti0 = jax.lax.top_k(s0, DTK)
        ts1, ti1 = jax.lax.top_k(s1, DTK)
        comb_s = (ts0[..., :, None] + ts1[..., None, :]).reshape(B, S, H, DTK * DTK)
        comb_i = (ti0[..., :, None] * DIMS[1] + ti1[..., None, :]).reshape(B, S, H, DTK * DTK)
        top_s, pos = jax.lax.top_k(comb_s, TOPK)
        idx = jnp.take_along_axis(comb_i, pos, axis=-1)
        w = jax.nn.softmax(top_s, axis=-1)
        down = expert_down[idx]
        up = expert_up[idx]
        eh = jnp.einsum('bshkd,bsd->bshk', down, hidden_states)
        eh = jax.nn.gelu(eh, approximate=False)
        out = jnp.einsum('bshko,bshk->bso', up, eh * w)
        return out

    def _L2_attn_ref(x, in_proj_w, conv_w, conv_b, A_log, D_param, dt_proj_w, dt_proj_b, out_proj_w):
        import jax, jax.numpy as jnp
        import numpy as np
        D_MODEL = 128
        D_STATE = 64
        D_CONV = 4
        EXPAND = 2
        DT_RANK = D_MODEL // 16
        D_INNER = EXPAND * D_MODEL
        BATCH, T = (2, 256)
        D_PROJ = 2 * D_INNER + 2 * D_STATE + DT_RANK

        def _reference_tuple_inner(x, in_proj_w, conv_w, conv_b, A_log, D_param, dt_proj_w, dt_proj_b, out_proj_w):
            Bsz = x.shape[0]
            proj = jnp.einsum('btd,pd->btp', x, in_proj_w)
            x_inner = proj[..., :D_INNER]
            z = proj[..., D_INNER:2 * D_INNER]
            B_param = proj[..., 2 * D_INNER:2 * D_INNER + D_STATE]
            C_param = proj[..., 2 * D_INNER + D_STATE:2 * D_INNER + 2 * D_STATE]
            delta_raw = proj[..., -DT_RANK:]
            xc = jax.lax.conv_general_dilated(x_inner.transpose(0, 2, 1), conv_w, (1,), [(D_CONV - 1, 0)], feature_group_count=D_INNER, dimension_numbers=('NCH', 'OIH', 'NCH'))
            xc = jax.nn.silu((xc + conv_b[None, :, None]).transpose(0, 2, 1))
            delta = jax.nn.softplus(jnp.einsum('btr,ir->bti', delta_raw, dt_proj_w) + dt_proj_b)
            A = -jnp.exp(A_log)
            h0 = jnp.zeros((Bsz, D_INNER, D_STATE), x.dtype)

            def step(h, inp):
                d_t, b_t, c_t, xc_t = inp
                dA = jnp.exp(A[None, None, :] * d_t[..., None])
                h = dA * h + d_t[..., None] * b_t[:, None, :] * xc_t[..., None]
                y = jnp.einsum('bis,bs->bi', h, c_t)
                return (h, y)
            hT, ys = jax.lax.scan(step, h0, (delta.transpose(1, 0, 2), B_param.transpose(1, 0, 2), C_param.transpose(1, 0, 2), xc.transpose(1, 0, 2)))
            y = ys.transpose(1, 0, 2) + D_param * xc
            out = jnp.einsum('bti,di->btd', y * jax.nn.silu(z), out_proj_w)
            return (out, hT)
        return _reference_tuple_inner(x, in_proj_w, conv_w, conv_b, A_log, D_param, dt_proj_w, dt_proj_b, out_proj_w)[0]

    def _L2_xattn_ref(x, context, Wq, Wk, Wv, Wo, bo):
        import jax, jax.numpy as jnp
        import numpy as np
        HEADS = 16
        DIM_HEAD = 64
        SCALE = DIM_HEAD ** (-0.5)
        QUERY_DIM = 128
        CONTEXT_DIM = 96
        INNER_DIM = HEADS * DIM_HEAD
        B, Nq, _ = x.shape
        Nk = context.shape[1]
        q = x @ Wq
        k = context @ Wk
        v = context @ Wv
        q = q.reshape(B, Nq, HEADS, DIM_HEAD).transpose(0, 2, 1, 3)
        k = k.reshape(B, Nk, HEADS, DIM_HEAD).transpose(0, 2, 1, 3)
        v = v.reshape(B, Nk, HEADS, DIM_HEAD).transpose(0, 2, 1, 3)
        sim = jnp.einsum('bhid,bhjd->bhij', q, k) * SCALE
        attn = jax.nn.softmax(sim, axis=-1)
        out = jnp.einsum('bhij,bhjd->bhid', attn, v)
        out = out.transpose(0, 2, 1, 3).reshape(B, Nq, INNER_DIM)
        return out @ Wo + bo

    def _L2_ffn_ref(x, gate_w, w1, b1, w2, b2, w3, b3, sw1, sw2, sw3):
        import jax, jax.numpy as jnp
        import numpy as np
        D = 128
        H = 128
        E = 8
        K = 2
        I = 2 * 128
        ROUTE_SCALE = 1.0
        B, S, _ = x.shape
        xt = x.reshape(-1, D)
        logits = xt @ gate_w.T
        scores = jax.nn.softmax(logits.astype(jnp.float32), axis=-1)
        top_vals, idx = jax.lax.top_k(scores, K)
        weights = jnp.take_along_axis(scores, idx, axis=1).astype(x.dtype) * ROUTE_SCALE
        xs = xt[:, None, :] * weights[:, :, None]
        y = jnp.zeros_like(xt)
        for e in range(E):
            mask = (idx == e).astype(x.dtype)
            h = jax.nn.silu(jnp.einsum('tkd,hd->tkh', xs, w1[e]) + b1[e])
            x2 = jnp.einsum('tkh,dh->tkd', h, w2[e]) + b2[e]
            x3 = jnp.einsum('tkd,hd->tkh', xs, w3[e]) + b3[e]
            y = y + jnp.sum(x2 * x3 * mask[:, :, None], axis=1)
        z = jax.nn.silu(xt @ sw1.T) * (xt @ sw2.T) @ sw3.T
        return (y + z).reshape(B, S, D)

    def _L3_attn_ref(hidden_states, past_states, Wq, bq, Wk, bk, Wv, bv, Wo, bo, Wrq, brq, Wrk, brk, Wrv, brv, Wg, bg):
        import jax, jax.numpy as jnp
        import numpy as np
        B, S, H, NH, P = (1, 256, 128, 16, 2)
        D = H // NH
        SCALE = 1.0 / np.sqrt(D).astype(np.float32)

        def _lin(x, W, b):
            return x @ W + b

        def _split_heads(x):
            return x.reshape(*x.shape[:-2], x.shape[-2], NH, D).swapaxes(-3, -2)

        def _merge_heads(x):
            return x.swapaxes(-3, -2).reshape(*x.shape[:-3], x.shape[-2], H)
        q = _split_heads(_lin(hidden_states, Wq, bq))
        k = _split_heads(_lin(hidden_states, Wk, bk))
        v = _split_heads(_lin(hidden_states, Wv, bv))
        scores = jnp.einsum('bhsd,bhtd->bhst', q, k) * SCALE
        attn = jax.nn.softmax(scores, axis=-1)
        ctx = jnp.einsum('bhst,bhtd->bhsd', attn, v)
        output = _lin(_merge_heads(ctx), Wo, bo)
        rq = _split_heads(_lin(output, Wrq, brq))
        rk = _split_heads(_lin(past_states, Wrk, brk))
        rv = _split_heads(_lin(past_states, Wrv, brv))
        rscores = jnp.einsum('bhsd,pbhtd->pbhst', rq, rk) * SCALE
        rattn = jax.nn.softmax(rscores, axis=-1)
        rctx = jnp.einsum('pbhst,pbhtd->pbhsd', rattn, rv)
        recursive_output = _merge_heads(rctx).mean(axis=0)
        gate = jax.nn.sigmoid(_lin(jnp.concatenate([output, recursive_output], axis=-1), Wg, bg))
        output = output * (1.0 - gate) + recursive_output * gate
        return output

    def _L3_xattn_ref(x_text, x_vision, text_mask, vision_mask, Wq, Wk, Wv, W_film_in, b_film_in, W_film_out, b_film_out, g_norm_in, b_norm_in, g_norm_out, b_norm_out, g_ffn, b_ffn, W1, b1, W2, b2, log_dt, A_re, A_im, C_re, C_im, D_skip, mod_gate):
        import jax, jax.numpy as jnp
        import numpy as np
        B, T, DT, G, DV = (16, 64, 128, 72, 96)
        H, DH = (4, 32)
        INNER = H * DH
        HID = 4 * DT
        N_STATE = 64
        K_TOP = 32

        def layernorm(x, g, b, eps=1e-05):
            m = x.mean(-1, keepdims=True)
            v = x.var(-1, keepdims=True)
            return (x - m) * jax.lax.rsqrt(v + eps) * g + b

        def s4d(x, log_dt, A_re, A_im, C_re, C_im, D_skip):
            Bb, L, D = x.shape
            dt = jnp.exp(log_dt)
            A = A_re + 1j * A_im
            C = C_re + 1j * C_im
            dtA = dt[:, None] * A
            dC = C * (jnp.exp(dtA) - 1.0) / A
            powers = jnp.exp(dtA[:, :, None] * jnp.arange(L))
            K = 2.0 * jnp.einsum('dn,dnl->dl', dC, powers).real
            n = 2 * L
            Kf = jnp.fft.rfft(K, n=n, axis=-1)
            xf = jnp.fft.rfft(x, n=n, axis=1)
            y = jnp.fft.irfft(xf * Kf.T[None], n=n, axis=1)[:, :L]
            return y + x * D_skip
        Bb, Tt, D = x_text.shape
        Gg = x_vision.shape[1]
        Q = (x_text @ Wq).reshape(Bb, Tt, H, DH)
        K = (x_vision @ Wk).reshape(Bb, Gg, H, DH)
        scores = jnp.einsum('bthd,bghd->bhtg', Q, K) / np.sqrt(DH).astype(np.float32)
        scores = jnp.where(vision_mask[:, None, None, :], scores, -jnp.inf)
        topv, topi = jax.lax.top_k(scores, K_TOP)
        probs = jax.nn.softmax(topv, axis=-1)
        bi = jnp.arange(Bb)[:, None, None, None]
        hi = jnp.arange(H)[None, :, None, None]
        ti = jnp.arange(Tt)[None, None, :, None]
        attn = jnp.zeros_like(scores).at[bi, hi, ti, topi].set(probs)
        attn_mean = attn.mean(axis=1)
        V = x_vision @ Wv
        c_t = jnp.einsum('btg,bgd->btd', attn_mean, V)
        c_t = c_t * text_mask[..., None]
        x = layernorm(x_text, g_norm_in, b_norm_in)
        scale_in, shift_in = jnp.split(c_t @ W_film_in + b_film_in, 2, axis=-1)
        x = x * (1.0 + mod_gate * scale_in) + mod_gate * shift_in
        y = s4d(x, log_dt, A_re, A_im, C_re, C_im, D_skip)
        scale_out, shift_out = jnp.split(c_t @ W_film_out + b_film_out, 2, axis=-1)
        y = y * (1.0 + mod_gate * scale_out) + mod_gate * shift_out
        xt = x_text + y
        h = layernorm(xt, g_ffn, b_ffn)
        h = jax.nn.gelu(h @ W1 + b1, approximate=False) @ W2 + b2
        xt = xt + h
        return layernorm(xt, g_norm_out, b_norm_out)

    def _L3_ffn_ref(x, gate_w, expert_bias, w_gate, w_up, w_down, shared_gate_w, shared_up_w, shared_down_w):
        import jax, jax.numpy as jnp
        import numpy as np
        B, S, D = (2, 64, 128)
        E, K, I = (16, 8, 128)
        I_SH = 128
        ROUTE_SCALE = 2.826
        gates = jnp.einsum('bsd,ed->bse', x, gate_w)
        scores = jax.nn.sigmoid(gates.astype(jnp.float32))
        sel_scores = scores + expert_bias
        _, inds = jax.lax.top_k(sel_scores, K)
        selected = jnp.take_along_axis(scores, inds, axis=-1)
        selected = selected / selected.sum(axis=-1, keepdims=True)
        selected = selected * ROUTE_SCALE
        onehot = jax.nn.one_hot(inds, E, dtype=selected.dtype)
        combine = jnp.einsum('bske,bsk->bse', onehot, selected)
        hg = jnp.einsum('bsd,eid->bsei', x, w_gate)
        hu = jnp.einsum('bsd,eid->bsei', x, w_up)
        h = jax.nn.silu(hg) * hu
        ye = jnp.einsum('bsei,edi->bsed', h, w_down)
        y = jnp.einsum('bsed,bse->bsd', ye, combine).astype(x.dtype)
        g = jnp.einsum('bsd,id->bsi', x, shared_gate_w)
        u = jnp.einsum('bsd,id->bsi', x, shared_up_w)
        y = y + jnp.einsum('bsi,di->bsd', jax.nn.silu(g) * u, shared_down_w)
        return y
    x = _layernorm(x + _L0_attn_ref(x, L0_attn_W_qkv, L0_attn_W_out), axis=-1)
    x = _layernorm(x + _L0_xattn_ref(ctx_768, x, mask_BxS2_bk0, L0_xattn_ln_x_g, L0_xattn_ln_x_b, L0_xattn_ln_l_g, L0_xattn_ln_l_b, L0_xattn_qn_g, L0_xattn_kn_g, L0_xattn_Wq, L0_xattn_Wkv, L0_xattn_Wlkv, L0_xattn_Wo, L0_xattn_bo), axis=-1)
    x = _layernorm(x + _L0_ffn_ref(x, L0_ffn_Wqkv, L0_ffn_q_scale, L0_ffn_k_scale, L0_ffn_Wo, L0_ffn_ln_g, L0_ffn_ln_b, L0_ffn_W1, L0_ffn_b1, L0_ffn_W2, L0_ffn_b2), axis=-1)
    x = _layernorm(x + _L1_attn_ref(x, L1_attn_ln_g, L1_attn_ln_b, L1_attn_w1_w, L1_attn_w1_b, L1_attn_v1_w, L1_attn_v1_b, L1_attn_w2_w, L1_attn_w2_b, L1_attn_conv_w, L1_attn_A_log, L1_attn_D_skip, L1_attn_W_dt, L1_attn_b_dt, L1_attn_W_B, L1_attn_W_C), axis=-1)
    x = _layernorm(x + _L1_xattn_ref(x, ctx_768, L1_xattn_Wq, L1_xattn_Wk, L1_xattn_Wv, L1_xattn_Wo, L1_xattn_bo), axis=-1)
    x = _layernorm(x + _L1_ffn_ref(x, L1_ffn_Wq, L1_ffn_bq, L1_ffn_bn_gamma, L1_ffn_bn_beta, L1_ffn_sub_key0, L1_ffn_sub_key1, L1_ffn_expert_down, L1_ffn_expert_up), axis=-1)
    x = _layernorm(x + _L2_attn_ref(x, L2_attn_in_proj_w, L2_attn_conv_w, L2_attn_conv_b, L2_attn_A_log, L2_attn_D_param, L2_attn_dt_proj_w, L2_attn_dt_proj_b, L2_attn_out_proj_w), axis=-1)
    x = _layernorm(x + _L2_xattn_ref(x, ctx_768, L2_xattn_Wq, L2_xattn_Wk, L2_xattn_Wv, L2_xattn_Wo, L2_xattn_bo), axis=-1)
    x = _layernorm(x + _L2_ffn_ref(x, L2_ffn_gate_w, L2_ffn_w1, L2_ffn_b1, L2_ffn_w2, L2_ffn_b2, L2_ffn_w3, L2_ffn_b3, L2_ffn_sw1, L2_ffn_sw2, L2_ffn_sw3), axis=-1)
    x = _layernorm(x + _L3_attn_ref(x, L3_attn_past_states, L3_attn_Wq, L3_attn_bq, L3_attn_Wk, L3_attn_bk, L3_attn_Wv, L3_attn_bv, L3_attn_Wo, L3_attn_bo, L3_attn_Wrq, L3_attn_brq, L3_attn_Wrk, L3_attn_brk, L3_attn_Wrv, L3_attn_brv, L3_attn_Wg, L3_attn_bg), axis=-1)
    x = _layernorm(x + _L3_xattn_ref(x, ctx_768, mask_BxS_bf1, mask_BxS2_bf1, L3_xattn_Wq, L3_xattn_Wk, L3_xattn_Wv, L3_xattn_W_film_in, L3_xattn_b_film_in, L3_xattn_W_film_out, L3_xattn_b_film_out, L3_xattn_g_norm_in, L3_xattn_b_norm_in, L3_xattn_g_norm_out, L3_xattn_b_norm_out, L3_xattn_g_ffn, L3_xattn_b_ffn, L3_xattn_W1, L3_xattn_b1, L3_xattn_W2, L3_xattn_b2, L3_xattn_log_dt, L3_xattn_A_re, L3_xattn_A_im, L3_xattn_C_re, L3_xattn_C_im, L3_xattn_D_skip, L3_xattn_mod_gate), axis=-1)
    x = _layernorm(x + _L3_ffn_ref(x, L3_ffn_gate_w, L3_ffn_expert_bias, L3_ffn_w_gate, L3_ffn_w_up, L3_ffn_w_down, L3_ffn_shared_gate_w, L3_ffn_shared_up_w, L3_ffn_shared_down_w), axis=-1)
    return x

_drawn_inputs = setup_inputs


def setup_inputs(seed=0):
    import zlib

    import numpy as np

    out = dict(_drawn_inputs(seed))
    spreads = {'L0_xattn_ln_x_g': (1.0, 0.6),
     'L0_xattn_ln_x_b': (0.0, 0.543),
     'L0_xattn_ln_l_g': (1.0, 0.2),
     'L0_xattn_ln_l_b': (0.0, 0.1),
     'L0_xattn_qn_g': (1.0, 0.593),
     'L0_xattn_kn_g': (1.0, 0.6),
     'L0_xattn_bo': (0.0, 0.1),
     'L0_ffn_q_scale': (1.0, 0.6),
     'L0_ffn_k_scale': (1.0, 0.6),
     'L0_ffn_ln_g': (1.0, 0.6),
     'L0_ffn_ln_b': (0.0, 0.8),
     'L0_ffn_b1': (0.0, 0.8),
     'L0_ffn_b2': (0.0, 0.1),
     'L1_attn_ln_g': (1.0, 0.2),
     'L1_attn_ln_b': (0.0, 0.1),
     'L1_attn_w1_b': (0.0, 0.1),
     'L1_attn_v1_b': (0.0, 0.324),
     'L1_attn_w2_b': (0.0, 0.1),
     'L1_attn_D_skip': (1.0, 0.2),
     'L1_attn_b_dt': (-4.0, 0.6),
     'L1_ffn_bq': (0.0, 0.8),
     'L1_ffn_bn_gamma': (1.0, 0.6),
     'L1_ffn_bn_beta': (0.0, 0.8),
     'L2_attn_conv_b': (0.0, 0.8),
     'L2_attn_D_param': (1.0, 0.6),
     'L2_attn_dt_proj_b': (0.0, 0.8),
     'L2_xattn_bo': (0.0, 0.1),
     'L3_attn_bq': (0.0, 0.8),
     'L3_attn_bk': (0.0, 0.8),
     'L3_attn_bv': (0.0, 0.74),
     'L3_attn_bo': (0.0, 0.1),
     'L3_attn_brq': (0.0, 0.8),
     'L3_attn_brk': (0.0, 0.8),
     'L3_attn_brv': (0.0, 0.1),
     'L3_attn_bg': (0.0, 0.8),
     'L3_xattn_b_film_in': (0.0, 0.1),
     'L3_xattn_b_film_out': (0.0, 0.303),
     'L3_xattn_g_norm_in': (1.0, 0.2),
     'L3_xattn_b_norm_in': (0.0, 0.1),
     'L3_xattn_g_norm_out': (1.0, 0.2),
     'L3_xattn_b_norm_out': (0.0, 0.1),
     'L3_xattn_g_ffn': (1.0, 0.6),
     'L3_xattn_b_ffn': (0.0, 0.8),
     'L3_xattn_b1': (0.0, 0.8),
     'L3_xattn_b2': (0.0, 0.276),
     'L3_xattn_A_re': (-0.5, 0.2),
     'L3_ffn_expert_bias': (0.0, 0.8)}
    factors = {'L0_ffn_W1': 3.778,
     'L0_ffn_W2': 3.73,
     'L1_attn_A_log': 3.311,
     'L1_attn_W_dt': 8.0,
     'L1_xattn_bo': 5.361,
     'L1_ffn_Wq': 8.0,
     'L1_ffn_sub_key0': 8.0,
     'L1_ffn_sub_key1': 8.0,
     'L1_ffn_expert_down': 2.988,
     'L1_ffn_expert_up': 3.938,
     'L2_attn_in_proj_w': 8.0,
     'L2_attn_conv_w': 8.0,
     'L2_attn_A_log': 8.0,
     'L2_attn_dt_proj_w': 8.0,
     'L2_attn_out_proj_w': 8.0,
     'L2_ffn_b1': 8.0,
     'L2_ffn_b2': 8.0,
     'L2_ffn_b3': 8.0,
     'L3_attn_past_states': 8.0,
     'L3_attn_Wq': 8.0,
     'L3_attn_Wk': 8.0,
     'L3_attn_Wv': 3.632,
     'L3_attn_Wo': 2.976,
     'L3_attn_Wrq': 8.0,
     'L3_attn_Wrk': 8.0,
     'L3_attn_Wrv': 8.0,
     'L3_attn_Wg': 8.0,
     'L3_xattn_Wq': 8.0,
     'L3_xattn_Wk': 8.0,
     'L3_xattn_Wv': 5.811,
     'L3_xattn_W_film_in': 6.978,
     'L3_xattn_W_film_out': 8.0,
     'L3_xattn_W1': 3.381,
     'L3_xattn_W2': 3.07,
     'L3_ffn_gate_w': 8.0,
     'L3_ffn_w_gate': 8.0,
     'L3_ffn_w_up': 8.0,
     'L3_ffn_w_down': 8.0,
     'L3_ffn_shared_gate_w': 8.0,
     'L3_ffn_shared_up_w': 8.0,
     'L3_ffn_shared_down_w': 8.0}
    for name, (base, spread) in spreads.items():
        noise = np.random.default_rng([zlib.crc32(name.encode()), seed]).standard_normal(out[name].shape)
        drawn = base * np.exp(spread * noise) if base else spread * noise
        out[name] = jnp.asarray(drawn.astype(out[name].dtype))
    for name, factor in factors.items():
        out[name] = (out[name] * factor).astype(out[name].dtype)
    return out
```

```python
from contextlib import ExitStack, contextmanager

import numpy as np

import concourse.bass as bass
from concourse import mybir

F32 = mybir.dt.float32
BF16 = mybir.dt.bfloat16
I32 = mybir.dt.int32
U8 = mybir.dt.uint8
ALU = mybir.AluOpType
ACT = mybir.ActivationFunctionType
AX = mybir.AxisListType.X

NB, T, D = 16, 128, 128
NC_, DC = 120, 96
G = 4
GT = G * T
H16 = 16
NEG = -1e30
EPS = 1e-5
ds = bass.ds


@contextmanager
def stage(nc, *names):
    with ExitStack() as es:
        sems = [es.enter_context(nc.semaphore(n)) for n in names]
        with nc.Block() as block:
            yield (block, *sems)
        if sems:
            with nc.Block() as clearing:
                @clearing.sync
                def _(sp):
                    for s in sems:
                        sp.sem_clear(s)


class Chain:

    def __init__(self, eng, sem):
        self.eng, self.sem, self.n = eng, sem, 0

    def __call__(self, ins):
        ins.then_inc(self.sem, 1)
        self.n += 1
        self.eng.wait_ge(self.sem, self.n)


class Core:

    def __init__(self, nc, ins, out, es):
        self.nc, self.ins, self.out, self.es = nc, ins, out, es
        self.prefix = ""
        self.psum = es.enter_context(nc.psum_tensor("psum", [128, 8 * 512], F32))
        self.bank = [self.psum[:, i * 512:(i + 1) * 512] for i in range(8)]
        self.f_psum = self.bank[7].rearrange("p (g d) -> p g d", g=G)

    def sb(self, es, name, shape, dt=F32):
        return es.enter_context(self.nc.sbuf_tensor(self.prefix + name, shape, dt))


def col(ap, n):
    return ap.unsqueeze(2).to_broadcast([*ap.shape, n])


def rows(ap, n):
    return ap.unsqueeze(1).to_broadcast([ap.shape[0], n, ap.shape[1]])


def load(K, *pairs):
    with stage(K.nc, "loaded") as (block, loaded):
        @block.sync
        def _(sp):
            with K.nc.allow_non_contiguous_dma(reason="small parameter columns"):
                for dst, src in pairs:
                    sp.dma_start(dst, src).then_inc(loaded, 16)
            sp.wait_ge(loaded, 16 * len(pairs))


def column(v):
    return v.rearrange("(p o) -> p o", o=1)


def row(v):
    return v.rearrange("(o n) -> o n", o=1)



def constants(K):
    nc, es = K.nc, K.es
    K.x_all = K.sb(es, "x_all", [128, NB, D])
    K.xg = K.sb(es, "xg", [128, G, D])
    K.xT = K.sb(es, "xT", [128, G, T])
    K.y = K.sb(es, "y", [128, G, D])
    K.ident = K.sb(es, "ident", [128, 128])
    K.ident16 = K.sb(es, "ident16", [128, 128], BF16)
    K.ones = K.sb(es, "ones", [128, 128])
    K.head8 = K.sb(es, "head8", [128, H16])
    K.minus_half = K.sb(es, "minus_half", [128, 64])
    K.ctx_all = K.sb(es, "ctx_all", [NC_, NB, DC])
    K.ctxT_all = K.sb(es, "ctxT_all", [DC, NB, NC_])
    K.cT = K.sb(es, "cT", [DC, G, NC_])
    K.pick3 = K.sb(es, "pick3", [96, 32], BF16)
    K.zeros16 = K.sb(es, "zeros16", [128, 512], BF16)
    K.stats = K.sb(es, "stats", [128, G, 6])
    K.mean_var = K.sb(es, "mean_var", [128, G, 2])
    K.rstd = K.sb(es, "rstd", [128, G])
    with stage(nc, "pool_step") as (block, pool_step):
        @block.gpsimd
        def _(pool):
            step = Chain(pool, pool_step)
            step(nc.gpsimd.memset(K.ident[:], 0.0))
            step(nc.gpsimd.affine_select(out=K.ident[:], in_=K.ident[:], compare_op=ALU.not_equal, fill=1.0,
                                         base=0, pattern=[[-1, 128]], channel_multiplier=1))
            step(nc.gpsimd.tensor_copy(K.ident16[:], K.ident[:]))
            step(nc.gpsimd.memset(K.ones[:], 1.0))
            step(nc.gpsimd.memset(K.minus_half[:], -0.5))
            step(nc.gpsimd.memset(K.head8[:], 1.0))
            step(nc.gpsimd.affine_select(out=K.head8[:], in_=K.head8[:], compare_op=ALU.is_ge, fill=0.0,
                                         base=0, pattern=[[-8, H16]], channel_multiplier=1))
            nc.gpsimd.affine_select(out=K.head8[:], in_=K.head8[:], compare_op=ALU.is_ge, fill=0.0,
                                    base=7, pattern=[[8, H16]], channel_multiplier=-1)

        @block.vector
        def _(dve):
            nc.vector.memset(K.zeros16[:], 0.0)
    with stage(nc) as (block,):
        @block.vector
        def _(dve):
            for r in range(3):
                rows_ = slice(32 * r, 32 * r + 32)
                nc.vector.tensor_copy(K.pick3[rows_, :], K.ident16[rows_, rows_])



def load_group(K, b0, src=None):
    nc = K.nc
    src = K.x_all if src is None else src
    ps = K.bank[0]
    with stage(nc, "x_copied", "x_transposed") as (block, x_copied, x_transposed):
        @block.vector
        def _(dve):
            nc.vector.tensor_copy(K.xg[:], src[:, ds(b0, G), :]).then_inc(x_copied, 1)

        @block.tensor
        def _(pe):
            pe.wait_ge(x_copied, 1)
            for g in range(G):
                last = nc.tensor.transpose(ps[:, g * T:(g + 1) * T], K.xg[:, g, :], K.ident[:])
            last.then_inc(x_transposed, 1)

        @block.scalar
        def _(act):
            act.wait_ge(x_transposed, 1)
            nc.scalar.copy(K.xT[:].rearrange("p g t -> p (g t)"), ps)


def layer_norm(K, dst, src, n, rows_=128, prep=None):
    nc = K.nc
    with stage(nc, "dve_step", "var_ready", "rstd_ready", "pool_step") as (block, dve_step, var_ready, rstd_ready, pool_step):
        @block.vector
        def _(dve):
            step = Chain(dve, dve_step)
            if prep:
                step(prep())
            for g in range(G):
                step(nc.vector.bn_stats(K.stats[:rows_, g, :], src(g)))
            for g in range(G):
                last = nc.vector.bn_aggr(K.mean_var[:rows_, g, :], K.stats[:rows_, g, :])
                last.then_inc(var_ready, 1)
            dve.wait_ge(rstd_ready, 1)
            for g in range(G):
                nc.vector.tensor_scalar(dst(g), src(g), K.mean_var[:rows_, g, 0:1], K.rstd[:rows_, g:g + 1],
                                        ALU.subtract, ALU.mult)

        @block.gpsimd
        def _(pool):
            pool.wait_ge(var_ready, G)
            step = Chain(pool, pool_step)
            step(nc.gpsimd.tensor_scalar(K.rstd[:rows_, :], K.mean_var[:rows_, :, 1], EPS, None, ALU.add))
            nc.gpsimd.tensor_tensor(K.rstd[:rows_, :], K.rstd[:rows_, :], K.minus_half[:rows_, 0:G],
                                    ALU.pow).then_inc(rstd_ready, 1)


def finish_group(K, b0, f=None):
    nc = K.nc
    layer_norm(K, lambda g: K.x_all[:, ds(b0 + g, 1), :].rearrange("p a d -> p (a d)"), lambda g: K.y[:, g, :], D,
               prep=lambda: nc.vector.tensor_tensor(K.y[:], K.f_psum if f is None else f, K.xg[:], ALU.add))


def transposed(K, src, dst, parts, n, banks=(0, 1), scale=None, bias=None):
    nc = K.nc
    cols = src(0).shape[1]
    lots = [(i, min(4, n - i)) for i in range(0, n, 4)]
    with stage(nc, "turned", "moved") as (block, turned, moved):
        @block.tensor
        def _(pe):
            for k, (i0, m) in enumerate(lots):
                if k >= 2:
                    pe.wait_ge(moved, k - 1)
                for i in range(m):
                    last = nc.tensor.transpose(K.bank[banks[k % 2]][:cols, i * parts:(i + 1) * parts], src(i0 + i),
                                               K.ident[:parts, :parts])
                last.then_inc(turned, 1)

        @block.scalar
        def _(act):
            for k, (i0, m) in enumerate(lots):
                act.wait_ge(turned, k + 1)
                tile = K.bank[banks[k % 2]][:cols, :m * parts].rearrange("p (m t) -> p m t", m=m)
                if scale is None:
                    nc.scalar.copy(dst(i0, m), tile).then_inc(moved, 1)
                else:
                    nc.scalar.activation(dst(i0, m), tile, ACT.Identity, bias=0.0 if bias is None else bias,
                                         scale=scale).then_inc(moved, 1)


def out_project(K, oT, w, chunks, bias=None):
    nc = K.nc
    with stage(nc) as (block,):
        @block.tensor
        def _(pe):
            for g in range(G):
                for c in range(chunks):
                    nc.tensor.matmul(K.f_psum[:, g, :], oT(c, g), w(c), start=(c == 0),
                                     stop=(c == chunks - 1 and bias is None))
                if bias is not None:
                    nc.tensor.matmul(K.f_psum[:, g, :], K.ones[0:1, :], bias, start=False, stop=True)


def attention_core(K, name, units, HU, SW, blocks, dh, scale, scores, values, out_to, es, o_bias=None):
    nc = K.nc
    NU = len(units)
    P_ = K.sb(es, name + "_p", [128, 2, HU * SW])
    PT = K.sb(es, name + "_pT", [128, 2, HU * len(blocks), T])
    mx = K.sb(es, name + "_max", [128, 2, HU])
    rs = K.sb(es, name + "_rsum", [128, 2, HU])
    W = sum(n for _, n in blocks)
    S = [K.bank[i][:, :HU * SW].rearrange("p (h k) -> p h k", h=HU) for i in (0, 1)]
    TP = [K.bank[i] for i in (2, 3)]
    O = [K.bank[i][:, :HU * (dh + 1)].rearrange("p (h d) -> p h d", h=HU) for i in (4, 5)]
    Pv = [P_[:, i, :].rearrange("p (h k) -> p h k", h=HU) for i in (0, 1)]
    n_turn = HU * len(blocks)

    def run():
        with stage(nc, "scored", "max_found", "shifted", "exped", "turned", "pT_moved", "valued", "recip", "out_ready") as (
                block, scored, max_found, shifted, exped, turned, pT_moved, valued, recip, out_ready):
            @block.tensor
            def _(pe):
                def score(u):
                    if u >= 2:
                        pe.wait_ge(shifted, u - 1)
                    scores(units[u], S[u % 2]).then_inc(scored, 1)

                def turn(u):
                    pe.wait_ge(exped, u + 1)
                    if u >= 2:
                        pe.wait_ge(pT_moved, u - 1)
                    k = 0
                    for i in range(HU):
                        for off, n in blocks:
                            last = nc.tensor.transpose(TP[u % 2][:n, k * T:(k + 1) * T],
                                                       Pv[u % 2][:, i, off:off + n], K.ident[:])
                            k += 1
                    last.then_inc(turned, 1)

                def value(u):
                    pe.wait_ge(pT_moved, u + 1)
                    if u >= 2:
                        pe.wait_ge(out_ready, u - 1)
                    for i in range(HU):
                        for b, (off, n) in enumerate(blocks):
                            last = nc.tensor.matmul(O[u % 2][:, i, :], PT[:n, u % 2, i * len(blocks) + b, :],
                                                    values(units[u], i, b), start=(b == 0), stop=(b == len(blocks) - 1))
                    last.then_inc(valued, 1)

                for s in range(NU + 3):
                    if s < NU:
                        score(s)
                    if 2 <= s < NU + 2:
                        turn(s - 2)
                    if s >= 3:
                        value(s - 3)

            @block.vector
            def _(dve):
                def shift(u):
                    dve.wait_ge(scored, u + 1)
                    nc.vector.reduce_max(mx[:, u % 2, :], S[u % 2][:, :, :W], AX).then_inc(max_found, 1)
                    dve.wait_ge(max_found, u + 1)
                    if u >= 2:
                        dve.wait_ge(turned, u - 1)
                    nc.vector.tensor_tensor(Pv[u % 2][:, :, :W], S[u % 2][:, :, :W], col(mx[:, u % 2, :], W),
                                            ALU.subtract).then_inc(shifted, 1)

                def normalise(u):
                    dve.wait_ge(valued, u + 1)
                    nc.vector.reciprocal(rs[:, u % 2, :], O[u % 2][:, :, dh]).then_inc(recip, 1)
                    dve.wait_ge(recip, u + 1)
                    nc.vector.tensor_tensor(out_to(units[u]), O[u % 2][:, :, 0:dh], col(rs[:, u % 2, :], dh),
                                            ALU.mult).then_inc(out_ready, 1)

                for s in range(NU + 3):
                    if s < NU:
                        shift(s)
                    if s >= 3:
                        normalise(s - 3)

            @block.scalar
            def _(act):
                def exp(u):
                    act.wait_ge(shifted, u + 1)
                    nc.scalar.activation(Pv[u % 2][:, :, :W], Pv[u % 2][:, :, :W], ACT.Exp, scale=scale).then_inc(exped, 1)

                def move(u):
                    act.wait_ge(turned, u + 1)
                    if u >= 2:
                        act.wait_ge(valued, u - 1)
                    sizes = sorted({n for _, n in blocks})
                    if len(sizes) == 1:
                        n = sizes[0]
                        nc.scalar.copy(PT[:n, u % 2, :, :], TP[u % 2][:n, :n_turn * T].rearrange(
                            "p (k t) -> p k t", t=T)).then_inc(pT_moved, 1)
                    else:
                        tp = TP[u % 2][:, :n_turn * T].rearrange("p (i b t) -> p i b t", b=len(blocks), t=T)
                        pt = PT[:, u % 2, :, :].rearrange("p (i b) t -> p i b t", b=len(blocks))
                        for b, (off, n) in enumerate(blocks):
                            last = nc.scalar.copy(pt[:n, :, b, :], tp[:n, :, b, :])
                            if b == len(blocks) - 1:
                                last.then_inc(pT_moved, 1)

                for s in range(NU + 2):
                    if s >= 2:
                        move(s - 2)
                    if s < NU:
                        exp(s)
    return run


def keys_by_head(K, kT, kTm, n, done=None):
    nc = K.nc
    with stage(nc) as (block,):
        @block.vector
        def _(dve):
            for h in range(10):
                nc.vector.tensor_scalar(kTm[:, h, :], kT, K.head8[:, h:h + 1], None, ALU.mult)

        @block.gpsimd
        def _(pool):
            for h in range(10, H16):
                nc.gpsimd.tensor_scalar(kTm[:, h, :], kT, K.head8[:, h:h + 1], 1.0, ALU.mult, ALU.mult)



def l0_attn(K):
    nc, I = K.nc, K.ins
    CS, dh = 64, 8
    scale = dh ** -0.5
    with ExitStack() as es:
        sb = lambda *a: K.sb(es, *a)
        wqkv = sb("wqkv", [128, 3 * D])
        wout = sb("wout", [128, D])
        mask = sb("chunk_mask", [128, T])
        mask16 = sb("chunk_mask16", [128, T], BF16)
        to_next = sb("to_next", [128, T])
        qT = sb("qT", [128, G, T])
        kT = sb("kT", [128, GT])
        kTm = sb("kTm", [128, H16, GT])
        v = sb("v", [128, G, H16, dh + 1])
        ksum = sb("ksum", [128, G])
        kmean = sb("kmean", [128, G, H16])
        o = sb("o", [128, G, D])
        oT = sb("oT", [128, G, T])
        cross = sb("cross", [128, G, H16])
        term = sb("term", [128, G, D])
        load(K, (wqkv[:], I["L0_attn_W_qkv"]), (wout[:], I["L0_attn_W_out"]))
        with stage(nc, "pool_step") as (block, pool_step):
            @block.gpsimd
            def _(pool):
                step = Chain(pool, pool_step)
                step(nc.gpsimd.memset(mask[:], 0.0))
                step(nc.gpsimd.affine_select(out=mask[:], in_=mask[:], compare_op=ALU.is_ge, fill=NEG, base=0,
                                             pattern=[[-1, T]], channel_multiplier=1))
                step(nc.gpsimd.memset(mask[CS:T, 0:CS], NEG))
                step(nc.gpsimd.tensor_copy(mask16[:], mask[:]))
                step(nc.gpsimd.memset(to_next[:], 0.0))
                nc.gpsimd.memset(to_next[0:CS, CS:T], 0.5 / CS)

            @block.vector
            def _(dve):
                nc.vector.memset(v[:], 1.0)

        def scores(u, S):
            g, c = u
            nc.tensor.matmul(S, qT[:, g, :], kTm[:, 4 * c:4 * c + 4, g * T:(g + 1) * T], start=True, stop=False)
            return nc.tensor.matmul(S, K.ident16[:], rows(mask16[:], 4), start=False, stop=True)

        core = attention_core(K, "l0a", [(g, c) for g in range(G) for c in range(4)], 4, T, [(0, T)], dh, scale, scores,
                              lambda u, i, b: v[:, u[0], 4 * u[1] + i, :],
                              lambda u: o[:, u[0], 32 * u[1]:32 * u[1] + 32].rearrange("p (h d) -> p h d", h=4), es)
        with nc.Fori(0, NB // G) as i:
            b0 = i * G
            load_group(K, b0)
            xT = K.xT[:].rearrange("p g t -> p (g t)")
            with stage(nc, "q_ready", "k_ready", "v_ready") as (block, q_ready, k_ready, v_ready):
                @block.tensor
                def _(pe):
                    nc.tensor.matmul(K.bank[0], wqkv[:, 0:D], xT, start=True, stop=True).then_inc(q_ready, 1)
                    nc.tensor.matmul(K.bank[1], wqkv[:, D:2 * D], xT, start=True, stop=True).then_inc(k_ready, 1)
                    for g in range(G):
                        last = nc.tensor.matmul(K.bank[2][:, g * D:(g + 1) * D], K.xT[:, g, :], wqkv[:, 2 * D:3 * D],
                                                start=True, stop=True)
                    last.then_inc(v_ready, 1)

                @block.scalar
                def _(act):
                    act.wait_ge(q_ready, 1)
                    nc.scalar.copy(qT[:].rearrange("p g t -> p (g t)"), K.bank[0])
                    act.wait_ge(v_ready, 1)
                    for g in range(G):
                        nc.scalar.copy(v[:, g, :, 0:dh], K.bank[2][:, g * D:(g + 1) * D].rearrange("p (h d) -> p h d", d=dh))

                @block.vector
                def _(dve):
                    dve.wait_ge(k_ready, 1)
                    nc.vector.tensor_copy(kT[:], K.bank[1])
                    nc.vector.reduce_sum(ksum[:], K.bank[1].rearrange("p (g t) -> p g t", g=G)[:, :, 0:CS], AX)
            keys_by_head(K, kT[:], kTm, GT)
            core()
            with stage(nc, "kmean_ready", "q_dot", "v_mean", "tanhed", "dve_step") as (block, kmean_ready, q_dot, v_mean, tanhed, dve_step):
                @block.vector
                def _(dve):
                    for g in range(G):
                        last = nc.vector.tensor_scalar(kmean[:, g, :], K.head8[:], ksum[:, g:g + 1], 1.0 / CS, ALU.mult, ALU.mult)
                        last.then_inc(kmean_ready, 1)
                    step = Chain(dve, dve_step)
                    dve.wait_ge(tanhed, 1)
                    step(nc.vector.tensor_scalar(cross[:], cross[:], 0.5, 0.5, ALU.mult, ALU.add))
                    dve.wait_ge(v_mean, 1)
                    for g in range(G):
                        step(nc.vector.tensor_tensor(term[:, g, :].rearrange("p (h d) -> p h d", h=H16),
                                                     K.bank[1][:, g * D:(g + 1) * D].rearrange("p (h d) -> p h d", h=H16),
                                                     col(cross[:, g, :], dh), ALU.mult))
                    nc.vector.tensor_tensor(o[:], o[:], term[:], ALU.add)

                @block.tensor
                def _(pe):
                    pe.wait_ge(kmean_ready, G)
                    for g in range(G):
                        last = nc.tensor.matmul(K.bank[0][:, g * H16:(g + 1) * H16], qT[:, g, :], kmean[:, g, :], start=True, stop=True)
                    last.then_inc(q_dot, 1)
                    for g in range(G):
                        last = nc.tensor.matmul(K.bank[1][:, g * D:(g + 1) * D], to_next[:], v[:, g, :, 0:dh], start=True, stop=True)
                    last.then_inc(v_mean, 1)

                @block.scalar
                def _(act):
                    act.wait_ge(q_dot, 1)
                    nc.scalar.activation(cross[:].rearrange("p g h -> p (g h)"), K.bank[0][:, 0:G * H16], ACT.Tanh,
                                         scale=0.5 * scale).then_inc(tanhed, 1)
            transposed(K, lambda i: o[:, i, :], lambda i, m: oT[:, i:i + m, :], T, G)
            out_project(K, lambda c, g: oT[:, g, :], lambda c: wout[:], 1)
            finish_group(K, b0)




def load_context(K):
    load(K, (K.ctx_all[:], K.ins["ctx_768"].rearrange("b t d -> t b d")))
    transposed(K, lambda i: K.ctx_all[:, i, :], lambda i, m: K.ctxT_all[:, i:i + m, :], NC_, NB)


def context_group(K, b0):
    nc = K.nc
    with stage(nc) as (block,):
        @block.vector
        def _(dve):
            nc.vector.tensor_copy(K.cT[:], K.ctxT_all[:, ds(b0, G), :])



def l0_xattn(K):
    nc, I = K.nc, K.ins
    H, dh = 2, 64
    L = T + NC_
    with ExitStack() as es:
        sb = lambda *a: K.sb(es, *a)
        wq = sb("wq", [D, D])
        wkv = sb("wkv", [DC, 2 * D])
        wlkv = sb("wlkv", [D, 2 * D])
        wo = sb("wo", [D, D])
        bo = sb("bo", [1, D])
        ln_x = sb("ln_x", [DC, 2])
        ln_l = sb("ln_l", [D, 2])
        gamma = sb("gamma", [D, 2])
        mask_bytes = sb("mask_bytes", [128, NB * NC_ // 4], I32)
        mask_all = sb("mask_all", [128, NB, NC_])
        mask = sb("mask", [128, G, NC_])
        cg = sb("cg", [NC_, G, DC])
        cn = sb("cn", [NC_, G, DC])
        xn = sb("xn", [128, G, D])
        cnT = sb("cnT", [DC, G, NC_])
        lnT = sb("lnT", [128, G, T])
        sq = sb("sq", [128, 3, G * D])
        ss = sb("ss", [128, 3, G * H])
        qkn = sb("qkn", [128, 3, G, D])
        qT = sb("qT", [128, G, T])
        kT = sb("kT", [128, G, L])
        v_lat = sb("v_lat", [128, G, H, dh + 1])
        v_ctx = sb("v_ctx", [NC_, G, H, dh + 1])
        o = sb("o", [128, G, D])
        oT = sb("oT", [128, G, T])
        g_ = lambda n: column(I["L0_xattn_" + n])
        load(K, (wq[:], I["L0_xattn_Wq"]), (wkv[:], I["L0_xattn_Wkv"]), (wlkv[:], I["L0_xattn_Wlkv"]),
             (wo[:], I["L0_xattn_Wo"]), (bo[:], row(I["L0_xattn_bo"])),
             (ln_x[:, 0:1], g_("ln_x_g")), (ln_x[:, 1:2], g_("ln_x_b")), (ln_l[:, 0:1], g_("ln_l_g")),
             (ln_l[:, 1:2], g_("ln_l_b")), (gamma[0:dh, 0:1], g_("qn_g")), (gamma[dh:D, 0:1], g_("qn_g")),
             (gamma[0:dh, 1:2], g_("kn_g")), (gamma[dh:D, 1:2], g_("kn_g")),
             (mask_bytes[:], I["mask_BxS2_bk0"].rearrange("b t -> (b t)").partition_broadcast(128)))
        with stage(nc) as (block,):
            @block.vector
            def _(dve):
                nc.vector.tensor_scalar(mask_all[:].rearrange("p b t -> p (b t)"), mask_bytes[:].bitcast(U8), -1.0, -NEG, ALU.add, ALU.mult)
                nc.vector.memset(ss[:], 1.0)
                nc.vector.memset(v_lat[:], 1.0)
                nc.vector.memset(v_ctx[:], 1.0)

            @block.scalar
            def _(act):
                nc.scalar.mul(gamma[:, 0:1], gamma[:, 0:1], dh ** -0.5)

        def scores(u, S):
            g, h = u
            nc.tensor.matmul(S[:, 0, 0:L], qT[dh * h:dh * h + dh, g, :], kT[dh * h:dh * h + dh, g, :], start=True, stop=False)
            return nc.tensor.matmul(S[:, 0, T:L], K.ones[dh * h:dh * h + 1, :], mask[dh * h:dh * h + 1, g, :], start=False, stop=True)

        core = attention_core(K, "l0x", [(g, h) for g in range(G) for h in range(H)], 1, 256, [(0, T), (T, NC_)], dh, 1.0, scores,
                              lambda u, i, b: (v_lat, v_ctx)[b][:, u[0], u[1], :],
                              lambda u: o[:, u[0], dh * u[1]:dh * u[1] + dh].rearrange("p (h d) -> p h d", h=1), es)
        parts = (128, 128, NC_)
        with nc.Fori(0, NB // G) as i:
            b0 = i * G
            with stage(nc) as (block,):
                @block.vector
                def _(dve):
                    nc.vector.tensor_copy(K.xg[:], K.x_all[:, ds(b0, G), :])
                    nc.vector.tensor_copy(cg[:], K.ctx_all[:, ds(b0, G), :])
                    nc.vector.tensor_copy(mask[:], mask_all[:, ds(b0, G), :])
            layer_norm(K, lambda g: xn[:, g, :], lambda g: K.xg[:, g, :], D)
            layer_norm(K, lambda g: cn[:, g, :], lambda g: cg[:, g, :], DC, rows_=NC_)
            transposed(K, lambda g: xn[:, g, :], lambda i, m: lnT[:, i:i + m, :], T, G, scale=ln_l[:, 0:1], bias=ln_l[:, 1:2])
            transposed(K, lambda g: cn[:, g, :], lambda i, m: cnT[:, i:i + m, :], NC_, G, scale=ln_x[:, 0:1], bias=ln_x[:, 1:2])
            with stage(nc, "projected", "squared", "ss_ready", "pool_step", "inv_ready") as (block, projected, squared, ss_ready, pool_step, inv_ready):
                @block.tensor
                def _(pe):
                    for n, (src, w) in enumerate(((lnT, wq[:, :]), (lnT, wlkv[:, 0:D]), (cnT, wkv[:, 0:D]),
                                                  (lnT, wlkv[:, D:]), (cnT, wkv[:, D:]))):
                        m = NC_ if src is cnT else T
                        for g in range(G):
                            last = nc.tensor.matmul(K.bank[n][:m, g * D:(g + 1) * D], src[:, g, :], w, start=True, stop=True)
                        last.then_inc(projected, 1)

                @block.scalar
                def _(act):
                    for n, m in enumerate(parts):
                        act.wait_ge(projected, n + 1)
                        nc.scalar.square(sq[:m, n, :], K.bank[n][:m, :]).then_inc(squared, 1)
                    act.wait_ge(projected, 5)
                    nc.scalar.copy(v_lat[:, :, :, 0:dh], K.bank[3].rearrange("p (g h d) -> p g h d", g=G, h=H))
                    nc.scalar.copy(v_ctx[:, :, :, 0:dh], K.bank[4][:NC_, :].rearrange("p (g h d) -> p g h d", g=G, h=H))

                @block.vector
                def _(dve):
                    for n, m in enumerate(parts):
                        dve.wait_ge(squared, n + 1)
                        nc.vector.reduce_sum(ss[:m, n, :], sq[:m, n, :].rearrange("p (g d) -> p g d", d=dh), AX).then_inc(ss_ready, 1)
                    dve.wait_ge(inv_ready, 1)
                    for n, m in enumerate(parts):
                        nc.vector.tensor_tensor(qkn[:m, n, :, :].rearrange("p g (h d) -> p (g h) d", h=H),
                                                K.bank[n][:m, :].rearrange("p (g d) -> p g d", d=dh),
                                                col(ss[:m, n, :], dh), ALU.mult)

                @block.gpsimd
                def _(pool):
                    pool.wait_ge(ss_ready, 3)
                    step = Chain(pool, pool_step)
                    flat = ss[:].rearrange("p n g -> p (n g)")
                    step(nc.gpsimd.tensor_scalar(flat, flat, 1.0 / dh, 1e-16, ALU.mult, ALU.max))
                    nc.gpsimd.tensor_tensor(flat, flat, K.minus_half[:, 0:3 * G * H], ALU.pow).then_inc(inv_ready, 1)
            transposed(K, lambda g: qkn[:, 0, g, :], lambda i, m: qT[:, i:i + m, :], T, G, scale=gamma[:, 0:1])
            transposed(K, lambda g: qkn[:, 1, g, :], lambda i, m: kT[:, i:i + m, 0:T], T, G, scale=gamma[:, 1:2])
            transposed(K, lambda g: qkn[:NC_, 2, g, :], lambda i, m: kT[:, i:i + m, T:L], NC_, G, scale=gamma[:, 1:2])
            core()
            transposed(K, lambda g: o[:, g, :], lambda i, m: oT[:, i:i + m, :], T, G)
            out_project(K, lambda c, g: oT[:, g, :], lambda c: wo[:], 1, bias=bo[:])
            finish_group(K, b0)



def l1_xattn(K):
    nc, I = K.nc, K.ins
    dh = 8
    with ExitStack() as es:
        sb = lambda *a: K.sb(es, *a)
        wq, wo = sb("wq", [D, D]), sb("wo", [D, D])
        wk, wv = sb("wk", [DC, D]), sb("wv", [DC, D])
        bo = sb("bo", [1, D])
        qT = sb("qT", [128, G, T])
        kT = sb("kT", [128, G * NC_])
        kTm = sb("kTm", [128, H16, G * NC_])
        v = sb("v", [NC_, G, H16, dh + 1])
        o = sb("o", [128, G, D])
        oT = sb("oT", [128, G, T])
        load(K, *[(t[:], I["L1_xattn_" + n]) for t, n in ((wq, "Wq"), (wk, "Wk"), (wv, "Wv"), (wo, "Wo"))],
             (bo[:], row(I["L1_xattn_bo"])))
        with stage(nc) as (block,):
            @block.vector
            def _(dve):
                nc.vector.memset(v[:], 1.0)

        def scores(u, S):
            g, c = u
            return nc.tensor.matmul(S[:, :, 0:NC_], qT[:, g, :], kTm[:, 4 * c:4 * c + 4, g * NC_:(g + 1) * NC_], start=True, stop=True)

        core = attention_core(K, "l1x", [(g, c) for g in range(G) for c in range(4)], 4, T, [(0, NC_)], dh, dh ** -0.5, scores,
                              lambda u, i, b: v[:, u[0], 4 * u[1] + i, :],
                              lambda u: o[:, u[0], 32 * u[1]:32 * u[1] + 32].rearrange("p (h d) -> p h d", h=4), es)
        with nc.Fori(0, NB // G) as i:
            b0 = i * G
            load_group(K, b0)
            context_group(K, b0)
            GC = G * NC_
            with stage(nc, "q_ready", "k_ready", "v_ready") as (block, q_ready, k_ready, v_ready):
                @block.tensor
                def _(pe):
                    nc.tensor.matmul(K.bank[0], wq[:], K.xT[:].rearrange("p g t -> p (g t)"), start=True, stop=True).then_inc(q_ready, 1)
                    nc.tensor.matmul(K.bank[1][:, :GC], wk[:], K.cT[:].rearrange("p g t -> p (g t)"), start=True, stop=True).then_inc(k_ready, 1)
                    for g in range(G):
                        last = nc.tensor.matmul(K.bank[2][:NC_, g * D:(g + 1) * D], K.cT[:, g, :], wv[:], start=True, stop=True)
                    last.then_inc(v_ready, 1)

                @block.scalar
                def _(act):
                    act.wait_ge(q_ready, 1)
                    nc.scalar.copy(qT[:].rearrange("p g t -> p (g t)"), K.bank[0])
                    act.wait_ge(v_ready, 1)
                    for g in range(G):
                        nc.scalar.copy(v[:, g, :, 0:dh], K.bank[2][:NC_, g * D:(g + 1) * D].rearrange("p (h d) -> p h d", d=dh))

                @block.vector
                def _(dve):
                    dve.wait_ge(k_ready, 1)
                    nc.vector.tensor_copy(kT[:], K.bank[1][:, :GC])
            keys_by_head(K, kT[:], kTm, GC)
            core()
            transposed(K, lambda g: o[:, g, :], lambda i, m: oT[:, i:i + m, :], T, G)
            out_project(K, lambda c, g: oT[:, g, :], lambda c: wo[:], 1, bias=bo[:])
            finish_group(K, b0)



WIDE_UNITS = [(g, c) for g in range(G) for c in range(4)]


def wide_scores(K, qT, kTd, n, mask=None):
    nc = K.nc

    def scores(u, S):
        g, c = u
        if mask is not None:
            nc.tensor.matmul(S[:, :, 0:n], K.ident16[:], rows(mask, 4), start=True, stop=False, skip_group_check=True)
        for i in range(2):
            last = nc.tensor.matmul(S[:, 2 * i:2 * i + 2, 0:n], qT[:, 2 * c + i, g, :], kTd[:, 2 * c + i, :, g, :],
                                    start=mask is None, stop=True, skip_group_check=mask is not None)
        return last
    return scores


def l2_xattn(K):
    nc, I = K.nc, K.ins
    dh = 64
    E = H16 * dh
    with ExitStack() as es:
        sb = lambda *a: K.sb(es, *a)
        wq = sb("wq", [D, E])
        wk, wv = sb("wk", [DC, E]), sb("wv", [DC, E])
        wo = sb("wo", [128, E // 128, D])
        bo = sb("bo", [1, D])
        qT = sb("qT", [128, E // 128, G, T])
        kT = sb("kT", [128, E // 128, 2, G, NC_])
        v = sb("v", [NC_, G, H16, dh + 1])
        o = sb("o", [128, G, E])
        oT = sb("oT", [128, G, E // 128, T])
        load(K, (wq[:], I["L2_xattn_Wq"]), (wk[:], I["L2_xattn_Wk"]), (wv[:], I["L2_xattn_Wv"]),
             (wo[:], I["L2_xattn_Wo"].rearrange("(c p) d -> p c d", p=128)), (bo[:], row(I["L2_xattn_bo"])))
        with stage(nc) as (block,):
            @block.vector
            def _(dve):
                nc.vector.memset(v[:], 1.0)
                nc.vector.memset(kT[:], 0.0)
        core = attention_core(K, "l2x", WIDE_UNITS, 4, T, [(0, NC_)], dh, dh ** -0.5, wide_scores(K, qT, kT, NC_),
                              lambda u, i, b: v[:, u[0], 4 * u[1] + i, :], wide_to(o), es)
        with nc.Fori(0, NB // G) as i:
            b0 = i * G
            load_group(K, b0)
            context_group(K, b0)
            GC = G * NC_
            with stage(nc, "q_ready", "k_ready", "v_ready", "q_moved", "k_moved", "v_moved") as (
                    block, q_ready, k_ready, v_ready, q_moved, k_moved, v_moved):
                @block.tensor
                def _(pe):
                    for c in range(E // 128):
                        if c >= 2:
                            pe.wait_ge(q_moved, c - 1)
                            pe.wait_ge(k_moved, c - 1)
                            pe.wait_ge(v_moved, c - 1)
                        nc.tensor.matmul(K.bank[c % 2], wq[:, c * 128:(c + 1) * 128], K.xT[:].rearrange("p g t -> p (g t)"),
                                         start=True, stop=True).then_inc(q_ready, 1)
                        nc.tensor.matmul(K.bank[2 + c % 2][:, :GC], wk[:, c * 128:(c + 1) * 128],
                                         K.cT[:].rearrange("p g t -> p (g t)"), start=True, stop=True).then_inc(k_ready, 1)
                        nc.tensor.matmul(K.bank[4 + c % 2][:NC_, :], K.cT[:, c // 2, :], wv[:, (c % 2) * 512:(c % 2) * 512 + 512],
                                         start=True, stop=True).then_inc(v_ready, 1)

                @block.scalar
                def _(act):
                    for c in range(E // 128):
                        act.wait_ge(q_ready, c + 1)
                        nc.scalar.copy(qT[:, c, :, :].rearrange("p g t -> p (g t)"), K.bank[c % 2]).then_inc(q_moved, 1)

                @block.vector
                def _(dve):
                    for c in range(E // 128):
                        dve.wait_ge(k_ready, c + 1)
                        for z in range(2):
                            r = slice(64 * z, 64 * z + 64)
                            last = nc.vector.tensor_copy(kT[r, c, z, :, :].rearrange("p g t -> p (g t)"), K.bank[2 + c % 2][r, :GC])
                        last.then_inc(k_moved, 1)
                        dve.wait_ge(v_ready, c + 1)
                        nc.vector.tensor_copy(v[:, c // 2, 8 * (c % 2):8 * (c % 2) + 8, 0:dh],
                                              K.bank[4 + c % 2][:NC_, :].rearrange("p (h d) -> p h d", d=dh)).then_inc(v_moved, 1)
            core()
            wide_out(K, o, oT, wo, bo[:])
            finish_group(K, b0)


def wide_to(o):
    return lambda u: o[:, u[0], 256 * u[1]:256 * u[1] + 256].rearrange("p (h d) -> p h d", d=64)


def wide_out(K, o, oT, wo, bias=None):
    n = o.shape[2] // 128
    transposed(K, lambda i: o[:, i // n, (i % n) * 128:(i % n) * 128 + 128],
               lambda i, m: oT[:, i // n, i % n:i % n + m, :], T, G * n)
    out_project(K, lambda c, g: oT[:, g, c, :], lambda c: wo[:, c, :], n, bias=bias)



def l3_attn(K):
    nc, I = K.nc, K.ins
    dh, NP, S2 = 8, 2, 256
    scale = dh ** -0.5
    with ExitStack() as es:
        sb = lambda *a: K.sb(es, *a)
        w = {n: sb("w_" + n, [D, D]) for n in ("q", "k", "v", "o", "rq", "rk", "rv")}
        wg = sb("w_g", [D, 2, D])
        cols_ = {n: sb("b_" + n, [D, 1]) for n in ("q", "k", "rq", "rk")}
        rws = {n: sb("b_" + n, [1, D]) for n in ("v", "o", "rv", "g")}
        past = sb("past", [128, 4, D])
        pastT = sb("pastT", [128, 4, T])
        rkTm = sb("rkTm", [128, H16, NP * S2])
        rv = sb("rv", [128, 4, H16, dh + 1])
        qT = sb("qT", [128, G, T])
        kT = sb("kT", [128, GT])
        kTm = sb("kTm", [128, H16, GT])
        v = sb("v", [128, G, H16, dh + 1])
        o = sb("o", [128, G, D])
        oT = sb("oT", [128, G, T])
        outp = sb("outp", [128, G, D])
        outT = sb("outT", [128, G, T])
        ro = sb("ro", [128, NP, G, D])
        recT = sb("recT", [128, G, T])
        gate = sb("gate", [128, G, D])
        load(K, *[(w[n][:], I["L3_attn_W" + n]) for n in w], (wg[:], I["L3_attn_Wg"].rearrange("(c p) d -> p c d", p=128)),
             *[(cols_[n][:], column(I["L3_attn_b" + n])) for n in cols_], *[(rws[n][:], row(I["L3_attn_b" + n])) for n in rws],
             (past[:], I["L3_attn_past_states"].rearrange("s o (h t) d -> t (s o h) d", t=T)))
        transposed(K, lambda i: past[:, i, :], lambda i, m: pastT[:, i:i + m, :], T, 4)

        def keys_values(xT, wk, bk, wv, bv, kTm_, v_, wq=None, bq=None, qT_=None):
            flat = xT[:].rearrange("p g t -> p (g t)")
            with stage(nc, "q_ready", "k_ready", "v_ready") as (block, q_ready, k_ready, v_ready):
                @block.tensor
                def _(pe):
                    if wq is not None:
                        nc.tensor.matmul(K.bank[0], wq[:], flat, start=True, stop=True).then_inc(q_ready, 1)
                    nc.tensor.matmul(K.bank[1], wk[:], flat, start=True, stop=True).then_inc(k_ready, 1)
                    for g in range(4):
                        nc.tensor.matmul(K.bank[2][:, g * D:(g + 1) * D], xT[:, g, :], wv[:], start=True, stop=False)
                        last = nc.tensor.matmul(K.bank[2][:, g * D:(g + 1) * D], K.ones[0:1, :], bv[:], start=False, stop=True)
                    last.then_inc(v_ready, 1)

                @block.scalar
                def _(act):
                    if wq is not None:
                        act.wait_ge(q_ready, 1)
                        nc.scalar.activation(qT_[:].rearrange("p g t -> p (g t)"), K.bank[0], ACT.Identity, bias=bq[:])
                    act.wait_ge(v_ready, 1)
                    for g in range(4):
                        nc.scalar.copy(v_[:, g, :, 0:dh], K.bank[2][:, g * D:(g + 1) * D].rearrange("p (h d) -> p h d", d=dh))

                @block.vector
                def _(dve):
                    dve.wait_ge(k_ready, 1)
                    nc.vector.tensor_scalar(kT[:], K.bank[1], bk[:], None, ALU.add)
            keys_by_head(K, kT[:], kTm_, GT)

        with stage(nc) as (block,):
            @block.vector
            def _(dve):
                nc.vector.memset(v[:], 1.0)
                nc.vector.memset(rv[:], 1.0)
        keys_values(pastT, w["rk"], cols_["rk"], w["rv"], rws["rv"], rkTm, rv)

        def scores(u, S):
            g, c = u
            return nc.tensor.matmul(S, qT[:, g, :], kTm[:, 4 * c:4 * c + 4, g * T:(g + 1) * T], start=True, stop=True)

        def past_scores(u, S):
            p, g, c, j = u
            return nc.tensor.matmul(S, qT[:, g, :], rkTm[:, 4 * c + 2 * j:4 * c + 2 * j + 2, p * S2:(p + 1) * S2], start=True, stop=True)

        core = attention_core(K, "l3a", [(g, c) for g in range(G) for c in range(4)], 4, T, [(0, T)], dh, scale, scores,
                              lambda u, i, b: v[:, u[0], 4 * u[1] + i, :],
                              lambda u: o[:, u[0], 32 * u[1]:32 * u[1] + 32].rearrange("p (h d) -> p h d", h=4), es)
        past_core = attention_core(K, "l3r", [(p, g, c, j) for p in range(NP) for g in range(G) for c in range(4) for j in range(2)],
                                   2, S2, [(0, T), (T, T)], dh, scale, past_scores,
                                   lambda u, i, b: rv[:, 2 * u[0] + b, 4 * u[2] + 2 * u[3] + i, :],
                                   lambda u: ro[:, u[0], u[1], 32 * u[2] + 16 * u[3]:32 * u[2] + 16 * u[3] + 16].rearrange(
                                       "p (h d) -> p h d", h=2), es)
        with nc.Fori(0, NB // G) as i:
            b0 = i * G
            load_group(K, b0)
            keys_values(K.xT, w["k"], cols_["k"], w["v"], rws["v"], kTm, v, w["q"], cols_["q"], qT)
            core()
            transposed(K, lambda g: o[:, g, :], lambda i, m: oT[:, i:i + m, :], T, G)
            out_project(K, lambda c, g: oT[:, g, :], lambda c: w["o"][:], 1, bias=rws["o"][:])
            with stage(nc) as (block,):
                @block.scalar
                def _(act):
                    nc.scalar.copy(outp[:], K.f_psum)
            transposed(K, lambda g: outp[:, g, :], lambda i, m: outT[:, i:i + m, :], T, G)
            with stage(nc, "q_ready") as (block, q_ready):
                @block.tensor
                def _(pe):
                    nc.tensor.matmul(K.bank[0], w["rq"][:], outT[:].rearrange("p g t -> p (g t)"), start=True, stop=True).then_inc(q_ready, 1)

                @block.scalar
                def _(act):
                    act.wait_ge(q_ready, 1)
                    nc.scalar.activation(qT[:].rearrange("p g t -> p (g t)"), K.bank[0], ACT.Identity, bias=cols_["rq"][:])
            past_core()
            with stage(nc, "dve_step") as (block, dve_step):
                @block.vector
                def _(dve):
                    step = Chain(dve, dve_step)
                    step(nc.vector.tensor_tensor(ro[:, 0, :, :], ro[:, 0, :, :], ro[:, 1, :, :], ALU.add))
                    nc.vector.tensor_scalar(ro[:, 0, :, :], ro[:, 0, :, :], 1.0 / NP, None, ALU.mult)
            transposed(K, lambda g: ro[:, 0, g, :], lambda i, m: recT[:, i:i + m, :], T, G)
            with stage(nc, "gate_dot", "tanhed", "dve_step") as (block, gate_dot, tanhed, dve_step):
                @block.tensor
                def _(pe):
                    for g in range(G):
                        out = K.bank[0][:, g * D:(g + 1) * D]
                        nc.tensor.matmul(out, outT[:, g, :], wg[:, 0, :], start=True, stop=False)
                        nc.tensor.matmul(out, recT[:, g, :], wg[:, 1, :], start=False, stop=False)
                        last = nc.tensor.matmul(out, K.ones[0:1, :], rws["g"][:], start=False, stop=True)
                    last.then_inc(gate_dot, 1)

                @block.scalar
                def _(act):
                    act.wait_ge(gate_dot, 1)
                    nc.scalar.activation(gate[:].rearrange("p g d -> p (g d)"), K.bank[0], ACT.Tanh, scale=0.5).then_inc(tanhed, 1)

                @block.vector
                def _(dve):
                    step = Chain(dve, dve_step)
                    step(nc.vector.tensor_tensor(ro[:, 0, :, :], ro[:, 0, :, :], outp[:], ALU.subtract))
                    dve.wait_ge(tanhed, 1)
                    step(nc.vector.tensor_scalar(gate[:], gate[:], 0.5, 0.5, ALU.mult, ALU.add))
                    step(nc.vector.tensor_tensor(gate[:], gate[:], ro[:, 0, :, :], ALU.mult))
                    nc.vector.tensor_tensor(gate[:], gate[:], outp[:], ALU.add)
            finish_group(K, b0, f=gate[:])




def l0_ffn(K):
    nc, I = K.nc, K.ins
    dh, DEPTH, W = 64, 6, 32
    E = H16 * dh
    HI = int(D * 4 * 2 / 3)
    HC = [(0, 128), (128, 128), (256, HI - 256)]
    pre = "L0_ffn_"
    with ExitStack() as es:
        sb = lambda *a: K.sb(es, *a)
        r_all = sb("r_all", [128, NB, D])
        band = sb("band", [128, T])
        band16 = sb("band16", [128, T], BF16)
        shift = sb("shift", [128, T])
        rot = sb("rot", [128, 4, dh])
        wq = sb("wq", [D, 3 * E])
        wo = sb("wo", [128, E // 128, D])
        w1 = sb("w1", [D, 2 * HI])
        w2 = sb("w2", [128, 3, D])
        b1 = sb("b1", [128, 2, 3])
        b2 = sb("b2", [1, D])
        ln = sb("ln", [D, 2])
        gains = sb("gains", [128, 4, dh])
        tab = sb("tab", [128, 4, dh])
        xsT = sb("xsT", [128, G, T])
        sq = sb("sq", [128, 2, E])
        ss = sb("ss", [128, 2, H16])
        qk = sb("qk", [128, 2, E])
        t1 = sb("t1", [128, 2, E])
        t2 = sb("t2", [128, 2, E])
        qT = sb("qT", [128, E // 128, G, T])
        kT = sb("kT", [128, E // 128, 2, G, T])
        v = sb("v", [128, G, H16, dh + 1])
        o = sb("o", [128, G, E])
        act_T = sb("act_T", [128, 3, GT])
        gel = sb("gel", [128, 3, GT])
        xs = sb("xs", [128, G, D])
        with stage(nc, "pool_step") as (block, pool_step):
            @block.gpsimd
            def _(pool):
                step = Chain(pool, pool_step)
                step(nc.gpsimd.memset(band[:], 0.0))
                step(nc.gpsimd.affine_select(out=band[:], in_=band[:], compare_op=ALU.is_ge, fill=NEG, base=0,
                                             pattern=[[-1, T]], channel_multiplier=1))
                step(nc.gpsimd.affine_select(out=band[:], in_=band[:], compare_op=ALU.is_ge, fill=NEG, base=W,
                                             pattern=[[1, T]], channel_multiplier=-1))
                step(nc.gpsimd.tensor_copy(band16[:], band[:]))
                step(nc.gpsimd.memset(shift[:], 0.0))
                nc.gpsimd.affine_select(out=shift[:], in_=shift[:], compare_op=ALU.not_equal, fill=1.0, base=1,
                                        pattern=[[-1, T]], channel_multiplier=1)

            @block.vector
            def _(dve):
                nc.vector.memset(v[:], 1.0)
                nc.vector.memset(xsT[:], 0.0)
                nc.vector.memset(kT[:], 0.0)
                nc.vector.tensor_copy(r_all[:], K.x_all[:])
        load(K, (rot[:], I["rotary"].rearrange("n t d -> t n d")))
        out_T = qT
        core = attention_core(K, "l0f", WIDE_UNITS, 4, T, [(0, T)], dh, 8.0,
                              wide_scores(K, qT, kT, T, mask=band16[:]),
                              lambda u, i, b: v[:, u[0], 4 * u[1] + i, :], wide_to(o), es)

        def layer(name, l):
            a = I[pre + name][ds(l, 1)]
            return a.rearrange("o a b -> (o a) b") if len(a.shape) == 3 else a

        with nc.Fori(0, DEPTH) as l:
            cl = lambda name, a, b: layer(name, l)[:, a:b].rearrange("o p -> p o")
            gain = lambda name, a, b: layer(name, l)[:, a:b].partition_broadcast(128).rearrange("p o d -> p (o d)")
            h2 = dh // 2
            load(K, (wq[:], layer("Wqkv", l)), (wo[:], layer("Wo", l).rearrange("(c p) d -> p c d", p=128)),
                 (w1[:], layer("W1", l)),
                 *[(w2[:n, c, :], layer("W2", l)[a:a + n, :]) for c, (a, n) in enumerate(HC)],
                 *[(b1[:n, k, c:c + 1], cl("b1", k * HI + a, k * HI + a + n)) for k in range(2) for c, (a, n) in enumerate(HC)],
                 (b2[:], layer("b2", l)), (ln[:, 0:1], cl("ln_g", 0, D)), (ln[:, 1:2], cl("ln_b", 0, D)),
                 *[(gains[:, 2 * k + s, z * h2:z * h2 + h2], gain(("q_scale", "k_scale")[k], (z ^ s) * h2, (z ^ s) * h2 + h2))
                   for k in range(2) for s in range(2) for z in range(2)])
            with stage(nc) as (block,):
                @block.vector
                def _(dve):
                    nc.vector.tensor_tensor(tab[:], rot[:], gains[:], ALU.mult)
            with nc.Fori(0, NB // G) as i:
                b0 = i * G
                with stage(nc, "copied", "turned") as (block, copied, turned):
                    @block.vector
                    def _(dve):
                        nc.vector.tensor_copy(K.xg[:], r_all[:, ds(b0, G), :]).then_inc(copied, 1)
                        dve.wait_ge(turned, 1)
                        ps = K.bank[0].rearrange("p (g t) -> p g t", g=G)
                        nc.vector.tensor_copy(xsT[0:64, :, :], ps[0:64, :, :])
                        nc.vector.tensor_copy(xsT[64:128, :, 1:T], ps[64:128, :, 0:T - 1])

                    @block.tensor
                    def _(pe):
                        pe.wait_ge(copied, 1)
                        for g in range(G):
                            last = nc.tensor.transpose(K.bank[0][:, g * T:(g + 1) * T], K.xg[:, g, :], K.ident[:])
                        last.then_inc(turned, 1)
                with stage(nc, "qk_dot", "v_dot", "squared", "ss_ready", "rooted", "inverse_step", "qk_ready", "sin_ready", "cos_ready",
                           "rotated", "v_moved", "turned", "moved") as (
                        block, qk_dot, v_dot, squared, ss_ready, rooted, inverse_step, qk_ready, sin_ready, cos_ready,
                        rotated, v_moved, turned, moved):
                    heads = lambda t, j: t[:, j % 2, :].rearrange("p (h d) -> p h d", d=dh)
                    table = lambda j, k: rows(tab[:, 2 * (j % 2) + k, :], H16)
                    dots = lambda j: K.psum[:, (j % 2) * E:(j % 2) * E + E]
                    NJ = 2 * G

                    @block.tensor
                    def _(pe):
                        def project(j):
                            if j >= 2:
                                pe.wait_ge(qk_ready, j - 1)
                            for n in range(2):
                                at = (j % 2) * E + n * 512
                                last = nc.tensor.matmul(K.bank[2 * (j % 2) + n], xsT[:, j // 2, :], wq[:, at:at + 512], start=True, stop=True)
                            last.then_inc(qk_dot, 1)

                        def project_v(j):
                            if j >= 2:
                                pe.wait_ge(v_moved, j - 1)
                            at = 2 * E + (j % 2) * 512
                            nc.tensor.matmul(K.bank[4 + j % 2], xsT[:, j // 2, :], wq[:, at:at + 512], start=True, stop=True).then_inc(v_dot, 1)

                        def turn(j):
                            pe.wait_ge(rotated, j + 1)
                            for k in range(2):
                                if j >= 1:
                                    pe.wait_ge(moved, 2 * j + k - 1)
                                for c in range(4):
                                    at = (4 * k + c) * 128
                                    last = nc.tensor.transpose(K.bank[6 + k][:, c * T:(c + 1) * T], t1[:, j % 2, at:at + 128], K.ident[:])
                                last.then_inc(turned, 1)

                        project(0)
                        for s in range(NJ + 2):
                            if s < NJ:
                                project_v(s)
                            if s >= 2:
                                turn(s - 2)
                            if s + 1 < NJ:
                                project(s + 1)

                    @block.scalar
                    def _(act):
                        def square(j):
                            act.wait_ge(qk_dot, j + 1)
                            if j >= 2:
                                act.wait_ge(ss_ready, j - 1)
                            nc.scalar.square(sq[:, j % 2, :], dots(j)).then_inc(squared, 1)

                        def root(j):
                            act.wait_ge(ss_ready, j + 1)
                            nc.scalar.activation(ss[:, j % 2, :], ss[:, j % 2, :], ACT.Sqrt).then_inc(rooted, 1)

                        def values(j):
                            act.wait_ge(v_dot, j + 1)
                            h0 = 8 * (j % 2)
                            nc.scalar.copy(v[:, j // 2, h0:h0 + 8, 0:dh], K.bank[4 + j % 2].rearrange("p (h d) -> p h d", d=dh)).then_inc(v_moved, 1)

                        def move(j):
                            for k in range(2):
                                act.wait_ge(turned, 2 * j + k + 1)
                                turns = K.bank[6 + k].rearrange("p (c t) -> p c t", t=T)
                                if j % 2 == 0:
                                    nc.scalar.copy(qT[:, 4 * k:4 * k + 4, j // 2, :], turns).then_inc(moved, 1)
                                else:
                                    nc.scalar.copy(kT[0:64, 4 * k:4 * k + 4, 0, j // 2, :], turns[0:64])
                                    nc.scalar.copy(kT[64:128, 4 * k:4 * k + 4, 1, j // 2, :], turns[64:128]).then_inc(moved, 1)

                        for s in range(NJ + 2):
                            if s < NJ:
                                square(s)
                                values(s)
                            if s >= 2:
                                move(s - 2)
                            if s < NJ:
                                root(s)

                    @block.vector
                    def _(dve):
                        inverse = Chain(dve, inverse_step)

                        def scaled(j):
                            dve.wait_ge(rooted, j + 1)
                            inverse(nc.vector.tensor_scalar(ss[:, j % 2, :], ss[:, j % 2, :], 1e-12, None, ALU.max))
                            inverse(nc.vector.reciprocal(ss[:, j % 2, :], ss[:, j % 2, :]))
                            if j >= 2:
                                dve.wait_ge(cos_ready, j - 1)
                                dve.wait_ge(sin_ready, 2 * j - 2)
                            nc.vector.tensor_tensor(heads(qk, j), dots(j).rearrange("p (h d) -> p h d", d=dh),
                                                    col(ss[:, j % 2, :], dh), ALU.mult).then_inc(qk_ready, 1)

                        def norm(j):
                            dve.wait_ge(squared, j + 1)
                            if j >= 2:
                                dve.wait_ge(qk_ready, j - 1)
                            nc.vector.reduce_sum(ss[:, j % 2, :], heads(sq, j), AX).then_inc(ss_ready, 1)

                        def sines(j):
                            dve.wait_ge(qk_ready, j + 1)
                            if j >= 2:
                                dve.wait_ge(rotated, j - 1)
                            for z in range(2):
                                half = slice(z * h2, z * h2 + h2)
                                other = slice((1 - z) * h2, (1 - z) * h2 + h2)
                                nc.vector.tensor_tensor(heads(t2, j)[:, :, half], heads(qk, j)[:, :, other], table(j, 1)[:, :, half],
                                                        ALU.mult).then_inc(sin_ready, 1)

                        def rotate(j):
                            dve.wait_ge(cos_ready, j + 1)
                            dve.wait_ge(sin_ready, 2 * j + 2)
                            nc.vector.tensor_tensor(t1[:, j % 2, :], t1[:, j % 2, :], t2[:, j % 2, :], ALU.add).then_inc(rotated, 1)

                        for s in range(NJ + 2):
                            if 1 <= s <= NJ:
                                scaled(s - 1)
                            if s >= 2:
                                rotate(s - 2)
                            if s < NJ:
                                norm(s)
                            if 1 <= s <= NJ:
                                sines(s - 1)

                    @block.gpsimd
                    def _(pool):
                        def cosines(j):
                            pool.wait_ge(qk_ready, j + 1)
                            if j >= 2:
                                pool.wait_ge(turned, 2 * j - 2)
                            nc.gpsimd.tensor_tensor(heads(t1, j), heads(qk, j), table(j, 0), ALU.mult).then_inc(cos_ready, 1)

                        for j in range(NJ):
                            cosines(j)
                core()
                wide_out(K, o, out_T[:, 0:8, :, :].rearrange("p (g2 c2) g t -> p g2 (c2 g) t", g2=4), wo)
                with stage(nc, "summed", "shifted") as (block, summed, shifted):
                    @block.vector
                    def _(dve):
                        nc.vector.tensor_tensor(K.xg[:], K.f_psum, K.xg[:], ALU.add).then_inc(summed, 1)
                        dve.wait_ge(summed, 1)
                        nc.vector.tensor_copy(xs[:, :, 0:64], K.xg[:, :, 0:64])
                        dve.wait_ge(shifted, 1)
                        nc.vector.tensor_copy(xs[:, :, 64:128], K.bank[0][:, 0:G * 64].rearrange("p (g d) -> p g d", g=G))

                    @block.tensor
                    def _(pe):
                        pe.wait_ge(summed, 1)
                        for g in range(G):
                            last = nc.tensor.matmul(K.bank[0][:, g * 64:(g + 1) * 64], shift[:], K.xg[:, g, 64:128], start=True, stop=True)
                        last.then_inc(shifted, 1)
                layer_norm(K, lambda g: xs[:, g, :], lambda g: xs[:, g, :], D)
                transposed(K, lambda g: xs[:, g, :], lambda i, m: K.xT[:, i:i + m, :], T, G, scale=ln[:, 0:1], bias=ln[:, 1:2])
                with stage(nc, "gate_dot", "a_dot", "gelued", "acted") as (block, gate_dot, a_dot, gelued, acted):
                    flat = K.xT[:].rearrange("p g t -> p (g t)")

                    @block.tensor
                    def _(pe):
                        for c, (a, n) in enumerate(HC):
                            nc.tensor.matmul(K.bank[2 * c][:n, :], w1[:, HI + a:HI + a + n], flat, start=True, stop=True).then_inc(gate_dot, 1)
                            nc.tensor.matmul(K.bank[2 * c + 1][:n, :], w1[:, a:a + n], flat, start=True, stop=True).then_inc(a_dot, 1)
                        pe.wait_ge(acted, 3)
                        for g in range(G):
                            for c, (a, n) in enumerate(HC):
                                nc.tensor.matmul(K.f_psum[:, g, :], act_T[:n, c, g * T:(g + 1) * T], w2[:n, c, :], start=(c == 0), stop=False)
                            nc.tensor.matmul(K.f_psum[:, g, :], K.ones[0:1, :], b2[:], start=False, stop=True)

                    @block.scalar
                    def _(act):
                        for c, (a, n) in enumerate(HC):
                            act.wait_ge(gate_dot, c + 1)
                            nc.scalar.activation(gel[:n, c, :], K.bank[2 * c][:n, :], ACT.Gelu, bias=b1[:n, 1, c:c + 1]).then_inc(gelued, 1)

                    @block.vector
                    def _(dve):
                        for c, (a, n) in enumerate(HC):
                            dve.wait_ge(a_dot, c + 1)
                            dve.wait_ge(gelued, c + 1)
                            nc.vector.scalar_tensor_tensor(out=act_T[:n, c, :], in0=K.bank[2 * c + 1][:n, :], scalar=b1[:n, 0, c:c + 1],
                                                           in1=gel[:n, c, :], op0=ALU.add, op1=ALU.mult).then_inc(acted, 1)
                with stage(nc) as (block,):
                    @block.vector
                    def _(dve):
                        nc.vector.tensor_tensor(r_all[:, ds(b0, G), :], K.f_psum, K.xg[:], ALU.add)
        with nc.Fori(0, NB // G) as i:
            b0 = i * G
            with stage(nc) as (block,):
                @block.vector
                def _(dve):
                    nc.vector.tensor_copy(K.xg[:], r_all[:, ds(b0, G), :])
                    nc.vector.tensor_copy(xs[:], K.x_all[:, ds(b0, G), :])
            finish_group(K, b0, f=xs[:])


def rotary_tables():
    f = np.float32
    half = np.arange(0, 64, 2, dtype=f)
    inv_freq = (f(1.0) / f(10000.0) ** (half / f(64))).astype(f)
    t = np.arange(T, dtype=f)
    freqs = t[:, None] * inv_freq[None, :]
    base = (half + f(0.4 * 64)) / f(1.4 * 64)
    scale = base[None, :] ** ((t - T // 2) / f(16))[:, None]
    two = lambda a, b: np.concatenate([a, b], -1)
    cos, sin = two(np.cos(freqs), np.cos(freqs)), two(-np.sin(freqs), np.sin(freqs))
    scale = two(scale, scale)
    inv = f(1.0) / scale
    return np.stack([cos * scale, sin * scale, cos * inv, sin * inv]).astype(f)


def clear_bank(K, ap):
    return K.nc.tensor.matmul(ap, K.ident16[:], K.zeros16[:, 0:ap.shape[1]], start=True, stop=True)


def accumulate(K, out, lhsT, rhs):
    return K.nc.tensor.matmul(out, lhsT, rhs, start=False, stop=True, skip_group_check=True)



SU = 16


def softplus(K, dst, z, bias, tmp):
    nc = K.nc
    with stage(nc, "act_step", "log_ready") as (block, act_step, log_ready):
        @block.scalar
        def _(act):
            step = Chain(act, act_step)
            step(nc.scalar.activation(dst, z, ACT.Identity, bias=bias))
            step(nc.scalar.activation(tmp, dst, ACT.Abs))
            step(nc.scalar.activation(tmp, tmp, ACT.Exp, scale=-1.0))
            nc.scalar.activation(tmp, tmp, ACT.Ln, bias=1.0).then_inc(log_ready, 1)

        @block.vector
        def _(dve):
            dve.wait_ge(log_ready, 1)
            nc.vector.scalar_tensor_tensor(out=dst, in0=dst, scalar=0.0, in1=tmp, op0=ALU.max, op1=ALU.add)


def split_rows(K, es, name, n, weights, rhs):
    nc = K.nc
    parts = K.sb(es, name + "_parts", [96, n, GT], BF16)
    rest = K.sb(es, name + "_rest", [96, n, GT])

    def run():
        with stage(nc, "dot", "first", "rest_ready", "dve_step") as (block, dot, first, rest_ready, dve_step):
            @block.tensor
            def _(pe):
                for q in range(n):
                    nc.tensor.matmul(K.bank[q][:96, :], weights(q), rhs, start=True, stop=True).then_inc(dot, 1)

            @block.scalar
            def _(act):
                for q in range(n):
                    act.wait_ge(dot, q + 1)
                    nc.scalar.copy(parts[:, q, :], K.bank[q][:96, :]).then_inc(first, 1)

            @block.vector
            def _(dve):
                for q in range(n):
                    dve.wait_ge(first, q + 1)
                    nc.vector.tensor_tensor(rest[:, q, :], K.bank[q][:96, :], parts[:, q, :], ALU.subtract).then_inc(rest_ready, 1)
                step = Chain(dve, dve_step)
                for q in range(n):
                    dve.wait_ge(rest_ready, q + 1)
                    nc.vector.tensor_copy(parts[32:64, q, :], rest[32:64, q, :])
                    step(nc.vector.tensor_copy(parts[64:96, q, :], rest[64:96, q, :]))
                    step(nc.vector.tensor_tensor(rest[64:96, q, :], rest[64:96, q, :], parts[64:96, q, :], ALU.subtract))
                    nc.vector.tensor_copy(parts[64:96, q, :], rest[64:96, q, :])
    return parts, run


def selective_scan(K, es, name, halves, chunks, dt, du, a, parts):
    nc = K.nc
    decay = K.sb(es, name + "_decay", [128, 3, G, T])
    drive = K.sb(es, name + "_drive", [128, 3, GT])
    state = K.sb(es, name + "_state", [128, 3, GT])
    read = K.sb(es, name + "_read", [128, 3, GT])
    c_rows = K.sb(es, name + "_c_rows", [128, 2, GT])
    items = [(n, h) for n in range(SU) for h in range(halves)]
    NI = len(items)
    flat = lambda t: t.rearrange("p g t -> p (g t)")

    def run():
        with stage(nc) as (block,):
            @block.tensor
            def _(pe):
                for h in range(halves):
                    clear_bank(K, K.bank[4 + h])

            @block.vector
            def _(dve):
                nc.vector.memset(decay[:], 0.0)
        with nc.Fori(0, chunks) as j:
            with stage(nc, "rows_ready", "c_moved", "decay_ready", "drive_ready", "scanned", "read_ready", "summed") as (
                    block, rows_ready, c_moved, decay_ready, drive_ready, scanned, read_ready, summed):
                @block.tensor
                def _(pe):
                    def rows_(n):
                        if n >= 2:
                            pe.wait_ge(drive_ready, halves * (n - 1))
                            pe.wait_ge(c_moved, n - 1)
                        for m in range(2):
                            last = nc.tensor.matmul(K.bank[2 * m + n % 2], K.pick3[:, m * SU + n:m * SU + n + 1].to_broadcast([96, 128]),
                                                    parts[:, ds(j, 1), :].rearrange("p o t -> p (o t)"),
                                                    start=True, stop=True)
                        last.then_inc(rows_ready, 1)

                    def add(k):
                        pe.wait_ge(read_ready, k + 1)
                        accumulate(K, K.bank[4 + items[k][1]], K.ident[:], read[:, k % 3, :]).then_inc(summed, 1)

                    rows_(0)
                    for k in range(NI + 2):
                        if k < NI and items[k][1] == 0 and items[k][0] + 1 < SU:
                            rows_(items[k][0] + 1)
                        if k >= 2:
                            add(k - 2)

                @block.scalar
                def _(act):
                    for k, (n, h) in enumerate(items):
                        if h == 0:
                            act.wait_ge(rows_ready, n + 1)
                            if n >= 2:
                                act.wait_ge(read_ready, halves * (n - 1))
                            nc.scalar.copy(c_rows[:, n % 2, :], K.bank[2 + n % 2]).then_inc(c_moved, 1)
                        if k >= 3:
                            act.wait_ge(scanned, k - 2)
                        nc.scalar.activation(decay[:, k % 3, :, 1:T], dt(h)[:, :, 1:T], ACT.Exp, scale=a(h, j * SU + n)).then_inc(decay_ready, 1)

                @block.vector
                def _(dve):
                    def drive_(k):
                        n, h = items[k]
                        dve.wait_ge(rows_ready, n + 1)
                        if k >= 3:
                            dve.wait_ge(scanned, k - 2)
                        nc.vector.tensor_tensor(drive[:, k % 3, :], K.bank[n % 2], flat(du(h)), ALU.mult).then_inc(drive_ready, 1)

                    def scan(k):
                        dve.wait_ge(drive_ready, k + 1)
                        dve.wait_ge(decay_ready, k + 1)
                        if k >= 3:
                            dve.wait_ge(read_ready, k - 2)
                        nc.vector.tensor_tensor_scan(state[:, k % 3, :], flat(decay[:, k % 3, :, :]), drive[:, k % 3, :], 0.0,
                                                     ALU.mult, ALU.add).then_inc(scanned, 1)

                    for k in range(NI + 1):
                        if k < NI:
                            drive_(k)
                        if k >= 1:
                            scan(k - 1)

                @block.gpsimd
                def _(pool):
                    for k, (n, h) in enumerate(items):
                        pool.wait_ge(scanned, k + 1)
                        pool.wait_ge(c_moved, n + 1)
                        if k >= 3:
                            pool.wait_ge(summed, k - 2)
                        nc.gpsimd.tensor_tensor(read[:, k % 3, :], c_rows[:, n % 2, :], state[:, k % 3, :], ALU.mult).then_inc(read_ready, 1)
    return run


def l1_attn(K):
    nc, I = K.nc, K.ins
    N = 16
    pre = "L1_attn_"
    with ExitStack() as es:
        sb = lambda *a: K.sb(es, *a)
        w1, v1, w2, wdt = (sb(n, [D, D]) for n in ("w1", "v1", "w2", "wdt"))
        wb, wc = sb("wb", [D, N]), sb("wc", [D, N])
        wbc3 = sb("wbc3", [D, 3, 2 * N])
        a = sb("a", [D, N])
        cw = sb("cw", [D, 3])
        cl = sb("cl", [D, 7])
        b2 = sb("b2", [1, D])
        x1 = sb("x1", [128, G, T + 2])
        u = sb("u", [128, G, T])
        u2 = sb("u2", [128, G, T])
        gate = sb("gate", [128, GT])
        dt, du, tmp = sb("dt", [128, GT]), sb("du", [128, GT]), sb("tmp", [128, GT])
        load(K, (w1[:], I[pre + "w1_w"]), (v1[:], I[pre + "v1_w"]), (w2[:], I[pre + "w2_w"]), (wdt[:], I[pre + "W_dt"]),
             (wb[:], I[pre + "W_B"]), (wc[:], I[pre + "W_C"]), (a[:], I[pre + "A_log"]),
             (cw[:], I[pre + "conv_w"].rearrange("d o k -> d (o k)")), (b2[:], row(I[pre + "w2_b"])),
             *[(cl[:, i:i + 1], column(I[pre + n])) for i, n in enumerate(("ln_g", "ln_b", "w1_b", "v1_b", "b_dt", "D_skip"))])
        with stage(nc, "exped") as (block, exped):
            @block.scalar
            def _(act):
                nc.scalar.activation(a[:], a[:], ACT.Exp).then_inc(exped, 1)

            @block.vector
            def _(dve):
                nc.vector.memset(x1[:], 0.0)
                for r in range(3):
                    nc.vector.tensor_copy(wbc3[:, r, 0:N], wb[:])
                    nc.vector.tensor_copy(wbc3[:, r, N:2 * N], wc[:])
                dve.wait_ge(exped, 1)
                nc.vector.tensor_scalar(a[:], a[:], -1.0, None, ALU.mult)
        flat = lambda t: t[:].rearrange("p g t -> p (g t)")
        parts, split = split_rows(K, es, "l1", 1, lambda q: wbc3[:].rearrange("d r n -> d (r n)"), flat(u))
        seq = lambda t: t[:].rearrange("p (g t) -> p g t", g=G)
        scan = selective_scan(K, es, "l1", 1, 1, lambda h: seq(dt), lambda h: seq(du), lambda h, n: a[:, ds(n, 1)], parts)
        with nc.Fori(0, NB // G) as i:
            b0 = i * G
            with stage(nc) as (block,):
                @block.vector
                def _(dve):
                    nc.vector.tensor_copy(K.xg[:], K.x_all[:, ds(b0, G), :])
            layer_norm(K, lambda g: K.y[:, g, :], lambda g: K.xg[:, g, :], D)
            transposed(K, lambda g: K.y[:, g, :], lambda i, m: K.xT[:, i:i + m, :], T, G, scale=cl[:, 0:1], bias=cl[:, 1:2])
            with stage(nc, "x1_dot", "v_dot", "x1_ready", "conv", "u_ready", "dt_dot") as (block, x1_dot, v_dot, x1_ready, conv, u_ready, dt_dot):
                @block.tensor
                def _(pe):
                    nc.tensor.matmul(K.bank[0], w1[:], flat(K.xT), start=True, stop=True).then_inc(x1_dot, 1)
                    nc.tensor.matmul(K.bank[1], v1[:], flat(K.xT), start=True, stop=True).then_inc(v_dot, 1)
                    pe.wait_ge(u_ready, 1)
                    nc.tensor.matmul(K.bank[2], wdt[:], flat(u), start=True, stop=True).then_inc(dt_dot, 1)

                @block.scalar
                def _(act):
                    act.wait_ge(x1_dot, 1)
                    nc.scalar.activation(x1[:, :, 1:T + 1], K.bank[0].rearrange("p (g t) -> p g t", g=G), ACT.Identity,
                                         bias=cl[:, 2:3]).then_inc(x1_ready, 1)
                    act.wait_ge(v_dot, 1)
                    nc.scalar.activation(gate[:], K.bank[1], ACT.Silu, bias=cl[:, 3:4])
                    act.wait_ge(conv, 3)
                    nc.scalar.activation(u[:], u2[:], ACT.Silu).then_inc(u_ready, 1)

                @block.vector
                def _(dve):
                    dve.wait_ge(x1_ready, 1)
                    step = Chain(dve, conv)
                    step(nc.vector.tensor_scalar(u2[:], x1[:, :, 0:T], cw[:, 0:1], None, ALU.mult))
                    for k in (1, 2):
                        step(nc.vector.scalar_tensor_tensor(out=u2[:], in0=x1[:, :, k:k + T], scalar=cw[:, k:k + 1], in1=u2[:],
                                                            op0=ALU.mult, op1=ALU.add))
            softplus(K, dt[:], K.bank[2], cl[:, 4:5], tmp[:])
            with stage(nc) as (block,):
                @block.vector
                def _(dve):
                    nc.vector.tensor_tensor(du[:], dt[:], flat(u), ALU.mult)
            split()
            scan()
            with stage(nc, "dve_step") as (block, dve_step):
                @block.vector
                def _(dve):
                    step = Chain(dve, dve_step)
                    step(nc.vector.scalar_tensor_tensor(out=flat(u), in0=flat(u), scalar=cl[:, 5:6], in1=K.bank[4], op0=ALU.mult, op1=ALU.add))
                    nc.vector.tensor_tensor(flat(u), flat(u), gate[:], ALU.mult)
            out_project(K, lambda c, g: u[:, g, :], lambda c: w2[:], 1, bias=b2[:])
            finish_group(K, b0)


def l2_attn(K):
    nc, I = K.nc, K.ins
    N, R, TAPS = 64, 8, 4
    DI = 2 * D
    pre = "L2_attn_"
    with ExitStack() as es:
        sb = lambda *a: K.sb(es, *a)
        wi = sb("wi", [D, 2 * DI + 2 * N + R])
        cw = sb("cw", [128, 2, TAPS])
        cl = sb("cl", [128, 3, 2])
        a = sb("a", [128, N])
        wdt = sb("wdt", [R, DI])
        wo = sb("wo", [128, 2, D])
        xi = sb("xi", [128, 2, G, T + TAPS - 1])
        conv = sb("conv", [128, 2, G, T])
        xc = sb("xc", [128, 2, G, T])
        z = sb("z", [128, 2, GT])
        wi3 = sb("wi3", [D, N // SU, 3, 2, SU])
        dr = sb("dr", [R, GT])
        dt, du, tmp = sb("dt", [128, 2, GT]), sb("du", [128, 2, GT]), sb("tmp", [128, GT])
        load(K, (wi[:], I[pre + "in_proj_w"]), (cw[:], I[pre + "conv_w"].rearrange("(h p) o k -> p h (o k)", p=128)),
             *[(cl[:, i, :], I[pre + n].rearrange("(h p) -> p h", p=128)) for i, n in enumerate(("conv_b", "D_param", "dt_proj_b"))],
             (a[:], I[pre + "A_log"].partition_broadcast(128)), (wdt[:], I[pre + "dt_proj_w"]),
             (wo[:], I[pre + "out_proj_w"].rearrange("(h p) d -> p h d", p=128)))
        with stage(nc, "exped") as (block, exped):
            @block.scalar
            def _(act):
                nc.scalar.activation(a[:], a[:], ACT.Exp).then_inc(exped, 1)

            @block.vector
            def _(dve):
                nc.vector.memset(xi[:], 0.0)
                for q in range(N // SU):
                    for r in range(3):
                        nc.vector.tensor_copy(wi3[:, q, r, :, :], wi[:, 2 * DI:2 * DI + 2 * N].rearrange(
                            "d (m n) -> d m n", m=2)[:, :, q * SU:(q + 1) * SU])
                dve.wait_ge(exped, 1)
                nc.vector.tensor_scalar(a[:], a[:], -1.0, None, ALU.mult)
        flat = lambda t: t.rearrange("p g t -> p (g t)")
        parts, split = split_rows(K, es, "l2", N // SU, lambda q: wi3[:, q, :, :, :].rearrange("d r m n -> d (r m n)"), flat(K.xT[:]))
        seq = lambda t, h: t[:, h, :].rearrange("p (g t) -> p g t", g=G)
        scan = selective_scan(K, es, "l2", 2, N // SU, lambda h: seq(dt, h), lambda h: seq(du, h),
                              lambda h, n: a[:, ds(n, 1)], parts)
        with nc.Fori(0, NB // G) as i:
            b0 = i * G
            load_group(K, b0)
            with stage(nc, "projected", "xi_ready", "conv_step", "dr_ready") as (block, projected, xi_ready, conv_step, dr_ready):
                @block.tensor
                def _(pe):
                    for c in range(4):
                        nc.tensor.matmul(K.bank[c], wi[:, c * 128:(c + 1) * 128], flat(K.xT[:]), start=True, stop=True).then_inc(projected, 1)
                    nc.tensor.matmul(K.bank[5][:R, :], wi[:, 640:640 + R], flat(K.xT[:]), start=True, stop=True).then_inc(projected, 1)
                    pe.wait_ge(dr_ready, 1)
                    for h in range(2):
                        nc.tensor.matmul(K.bank[6 + h], wdt[:, h * 128:(h + 1) * 128], dr[:], start=True, stop=True)

                @block.scalar
                def _(act):
                    act.wait_ge(projected, 5)
                    nc.scalar.copy(dr[:], K.bank[5][:R, :]).then_inc(dr_ready, 1)
                    for h in range(2):
                        nc.scalar.copy(xi[:, h, :, TAPS - 1:], K.bank[h].rearrange("p (g t) -> p g t", g=G)).then_inc(xi_ready, 1)
                    for h in range(2):
                        nc.scalar.activation(z[:, h, :], K.bank[2 + h], ACT.Silu)
                    for h in range(2):
                        act.wait_ge(conv_step, TAPS * (h + 1))
                        nc.scalar.activation(flat(xc[:, h, :, :]), flat(conv[:, h, :, :]), ACT.Silu, bias=cl[:, 0, h:h + 1])

                @block.vector
                def _(dve):
                    step = Chain(dve, conv_step)
                    for h in range(2):
                        dve.wait_ge(xi_ready, h + 1)
                        step(nc.vector.tensor_scalar(conv[:, h, :, :], xi[:, h, :, 0:T], cw[:, h, 0:1], None, ALU.mult))
                        for k in range(1, TAPS):
                            step(nc.vector.scalar_tensor_tensor(out=conv[:, h, :, :], in0=xi[:, h, :, k:k + T], scalar=cw[:, h, k:k + 1],
                                                                in1=conv[:, h, :, :], op0=ALU.mult, op1=ALU.add))
            for h in range(2):
                softplus(K, dt[:, h, :], K.bank[6 + h], cl[:, 2, h:h + 1], tmp[:])
            with stage(nc) as (block,):
                @block.vector
                def _(dve):
                    nc.vector.tensor_tensor(du[:], dt[:], xc[:].rearrange("p h g t -> p h (g t)"), ALU.mult)
            split()
            scan()
            with stage(nc, "dve_step") as (block, dve_step):
                @block.vector
                def _(dve):
                    step = Chain(dve, dve_step)
                    for h in range(2):
                        y = flat(xc[:, h, :, :])
                        step(nc.vector.scalar_tensor_tensor(out=y, in0=y, scalar=cl[:, 1, h:h + 1], in1=K.bank[4 + h], op0=ALU.mult, op1=ALU.add))
                        step(nc.vector.tensor_tensor(y, y, z[:, h, :], ALU.mult))
            out_project(K, lambda c, g: xc[:, c, g, :], lambda c: wo[:, c, :], 2)
            finish_group(K, b0)



def l1_ffn(K):
    nc, I = K.nc, K.ins
    H, QD, NK, E = 8, 32, 32, 128
    HALF = QD // 2
    pre = "L1_ffn_"
    with ExitStack() as es:
        sb = lambda *a: K.sb(es, *a)
        wq = sb("wq", [D, H * QD])
        bq = sb("bq", [1, H * QD])
        down, up = sb("down", [D, E]), sb("up", [E, D])
        gb = sb("gb", [128, 2, QD])
        keys = sb("keys", [NK, 2, HALF])
        key_sq = sb("key_sq", [NK, 2, HALF])
        key_ss = sb("key_ss", [NK, 2])
        key_rep = sb("key_rep", [NK, 4, 2, HALF])
        of_half = sb("of_half", [128, 8])
        key_diag = sb("key_diag", [128, 8, NK])
        q_all = sb("q_all", [128, NB, H * QD])
        qsq = sb("qsq", [128, 4, H * QD])
        mom = sb("mom", [128, 2, QD])
        bn = sb("bn", [128, 3, QD])
        qn = sb("qn", [128, G, H * QD])
        ss = sb("ss", [128, G * 2 * H])
        qhT = sb("qhT", [128, G * 2, T])
        s_ = sb("s", [128, G, 2 * H, NK])
        e_ = sb("e", [128, G, 2 * H, NK])
        m8 = sb("m8", [128, G * 2 * H, 8])
        sm = sb("sm", [128, G * 2 * H])
        pairs = sb("pairs", [128, 2, 4, NK, H])
        wt = sb("wt", [128, G, E])
        extra = sb("extra", [128, G])
        eh = sb("eh", [128, G, E])
        ehT = sb("ehT", [128, G, T])
        load(K, (wq[:], I[pre + "Wq"]), (bq[:], row(I[pre + "bq"])), (down[:], I[pre + "expert_down"]), (up[:], I[pre + "expert_up"]),
             (gb[:, 0, :], I[pre + "bn_gamma"].partition_broadcast(128)), (gb[:, 1, :], I[pre + "bn_beta"].partition_broadcast(128)),
             (keys[:, 0, :], I[pre + "sub_key0"]), (keys[:, 1, :], I[pre + "sub_key1"]))
        with stage(nc, "ss_ready", "inv_ready", "rep_ready", "spread", "block_ready", "dve_step", "pool_step") as (
                block, ss_ready, inv_ready, rep_ready, spread, block_ready, dve_step, pool_step):
            @block.vector
            def _(dve):
                step = Chain(dve, dve_step)
                step(nc.vector.tensor_tensor(key_sq[:], keys[:], keys[:], ALU.mult))
                nc.vector.reduce_sum(key_ss[:], key_sq[:], AX).then_inc(ss_ready, 1)
                dve.wait_ge(inv_ready, 1)
                step(nc.vector.tensor_tensor(key_sq[:], keys[:], col(key_ss[:], HALF), ALU.mult))
                for j in range(4):
                    last = nc.vector.tensor_copy(key_rep[:, j, :, :], key_sq[:])
                    last.then_inc(rep_ready, 1)
                dve.wait_ge(spread, 1)
                dve.wait_ge(block_ready, 1)
                nc.vector.tensor_tensor(key_diag[:], rows(K.bank[0][:, 0:NK], 8), col(of_half[:], NK), ALU.mult)

            @block.gpsimd
            def _(pool):
                step = Chain(pool, pool_step)
                step(nc.gpsimd.memset(of_half[:], 1.0))
                step(nc.gpsimd.affine_select(out=of_half[:], in_=of_half[:], compare_op=ALU.is_ge, fill=0.0, base=0,
                                             pattern=[[-HALF, 8]], channel_multiplier=1))
                nc.gpsimd.affine_select(out=of_half[:], in_=of_half[:], compare_op=ALU.is_ge, fill=0.0, base=HALF - 1,
                                        pattern=[[HALF, 8]], channel_multiplier=-1).then_inc(block_ready, 1)
                pool.wait_ge(ss_ready, 1)
                step(nc.gpsimd.tensor_scalar(key_ss[:], key_ss[:], 1e-24, None, ALU.max))
                nc.gpsimd.tensor_tensor(key_ss[:], key_ss[:], K.minus_half[:NK, 0:2], ALU.pow).then_inc(inv_ready, 1)

            @block.tensor
            def _(pe):
                pe.wait_ge(rep_ready, 4)
                nc.tensor.matmul(K.bank[0][:, 0:NK], key_rep[:].rearrange("k a b c -> k (a b c)"), K.ident[:NK, :NK],
                                 start=True, stop=True).then_inc(spread, 1)
                clear_bank(K, K.bank[6])
        with nc.Fori(0, NB // G) as i:
            b0 = i * G
            load_group(K, b0)
            with stage(nc, "q_dot", "q_moved", "squared") as (block, q_dot, q_moved, squared):
                @block.tensor
                def _(pe):
                    for g in range(G):
                        nc.tensor.matmul(K.bank[g][:, 0:256], K.xT[:, g, :], wq[:], start=True, stop=False)
                        nc.tensor.matmul(K.bank[g][:, 0:256], K.ones[0:1, :], bq[:], start=False, stop=True).then_inc(q_dot, 1)
                    for g in range(G):
                        pe.wait_ge(q_moved, g + 1)
                        pe.wait_ge(squared, g + 1)
                        accumulate(K, K.bank[6][:, 0:256], K.ones[:], qn[:, g, :])
                        accumulate(K, K.bank[6][:, 256:512], K.ones[:], qsq[:, g, :])

                @block.vector
                def _(dve):
                    for g in range(G):
                        dve.wait_ge(q_dot, g + 1)
                        nc.vector.tensor_copy(qn[:, g, :], K.bank[g][:, 0:256]).then_inc(q_moved, 1)
                    dve.wait_ge(q_moved, G)
                    nc.vector.tensor_copy(q_all[:, ds(b0, G), :], qn[:])

                @block.scalar
                def _(act):
                    for g in range(G):
                        act.wait_ge(q_moved, g + 1)
                        nc.scalar.square(qsq[:, g, :], qn[:, g, :]).then_inc(squared, 1)
        with stage(nc, "dve_step", "var_ready", "rstd_ready", "pool_step") as (block, dve_step, var_ready, rstd_ready, pool_step):
            @block.vector
            def _(dve):
                step = Chain(dve, dve_step)
                count = 1.0 / (NB * T * H)
                step(nc.vector.reduce_sum(mom[:], K.bank[6].rearrange("p (m h q) -> p m q h", m=2, h=H), AX))
                step(nc.vector.tensor_scalar(mom[:], mom[:], count, None, ALU.mult))
                step(nc.vector.tensor_tensor(bn[:, 0, :], mom[:, 0, :], mom[:, 0, :], ALU.mult))
                nc.vector.tensor_tensor(bn[:, 1, :], mom[:, 1, :], bn[:, 0, :], ALU.subtract).then_inc(var_ready, 1)
                dve.wait_ge(rstd_ready, 1)
                step(nc.vector.tensor_tensor(bn[:, 1, :], bn[:, 1, :], gb[:, 0, :], ALU.mult))
                step(nc.vector.tensor_tensor(bn[:, 2, :], mom[:, 0, :], bn[:, 1, :], ALU.mult))
                nc.vector.tensor_tensor(bn[:, 2, :], gb[:, 1, :], bn[:, 2, :], ALU.subtract)

            @block.gpsimd
            def _(pool):
                pool.wait_ge(var_ready, 1)
                step = Chain(pool, pool_step)
                step(nc.gpsimd.tensor_scalar(bn[:, 1, :], bn[:, 1, :], EPS, None, ALU.add))
                nc.gpsimd.tensor_tensor(bn[:, 1, :], bn[:, 1, :], K.minus_half[:, 0:QD], ALU.pow).then_inc(rstd_ready, 1)
        with nc.Fori(0, NB // G) as i:
            b0 = i * G
            load_group(K, b0)
            with stage(nc, "dve_step", "normed", "squared", "ss_ready", "inv_ready", "pool_step") as (
                    block, dve_step, normed, squared, ss_ready, inv_ready, pool_step):
                sq = s_[:, 0:2, :, :].rearrange("p a b c -> p (a b c)")

                @block.vector
                def _(dve):
                    step = Chain(dve, dve_step)
                    q3 = qn[:].rearrange("p g (h q) -> p (g h) q", q=QD)
                    step(nc.vector.tensor_tensor(q3, q_all[:, ds(b0, G), :].rearrange("p g (h q) -> p (g h) q", q=QD),
                                                 rows(bn[:, 1, :], G * H), ALU.mult))
                    nc.vector.tensor_tensor(q3, q3, rows(bn[:, 2, :], G * H), ALU.add).then_inc(normed, 1)
                    dve.wait_ge(squared, 1)
                    nc.vector.reduce_sum(ss[:], sq.rearrange("p (h q) -> p h q", q=HALF), AX).then_inc(ss_ready, 1)
                    dve.wait_ge(inv_ready, 1)
                    qh = qn[:].rearrange("p g (h q) -> p (g h) q", q=HALF)
                    nc.vector.tensor_tensor(qh, qh, col(ss[:], HALF), ALU.mult)

                @block.scalar
                def _(act):
                    act.wait_ge(normed, 1)
                    nc.scalar.square(sq, qn[:].rearrange("p g q -> p (g q)")).then_inc(squared, 1)

                @block.gpsimd
                def _(pool):
                    pool.wait_ge(ss_ready, 1)
                    step = Chain(pool, pool_step)
                    step(nc.gpsimd.tensor_scalar(ss[:], ss[:], 1e-24, None, ALU.max))
                    nc.gpsimd.tensor_tensor(ss[:], ss[:], K.minus_half[:], ALU.pow).then_inc(inv_ready, 1)
            transposed(K, lambda i: qn[:, i // 2, (i % 2) * 128:(i % 2) * 128 + 128], lambda i, m: qhT[:, i:i + m, :], T, 2 * G, banks=(4, 5))
            with stage(nc, "scored", "s_moved", "found", "dve_step", "exped", "eh_dot", "gelued") as (
                    block, scored, s_moved, found, dve_step, exped, eh_dot, gelued):
                @block.tensor
                def _(pe):
                    for g in range(G):
                        for c in range(2):
                            last = nc.tensor.matmul(K.bank[g][:, c * 256:(c + 1) * 256], qhT[:, 2 * g + c, :],
                                                    key_diag[:].rearrange("p a b -> p (a b)"), start=True, stop=True)
                        last.then_inc(scored, 1)
                    for g in range(G):
                        last = nc.tensor.matmul(K.bank[4][:, g * E:(g + 1) * E], K.xT[:, g, :], down[:], start=True, stop=True)
                    last.then_inc(eh_dot, 1)

                @block.scalar
                def _(act):
                    for g in range(G):
                        act.wait_ge(scored, g + 1)
                        nc.scalar.copy(s_[:, g, :, :].rearrange("p h k -> p (h k)"), K.bank[g]).then_inc(s_moved, 1)
                    act.wait_ge(eh_dot, 1)
                    nc.scalar.activation(eh[:].rearrange("p g e -> p (g e)"), K.bank[4], ACT.Gelu).then_inc(gelued, 1)
                    act.wait_ge(dve_step, 1)
                    nc.scalar.activation(e_[:], e_[:], ACT.Exp).then_inc(exped, 1)

                @block.vector
                def _(dve):
                    step = Chain(dve, dve_step)
                    sf = s_[:].rearrange("p g h k -> p (g h) k")
                    ef = e_[:].rearrange("p g h k -> p (g h) k")
                    for g in range(G):
                        dve.wait_ge(s_moved, g + 1)
                        for h in range(2 * H):
                            nc.vector.max(m8[:, g * 2 * H + h, :], s_[:, g, h, :]).then_inc(found, 1)
                    dve.wait_ge(found, G * 2 * H)
                    step(nc.vector.tensor_tensor(ef, sf, col(m8[:, :, 0], NK), ALU.subtract))
                    step(nc.vector.tensor_tensor(sf, sf, col(m8[:, :, 3], NK), ALU.is_ge))
                    dve.wait_ge(exped, 1)
                    step(nc.vector.tensor_tensor(ef, ef, sf, ALU.mult))
                    step(nc.vector.reduce_sum(sm[:], ef, AX))
                    step(nc.vector.reciprocal(sm[:], sm[:]))
                    step(nc.vector.tensor_tensor(ef, ef, col(sm[:], NK), ALU.mult))
                    for g in range(G):
                        p = e_[:, g, :, :].rearrange("p (h s) k -> p s k h", s=2)
                        step(nc.vector.tensor_tensor(pairs[:, g % 2, :, :, :], p[:, 0, 0:4, :].unsqueeze(2).to_broadcast([128, 4, NK, H]),
                                                     p[:, 1, :, :].unsqueeze(1).to_broadcast([128, 4, NK, H]), ALU.mult))
                        step(nc.vector.reduce_sum(wt[:, g, :].rearrange("p (a b) -> p a b", a=4), pairs[:, g % 2, :, :, :], AX))
                        step(nc.vector.tensor_reduce(extra[:, g:g + 1], p[:, 0, 4:NK, :], mybir.AxisListType.XY, ALU.add))
                    step(nc.vector.tensor_tensor(wt[:, :, E - 1], wt[:, :, E - 1], extra[:], ALU.add))
                    dve.wait_ge(gelued, 1)
                    nc.vector.tensor_tensor(eh[:], eh[:], wt[:], ALU.mult)
            transposed(K, lambda g: eh[:, g, :], lambda i, m: ehT[:, i:i + m, :], T, G)
            out_project(K, lambda c, g: ehT[:, g, :], lambda c: up[:], 1)
            finish_group(K, b0)



def l2_ffn(K):
    nc, I = K.nc, K.ins
    E = 8
    pre = "L2_ffn_"
    with ExitStack() as es:
        sb = lambda *a: K.sb(es, *a)
        gate = sb("gate", [D, E])
        w = [sb(f"w{i}", [128, E, D]) for i in (1, 2, 3)]
        b = [sb(f"b{i}", [128, E]) for i in (1, 2, 3)]
        sw1, sw2 = sb("sw1", [D, 2 * D]), sb("sw2", [D, 2 * D])
        sw3 = sb("sw3", [128, 2, D])
        sc, sel = sb("sc", [128, G, E]), sb("sel", [128, G, E])
        m8 = sb("m8", [128, G, 8])
        sm = sb("sm", [128, G])
        xs, xsT, hT, x3, pr = (sb(n, [128, 2, GT]) for n in ("xs", "xsT", "hT", "x3", "pr"))
        total = sb("total", [128, G, D])
        load(K, (gate[:], I[pre + "gate_w"]), *[(w[i][:], I[pre + f"w{i + 1}"].rearrange("e a b -> a e b")) for i in range(3)],
             *[(b[i][:], I[pre + f"b{i + 1}"]) for i in range(3)],
             (sw1[:], I[pre + "sw1"]), (sw2[:], I[pre + "sw2"]), (sw3[:], I[pre + "sw3"].rearrange("(c p) d -> p c d", p=128)))
        xT = K.xT[:].rearrange("p g t -> p (g t)")
        with nc.Fori(0, NB // G) as i:
            b0 = i * G
            load_group(K, b0)
            with stage(nc, "logits", "shifted", "exped", "dve_step", "shared", "silued", "z_ready", "shared_out") as (
                    block, logits, shifted, exped, dve_step, shared, silued, z_ready, shared_out):
                @block.tensor
                def _(pe):
                    for g in range(G):
                        last = nc.tensor.matmul(K.bank[0][:, g * E:(g + 1) * E], K.xT[:, g, :], gate[:], start=True, stop=True)
                    last.then_inc(logits, 1)
                    for c in range(2):
                        nc.tensor.matmul(K.bank[1 + c], sw1[:, c * 128:(c + 1) * 128], xT, start=True, stop=True)
                        nc.tensor.matmul(K.bank[3 + c], sw2[:, c * 128:(c + 1) * 128], xT, start=True, stop=True).then_inc(shared, 1)
                    pe.wait_ge(z_ready, 2)
                    for g in range(G):
                        for c in range(2):
                            last = nc.tensor.matmul(K.f_psum[:, g, :], pr[:, c, g * T:(g + 1) * T], sw3[:, c, :], start=(c == 0), stop=(c == 1))
                    last.then_inc(shared_out, 1)

                @block.scalar
                def _(act):
                    act.wait_ge(shifted, 1)
                    nc.scalar.activation(sc[:], sc[:], ACT.Exp).then_inc(exped, 1)
                    for c in range(2):
                        act.wait_ge(shared, c + 1)
                        nc.scalar.activation(hT[:, c, :], K.bank[1 + c], ACT.Silu).then_inc(silued, 1)
                    act.wait_ge(shared_out, 1)
                    nc.scalar.copy(total[:], K.f_psum)

                @block.vector
                def _(dve):
                    step = Chain(dve, dve_step)
                    dve.wait_ge(logits, 1)
                    step(nc.vector.tensor_copy(sel[:].rearrange("p g e -> p (g e)"), K.bank[0][:, 0:G * E]))
                    for g in range(G):
                        step(nc.vector.max(m8[:, g, :], sel[:, g, :]))
                    nc.vector.tensor_tensor(sc[:], sel[:], col(m8[:, :, 0], E), ALU.subtract).then_inc(shifted, 1)
                    step(nc.vector.tensor_tensor(sel[:], sel[:], col(m8[:, :, 1], E), ALU.is_ge))
                    dve.wait_ge(exped, 1)
                    step(nc.vector.reduce_sum(sm[:], sc[:], AX))
                    step(nc.vector.reciprocal(sm[:], sm[:]))
                    step(nc.vector.tensor_tensor(sc[:], sc[:], col(sm[:], E), ALU.mult))
                    step(nc.vector.tensor_tensor(sc[:], sc[:], sel[:], ALU.mult))
                    for c in range(2):
                        dve.wait_ge(silued, c + 1)
                        nc.vector.tensor_tensor(pr[:, c, :], K.bank[3 + c], hT[:, c, :], ALU.mult).then_inc(z_ready, 1)
            with stage(nc, "xs_made", "turned", "xs_moved", "h_dot", "x3_dot", "h_ready", "x3_ready", "x2_dot", "product", "back", "added") as (
                    block, xs_made, turned, xs_moved, h_dot, x3_dot, h_ready, x3_ready, x2_dot, product, back, added):
                @block.gpsimd
                def _(pool):
                    for e in range(E):
                        if e >= 2:
                            pool.wait_ge(turned, e - 1)
                        for g in range(G):
                            nc.gpsimd.tensor_scalar(xs[:, e % 2, g * D:(g + 1) * D], K.xg[:, g, :], sc[:, g, e:e + 1], 1.0,
                                                    ALU.mult, ALU.mult).then_inc(xs_made, 1)

                @block.tensor
                def _(pe):
                    def turn(e):
                        pe.wait_ge(xs_made, G * (e + 1))
                        if e >= 2:
                            pe.wait_ge(xs_moved, e - 1)
                        for g in range(G):
                            last = nc.tensor.transpose(K.bank[e % 2][:, g * T:(g + 1) * T], xs[:, e % 2, g * D:(g + 1) * D], K.ident[:])
                        last.then_inc(turned, 1)

                    def first(e):
                        pe.wait_ge(xs_moved, e + 1)
                        if e >= 1:
                            pe.wait_ge(h_ready, e)
                            pe.wait_ge(x3_ready, e)
                        nc.tensor.matmul(K.bank[2], w[0][:, e, :], xsT[:, e % 2, :], start=True, stop=True).then_inc(h_dot, 1)
                        nc.tensor.matmul(K.bank[3], w[2][:, e, :], xsT[:, e % 2, :], start=True, stop=True).then_inc(x3_dot, 1)

                    def second(e):
                        pe.wait_ge(h_ready, e + 1)
                        if e >= 1:
                            pe.wait_ge(product, e)
                        nc.tensor.matmul(K.bank[4], w[1][:, e, :], hT[:, e % 2, :], start=True, stop=True).then_inc(x2_dot, 1)

                    def turn_back(e):
                        pe.wait_ge(product, e + 1)
                        if e >= 2:
                            pe.wait_ge(added, G * (e - 1))
                        for g in range(G):
                            last = nc.tensor.transpose(K.bank[5 + e % 2][:, g * D:(g + 1) * D], pr[:, e % 2, g * T:(g + 1) * T], K.ident[:])
                        last.then_inc(back, 1)

                    turn(0)
                    for s in range(E + 2):
                        if s + 1 < E:
                            turn(s + 1)
                        if s < E:
                            first(s)
                        if 1 <= s <= E:
                            second(s - 1)
                        if s >= 2:
                            turn_back(s - 2)

                @block.scalar
                def _(act):
                    def move(e):
                        act.wait_ge(turned, e + 1)
                        if e >= 2:
                            act.wait_ge(x3_dot, e - 1)
                        nc.scalar.copy(xsT[:, e % 2, :], K.bank[e % 2]).then_inc(xs_moved, 1)

                    move(0)
                    for e in range(E):
                        if e + 1 < E:
                            move(e + 1)
                        act.wait_ge(h_dot, e + 1)
                        if e >= 2:
                            act.wait_ge(x2_dot, e - 1)
                        nc.scalar.activation(hT[:, e % 2, :], K.bank[2], ACT.Silu, bias=b[0][:, e:e + 1]).then_inc(h_ready, 1)
                        act.wait_ge(x3_dot, e + 1)
                        if e >= 2:
                            act.wait_ge(product, e - 1)
                        nc.scalar.activation(x3[:, e % 2, :], K.bank[3], ACT.Identity, bias=b[2][:, e:e + 1]).then_inc(x3_ready, 1)

                @block.vector
                def _(dve):
                    for s in range(1, E + 3):
                        if s <= E:
                            e = s - 1
                            dve.wait_ge(x2_dot, e + 1)
                            dve.wait_ge(x3_ready, e + 1)
                            if e >= 2:
                                dve.wait_ge(back, e - 1)
                            nc.vector.scalar_tensor_tensor(out=pr[:, e % 2, :], in0=K.bank[4], scalar=b[1][:, e:e + 1], in1=x3[:, e % 2, :],
                                                           op0=ALU.add, op1=ALU.mult).then_inc(product, 1)
                        if 2 <= s < E + 2:
                            e = s - 2
                            dve.wait_ge(back, e + 1)
                            if e >= 1:
                                dve.wait_ge(added, G * e)
                            for g in range(G):
                                nc.vector.scalar_tensor_tensor(out=total[:, g, :], in0=K.bank[5 + e % 2][:, g * D:(g + 1) * D],
                                                               scalar=sel[:, g, e:e + 1], in1=total[:, g, :], op0=ALU.mult,
                                                               op1=ALU.add).then_inc(added, 1)
            finish_group(K, b0, f=total[:])


def l3_ffn(K):
    nc, I = K.nc, K.ins
    E, TOP = 16, 8
    ROUTE = 2.826
    pre = "L3_ffn_"
    with ExitStack() as es:
        sb = lambda *a: K.sb(es, *a)
        gate = sb("gate", [D, E])
        bias = sb("bias", [128, E])
        w = [sb(n, [128, E, D]) for n in ("w_gate", "w_up", "w_down")]
        sg, su, sd = (sb(n, [128, D]) for n in ("sg", "su", "sd"))
        sc, ch, rp = (sb(n, [128, G, E]) for n in ("sc", "ch", "rp"))
        m8 = sb("m8", [128, G, 8])
        sm = sb("sm", [128, G])
        hT, pr = (sb(n, [128, 2, GT]) for n in ("hT", "pr"))
        total = sb("total", [128, G, D])
        load(K, (gate[:], I[pre + "gate_w"]), (bias[:], I[pre + "expert_bias"].partition_broadcast(128)),
             *[(w[i][:], I[pre + n].rearrange("e a b -> a e b")) for i, n in enumerate(("w_gate", "w_up", "w_down"))],
             (sg[:], I[pre + "shared_gate_w"]), (su[:], I[pre + "shared_up_w"]), (sd[:], I[pre + "shared_down_w"]))
        xT = K.xT[:].rearrange("p g t -> p (g t)")
        with nc.Fori(0, NB // G) as i:
            b0 = i * G
            load_group(K, b0)
            with stage(nc, "logits", "tanhed", "dve_step", "shared", "silued", "z_ready", "shared_out") as (
                    block, logits, tanhed, dve_step, shared, silued, z_ready, shared_out):
                @block.tensor
                def _(pe):
                    for g in range(G):
                        last = nc.tensor.matmul(K.bank[0][:, g * E:(g + 1) * E], K.xT[:, g, :], gate[:], start=True, stop=True)
                    last.then_inc(logits, 1)
                    nc.tensor.matmul(K.bank[1], sg[:], xT, start=True, stop=True)
                    nc.tensor.matmul(K.bank[3], su[:], xT, start=True, stop=True).then_inc(shared, 1)
                    pe.wait_ge(z_ready, 1)
                    for g in range(G):
                        last = nc.tensor.matmul(K.f_psum[:, g, :], pr[:, 0, g * T:(g + 1) * T], sd[:], start=True, stop=True)
                    last.then_inc(shared_out, 1)

                @block.scalar
                def _(act):
                    act.wait_ge(logits, 1)
                    nc.scalar.activation(sc[:].rearrange("p g e -> p (g e)"), K.bank[0][:, 0:G * E], ACT.Tanh, scale=0.5).then_inc(tanhed, 1)
                    act.wait_ge(shared, 1)
                    nc.scalar.activation(hT[:, 0, :], K.bank[1], ACT.Silu).then_inc(silued, 1)
                    act.wait_ge(shared_out, 1)
                    nc.scalar.copy(total[:], K.f_psum)

                @block.vector
                def _(dve):
                    step = Chain(dve, dve_step)
                    dve.wait_ge(tanhed, 1)
                    step(nc.vector.tensor_scalar(sc[:], sc[:], 0.5, 0.5, ALU.mult, ALU.add))
                    step(nc.vector.tensor_tensor(ch[:], sc[:], rows(bias[:], G), ALU.add))
                    for g in range(G):
                        step(nc.vector.max(m8[:, g, :], ch[:, g, :]))
                        step(nc.vector.match_replace(rp[:, g, :], m8[:, g, :], ch[:, g, :], NEG))
                    step(nc.vector.tensor_tensor(ch[:], ch[:], rp[:], ALU.not_equal))
                    step(nc.vector.tensor_tensor(sc[:], sc[:], ch[:], ALU.mult))
                    step(nc.vector.reduce_sum(sm[:], sc[:], AX))
                    step(nc.vector.reciprocal(sm[:], sm[:]))
                    step(nc.vector.tensor_scalar(sm[:], sm[:], ROUTE, None, ALU.mult))
                    step(nc.vector.tensor_tensor(sc[:], sc[:], col(sm[:], E), ALU.mult))
                    dve.wait_ge(silued, 1)
                    nc.vector.tensor_tensor(pr[:, 0, :], K.bank[3], hT[:, 0, :], ALU.mult).then_inc(z_ready, 1)
            with stage(nc, "g_dot", "u_dot", "silued", "product", "y_dot", "added") as (block, g_dot, u_dot, silued, product, y_dot, added):
                @block.tensor
                def _(pe):
                    for s in range(E + 2):
                        if s < E:
                            if s >= 2:
                                pe.wait_ge(silued, s - 1)
                                pe.wait_ge(product, s - 1)
                            nc.tensor.matmul(K.bank[s % 2], w[0][:, s, :], xT, start=True, stop=True).then_inc(g_dot, 1)
                            nc.tensor.matmul(K.bank[2 + s % 2], w[1][:, s, :], xT, start=True, stop=True).then_inc(u_dot, 1)
                        if s >= 2:
                            e = s - 2
                            pe.wait_ge(product, e + 1)
                            if e >= 2:
                                pe.wait_ge(added, G * (e - 1))
                            for g in range(G):
                                last = nc.tensor.matmul(K.bank[4 + e % 2][:, g * D:(g + 1) * D], pr[:, e % 2, g * T:(g + 1) * T], w[2][:, e, :],
                                                        start=True, stop=True)
                            last.then_inc(y_dot, 1)

                @block.scalar
                def _(act):
                    for e in range(E):
                        act.wait_ge(g_dot, e + 1)
                        if e >= 2:
                            act.wait_ge(product, e - 1)
                        nc.scalar.activation(hT[:, e % 2, :], K.bank[e % 2], ACT.Silu).then_inc(silued, 1)

                @block.vector
                def _(dve):
                    for s in range(E + 2):
                        if s < E:
                            dve.wait_ge(silued, s + 1)
                            dve.wait_ge(u_dot, s + 1)
                            if s >= 2:
                                dve.wait_ge(y_dot, s - 1)
                            nc.vector.tensor_tensor(pr[:, s % 2, :], K.bank[2 + s % 2], hT[:, s % 2, :], ALU.mult).then_inc(product, 1)
                        if s >= 2:
                            e = s - 2
                            dve.wait_ge(y_dot, e + 1)
                            if e >= 1:
                                dve.wait_ge(added, G * e)
                            for g in range(G):
                                nc.vector.scalar_tensor_tensor(out=total[:, g, :], in0=K.bank[4 + e % 2][:, g * D:(g + 1) * D],
                                                               scalar=sc[:, g, e:e + 1], in1=total[:, g, :],
                                                               op0=ALU.mult, op1=ALU.add).then_inc(added, 1)
            finish_group(K, b0, f=total[:])



TWO_PI_HI = 6.28125
TWO_PI_LO = float(2 * np.pi - 6.28125)
ROUND = 1.5 * 2.0 ** 23


def s4d_kernel(K, kern):
    nc, I = K.nc, K.ins
    N = 64
    pre = "L3_xattn_"
    with ExitStack() as es:
        sb = lambda *a: K.sb(es, *a)
        dt = sb("dt", [128, 1])
        ar, ai, cr, ci = (sb(n, [128, N]) for n in ("ar", "ai", "cr", "ci"))
        th, k_, em, ex, sn, sh, c1 = (sb(n, [128, N]) for n in ("th", "kk", "em", "ex", "sn", "sh", "c1"))
        zr, zi, t1, t2, t3, t4 = (sb(n, [128, N]) for n in ("zr", "zi", "s4t1", "s4t2", "s4t3", "s4t4"))
        wr, wi = sb("wr", [128, T, N]), sb("wim", [128, T, N])
        p1, p2 = sb("p1", [128, T // 2, N]), sb("p2", [128, T // 2, N])
        load(K, (dt[:], column(I[pre + "log_dt"])), (ar[:], I[pre + "A_re"]), (ai[:], I[pre + "A_im"]),
             (cr[:], I[pre + "C_re"]), (ci[:], I[pre + "C_im"]))
        with stage(nc, "dt_ready", "angle", "act_done", "act_step", "dve_step") as (block, dt_ready, angle, act_done, act_step, dve_step):
            mul = lambda o, a, b: nc.vector.tensor_tensor(o, a, b, ALU.mult)
            add = lambda o, a, b: nc.vector.tensor_tensor(o, a, b, ALU.add)
            sub = lambda o, a, b: nc.vector.tensor_tensor(o, a, b, ALU.subtract)

            @block.scalar
            def _(act):
                nc.scalar.activation(dt[:], dt[:], ACT.Exp).then_inc(dt_ready, 1)
                act.wait_ge(angle, 1)
                nc.scalar.activation(sn[:], th[:], ACT.Sin)
                nc.scalar.activation(sh[:], th[:], ACT.Sin, scale=0.5)
                nc.scalar.activation(em[:], ex[:], ACT.Tanh, scale=0.5)
                nc.scalar.activation(k_[:], ex[:], ACT.Exp).then_inc(act_done, 1)

            @block.vector
            def _(dve):
                step = Chain(dve, dve_step)
                dve.wait_ge(dt_ready, 1)
                step(nc.vector.tensor_scalar(ex[:], ar[:], dt[:], None, ALU.mult))
                step(nc.vector.tensor_scalar(th[:], ai[:], dt[:], None, ALU.mult))
                step(nc.vector.tensor_scalar(t1[:], th[:], float(1 / (2 * np.pi)), ROUND, ALU.mult, ALU.add))
                step(nc.vector.tensor_scalar(t1[:], t1[:], ROUND, None, ALU.subtract))
                step(nc.vector.scalar_tensor_tensor(out=th[:], in0=t1[:], scalar=-TWO_PI_HI, in1=th[:], op0=ALU.mult, op1=ALU.add))
                step(nc.vector.scalar_tensor_tensor(out=th[:], in0=t1[:], scalar=-TWO_PI_LO, in1=th[:], op0=ALU.mult, op1=ALU.add))
                nc.vector.tensor_scalar(th[:], th[:], float(np.float32(3.1415925)), float(np.float32(-3.1415925)), ALU.min, ALU.max).then_inc(angle, 1)
                dve.wait_ge(act_done, 1)
                step(nc.vector.scalar_tensor_tensor(out=em[:], in0=k_[:], scalar=1.0, in1=em[:], op0=ALU.add, op1=ALU.mult))
                step(nc.vector.tensor_scalar(ex[:], em[:], 1.0, None, ALU.add))
                step(nc.vector.scalar_tensor_tensor(out=c1[:], in0=sh[:], scalar=-2.0, in1=sh[:], op0=ALU.mult, op1=ALU.mult))
                step(nc.vector.scalar_tensor_tensor(out=zr[:], in0=c1[:], scalar=1.0, in1=em[:], op0=ALU.add, op1=ALU.mult))
                step(add(zr[:], zr[:], c1[:]))
                step(mul(zi[:], ex[:], sn[:]))
                step(mul(t1[:], ar[:], ar[:]))
                step(mul(t2[:], ai[:], ai[:]))
                step(add(t1[:], t1[:], t2[:]))
                step(nc.vector.reciprocal(t4[:], t1[:]))
                step(mul(t1[:], zr[:], ar[:]))
                step(mul(t2[:], zi[:], ai[:]))
                step(add(t1[:], t1[:], t2[:]))
                step(mul(t1[:], t1[:], t4[:]))
                step(mul(t2[:], zi[:], ar[:]))
                step(mul(t3[:], zr[:], ai[:]))
                step(sub(t2[:], t2[:], t3[:]))
                step(mul(t2[:], t2[:], t4[:]))
                step(mul(t3[:], cr[:], t1[:]))
                step(mul(t4[:], ci[:], t2[:]))
                step(sub(wr[:, 0, :], t3[:], t4[:]))
                step(mul(t3[:], cr[:], t2[:]))
                step(mul(t4[:], ci[:], t1[:]))
                step(add(wi[:, 0, :], t3[:], t4[:]))
                step(nc.vector.tensor_scalar(zr[:], zr[:], 1.0, None, ALU.add))
                m = 1
                while m < T:
                    zrb, zib = rows(zr[:], m), rows(zi[:], m)
                    step(mul(p1[:, 0:m, :], wr[:, 0:m, :], zrb))
                    step(mul(p2[:, 0:m, :], wi[:, 0:m, :], zib))
                    step(sub(wr[:, m:2 * m, :], p1[:, 0:m, :], p2[:, 0:m, :]))
                    step(mul(p1[:, 0:m, :], wr[:, 0:m, :], zib))
                    step(mul(p2[:, 0:m, :], wi[:, 0:m, :], zrb))
                    step(add(wi[:, m:2 * m, :], p1[:, 0:m, :], p2[:, 0:m, :]))
                    m *= 2
                    if m < T:
                        step(mul(t1[:], zr[:], zr[:]))
                        step(mul(t2[:], zi[:], zi[:]))
                        step(mul(t3[:], zr[:], zi[:]))
                        step(sub(zr[:], t1[:], t2[:]))
                        step(nc.vector.tensor_scalar(zi[:], t3[:], 2.0, None, ALU.mult))
                step(nc.vector.reduce_sum(kern, wr[:], AX))
                nc.vector.tensor_scalar(kern, kern, 2.0, None, ALU.mult)


def l3_xattn(K):
    nc, I = K.nc, K.ins
    H, DH, TOP = 4, 32, 32
    HID = 4 * D
    pre = "L3_xattn_"
    with ExitStack() as es:
        sb = lambda *a: K.sb(es, *a)
        kern = sb("kern", [128, T])
        s4d_kernel(K, kern[:])
        wq, wk, wv = sb("wq", [D, D]), sb("wk", [DC, D]), sb("wv", [DC, D])
        film = sb("film", [D, 2, 2 * D])
        cl = sb("cl", [D, 11])
        w1 = sb("w1", [D, HID])
        b1 = sb("b1", [128, HID // 128])
        w2 = sb("w2", [128, HID // 128, D])
        b2 = sb("b2", [D, 1])
        mod = sb("mod", [128, 1])
        gb_out = sb("gb_out", [128, 2, D])
        vm_bytes = sb("vm_bytes", [128, NB * NC_ // 4], I32)
        vm_all = sb("vm_all", [128, NB, NC_])
        vm = sb("vm", [128, G, NC_])
        tm_bytes = sb("tm_bytes", [NB, T // 4], I32)
        tm_rows = sb("tm_rows", [NB, T])
        tm_all = sb("tm_all", [128, NB])
        tm = sb("tm", [128, G])
        qT, kT = sb("qT", [128, G, T]), sb("kT", [128, G, NC_])
        v = sb("v", [NC_, G, D])
        s_ = sb("s", [128, G * H, NC_])
        left = sb("left", [128, G * H, NC_])
        m8 = sb("m8", [128, 4, G * H, 8])
        sm = sb("sm", [128, G * H])
        am = sb("am", [128, G, NC_])
        amT = sb("amT", [NC_, G, T])
        cT = sb("ctT", [128, G, T])
        mods = sb("mods", [128, 4, GT])
        xf = sb("xf", [128, G, T])
        y = sb("yT", [128, G, T])
        xtT = sb("xtT", [128, G, T])
        tok = sb("tok", [128, G, D])
        hid = sb("hid", [128, HID // 128, GT])
        load(K, (wq[:], I[pre + "Wq"]), (wk[:], I[pre + "Wk"]), (wv[:], I[pre + "Wv"]),
             (film[:, 0, :], I[pre + "W_film_in"]), (film[:, 1, :], I[pre + "W_film_out"]),
             (cl[:, 0:2], I[pre + "b_film_in"].rearrange("(k p) -> p k", p=128)),
             (cl[:, 2:4], I[pre + "b_film_out"].rearrange("(k p) -> p k", p=128)),
             *[(cl[:, 4 + i:5 + i], column(I[pre + n])) for i, n in enumerate(
                 ("g_norm_in", "b_norm_in", "g_norm_out", "b_norm_out", "g_ffn", "b_ffn", "D_skip"))],
             (w1[:], I[pre + "W1"]), (b1[:], I[pre + "b1"].rearrange("(c p) -> p c", p=128)),
             (w2[:], I[pre + "W2"].rearrange("(c p) d -> p c d", p=128)), (b2[:], column(I[pre + "b2"])),
             (mod[:], I[pre + "mod_gate"].partition_broadcast(128)),
             (gb_out[:, 0, :], I[pre + "g_norm_out"].partition_broadcast(128)), (gb_out[:, 1, :], I[pre + "b_norm_out"].partition_broadcast(128)),
             (vm_bytes[:], I["mask_BxS2_bf1"].rearrange("b t -> (b t)").partition_broadcast(128)), (tm_bytes[:], I["mask_BxS_bf1"]))
        with stage(nc) as (block,):
            @block.vector
            def _(dve):
                nc.vector.tensor_scalar(vm_all[:].rearrange("p b t -> p (b t)"), vm_bytes[:].bitcast(U8), -1.0, -NEG, ALU.add, ALU.mult)
                nc.vector.tensor_copy(tm_rows[:], tm_bytes[:].bitcast(U8))
        transposed(K, lambda i: tm_rows[:], lambda i, m: tm_all[:].unsqueeze(1), NB, 1)
        flat = lambda t: t[:].rearrange("p g t -> p (g t)")
        GC = G * NC_
        with nc.Fori(0, NB // G) as i:
            b0 = i * G
            load_group(K, b0)
            context_group(K, b0)
            with stage(nc, "q_dot", "k_dot", "v_dot") as (block, q_dot, k_dot, v_dot):
                @block.tensor
                def _(pe):
                    nc.tensor.matmul(K.bank[0], wq[:], flat(K.xT), start=True, stop=True).then_inc(q_dot, 1)
                    nc.tensor.matmul(K.bank[1][:, :GC], wk[:], flat(K.cT), start=True, stop=True).then_inc(k_dot, 1)
                    for g in range(G):
                        last = nc.tensor.matmul(K.bank[2][:NC_, g * D:(g + 1) * D], K.cT[:, g, :], wv[:], start=True, stop=True)
                    last.then_inc(v_dot, 1)

                @block.scalar
                def _(act):
                    act.wait_ge(q_dot, 1)
                    nc.scalar.mul(flat(qT), K.bank[0], DH ** -0.5)
                    act.wait_ge(v_dot, 1)
                    nc.scalar.copy(flat(v), K.bank[2][:NC_, :])

                @block.vector
                def _(dve):
                    nc.vector.tensor_copy(vm[:], vm_all[:, ds(b0, G), :])
                    nc.vector.tensor_copy(tm[:], tm_all[:, ds(b0, G)])
                    dve.wait_ge(k_dot, 1)
                    nc.vector.tensor_copy(flat(kT), K.bank[1][:, :GC])
            with stage(nc, "scored") as (block, scored):
                @block.tensor
                def _(pe):
                    for h in range(H):
                        for g in range(G):
                            out = K.bank[h][:, g * 128:g * 128 + NC_]
                            nc.tensor.matmul(out, qT[DH * h:DH * h + DH, g, :], kT[DH * h:DH * h + DH, g, :], start=True, stop=False)
                            last = nc.tensor.matmul(out, K.ones[DH * h:DH * h + 1, :], vm[DH * h:DH * h + 1, g, :], start=False, stop=True)
                        last.then_inc(scored, 1)

                @block.scalar
                def _(act):
                    for h in range(H):
                        act.wait_ge(scored, h + 1)
                        nc.scalar.copy(s_[:].rearrange("p (g h) k -> p g h k", h=H)[:, :, h, :],
                                       K.bank[h].rearrange("p (g k) -> p g k", g=G)[:, :, 0:NC_])
            with stage(nc, "found", "taken", "dve_step", "exped") as (block, found, taken, dve_step, exped):
                @block.vector
                def _(dve):
                    for r in range(TOP // 8):
                        src = s_ if r == 0 else left
                        for k in range(G * H):
                            if r:
                                dve.wait_ge(taken, (r - 1) * G * H + k + 1)
                            nc.vector.max(m8[:, r, k, :], src[:, k, :]).then_inc(found, 1)
                        for k in range(G * H):
                            dve.wait_ge(found, r * G * H + k + 1)
                            nc.vector.match_replace(left[:, k, :], m8[:, r, k, :], src[:, k, :], -3e38).then_inc(taken, 1)
                    dve.wait_ge(taken, TOP // 8 * G * H)
                    step = Chain(dve, dve_step)
                    step(nc.vector.tensor_tensor(left[:], left[:], s_[:], ALU.not_equal))
                    step(nc.vector.tensor_tensor(s_[:], s_[:], col(m8[:, 0, :, 0], NC_), ALU.subtract))
                    dve.wait_ge(exped, 1)
                    step(nc.vector.tensor_tensor(s_[:], s_[:], left[:], ALU.mult))
                    step(nc.vector.reduce_sum(sm[:], s_[:], AX))
                    step(nc.vector.reciprocal(sm[:], sm[:]))
                    step(nc.vector.tensor_scalar(sm[:], sm[:], 1.0 / H, None, ALU.mult))
                    step(nc.vector.tensor_tensor(sm[:].rearrange("p (g h) -> p g h", h=H), sm[:].rearrange("p (g h) -> p g h", h=H),
                                                 col(tm[:], H), ALU.mult))
                    step(nc.vector.tensor_tensor(s_[:], s_[:], col(sm[:], NC_), ALU.mult))
                    step(nc.vector.reduce_sum(am[:], s_[:].rearrange("p (g h) k -> p g k h", h=H), AX))

                @block.scalar
                def _(act):
                    act.wait_ge(dve_step, 2)
                    nc.scalar.activation(s_[:], s_[:], ACT.Exp).then_inc(exped, 1)
            transposed(K, lambda g: am[:, g, :], lambda i, m: amT[:, i:i + m, :], T, G)
            with stage(nc, "c_dot", "c_ready", "film_dot") as (block, c_dot, c_ready, film_dot):
                @block.tensor
                def _(pe):
                    for g in range(G):
                        last = nc.tensor.matmul(K.bank[0][:, g * T:(g + 1) * T], v[:, g, :], amT[:, g, :], start=True, stop=True)
                    last.then_inc(c_dot, 1)
                    pe.wait_ge(c_ready, 1)
                    for k in range(4):
                        nc.tensor.matmul(K.bank[1 + k], film[:, k // 2, (k % 2) * D:(k % 2) * D + D], flat(cT), start=True, stop=True).then_inc(film_dot, 1)

                @block.scalar
                def _(act):
                    act.wait_ge(c_dot, 1)
                    nc.scalar.copy(flat(cT), K.bank[0]).then_inc(c_ready, 1)

                @block.vector
                def _(dve):
                    for k in range(4):
                        dve.wait_ge(film_dot, k + 1)
                        nc.vector.tensor_scalar(mods[:, k, :], K.bank[1 + k], cl[:, k:k + 1], mod[:], ALU.add, ALU.mult)
            layer_norm(K, lambda g: tok[:, g, :], lambda g: K.xg[:, g, :], D)
            transposed(K, lambda g: tok[:, g, :], lambda i, m: xf[:, i:i + m, :], T, G, scale=cl[:, 4:5], bias=cl[:, 5:6])
            with stage(nc, "dve_step") as (block, dve_step):
                @block.vector
                def _(dve):
                    step = Chain(dve, dve_step)
                    film_ = lambda t, k: (
                        step(nc.vector.scalar_tensor_tensor(out=mods[:, k, :], in0=mods[:, k, :], scalar=1.0, in1=flat(t), op0=ALU.add, op1=ALU.mult)),
                        step(nc.vector.tensor_tensor(flat(t), mods[:, k, :], mods[:, k + 1, :], ALU.add)))
                    film_(xf, 0)
                    step(nc.vector.tensor_scalar(y[:], xf[:], cl[:, 10:11], None, ALU.mult))
                    for l in range(T):
                        step(nc.vector.scalar_tensor_tensor(out=y[:, :, l:T], in0=xf[:, :, 0:T - l], scalar=kern[:, l:l + 1], in1=y[:, :, l:T],
                                                            op0=ALU.mult, op1=ALU.add))
                    film_(y, 2)
                    step(nc.vector.tensor_tensor(xtT[:], K.xT[:], y[:], ALU.add))
            transposed(K, lambda g: xtT[:, g, :], lambda i, m: tok[:, i:i + m, :], T, G)
            layer_norm(K, lambda g: K.y[:, g, :], lambda g: tok[:, g, :], D)
            transposed(K, lambda g: K.y[:, g, :], lambda i, m: xf[:, i:i + m, :], T, G, scale=cl[:, 8:9], bias=cl[:, 9:10])
            with stage(nc, "h_dot", "gelued", "o_dot") as (block, h_dot, gelued, o_dot):
                @block.tensor
                def _(pe):
                    for c in range(HID // 128):
                        nc.tensor.matmul(K.bank[c], w1[:, c * 128:(c + 1) * 128], flat(xf), start=True, stop=True).then_inc(h_dot, 1)
                    for c in range(HID // 128):
                        pe.wait_ge(gelued, c + 1)
                        last = nc.tensor.matmul(K.bank[4], w2[:, c, :], hid[:, c, :], start=(c == 0), stop=(c == HID // 128 - 1))
                    last.then_inc(o_dot, 1)

                @block.scalar
                def _(act):
                    for c in range(HID // 128):
                        act.wait_ge(h_dot, c + 1)
                        nc.scalar.activation(hid[:, c, :], K.bank[c], ACT.Gelu, bias=b1[:, c:c + 1]).then_inc(gelued, 1)

                @block.vector
                def _(dve):
                    dve.wait_ge(o_dot, 1)
                    nc.vector.scalar_tensor_tensor(out=flat(xtT), in0=K.bank[4], scalar=b2[:], in1=flat(xtT), op0=ALU.add, op1=ALU.add)
            transposed(K, lambda g: xtT[:, g, :], lambda i, m: tok[:, i:i + m, :], T, G)
            layer_norm(K, lambda g: tok[:, g, :], lambda g: tok[:, g, :], D)
            with stage(nc, "dve_step") as (block, dve_step):
                @block.vector
                def _(dve):
                    step = Chain(dve, dve_step)
                    step(nc.vector.tensor_tensor(tok[:], tok[:], rows(gb_out[:, 0, :], G), ALU.mult))
                    nc.vector.tensor_tensor(tok[:], tok[:], rows(gb_out[:, 1, :], G), ALU.add)
            finish_group(K, b0, f=tok[:])


PHASES = {0: l0_attn, 1: l0_xattn, 2: l0_ffn, 3: l1_attn, 5: l1_ffn, 6: l2_attn, 4: l1_xattn, 7: l2_xattn, 8: l2_ffn, 10: l3_xattn, 11: l3_ffn, 9: l3_attn}
_T = lambda a: np.ascontiguousarray(np.swapaxes(a, -1, -2))
LAYOUT = {"L2_ffn_gate_w": _T, "L2_ffn_w1": _T, "L2_ffn_w2": _T, "L2_ffn_w3": _T, "L2_ffn_b1": _T, "L2_ffn_b2": _T, "L2_ffn_b3": _T,
          "L2_ffn_sw1": _T, "L2_ffn_sw2": _T, "L2_ffn_sw3": _T,
          **{"L3_ffn_" + n: _T for n in ("gate_w", "w_gate", "w_up", "w_down", "shared_gate_w", "shared_up_w", "shared_down_w")},
          "L2_attn_in_proj_w": _T, "L2_attn_dt_proj_w": _T, "L2_attn_out_proj_w": _T, "L1_ffn_expert_down": _T,
          "L0_xattn_Wq": _T, "L0_xattn_Wkv": _T, "L0_xattn_Wlkv": _T, "L0_xattn_Wo": _T}


def program(nc, ins, out, phases=range(12)):
    with ExitStack() as es:
        K = Core(nc, ins, out, es)
        constants(K)
        load(K, (K.x_all[:], ins["x"].rearrange("b t d -> t b d")))
        load_context(K)
        for n in phases:
            K.prefix = PHASES[n].__name__ + "_"
            PHASES[n](K)
        with stage(nc, "stored") as (block, stored):
            @block.sync
            def _(sp):
                sp.dma_start(out.rearrange("b t d -> t b d"), K.x_all[:]).then_inc(stored, 16)
                sp.wait_ge(stored, 16)



def kernel(**inputs):
    import concourse.bacc as bacc
    from concourse.bass_utils import run_bass_kernel_spmd as run

    nc = bacc.Bacc("TRN2", target_bir_lowering=False, num_devices=1)
    arrays, ins = {}, {}
    for name, value in [*inputs.items(), ("rotary", rotary_tables())]:
        a = np.asarray(value)
        if a.dtype == np.bool_:
            a = a.view(np.int32)
        if a.ndim == 0:
            a = a.reshape(1)
        a = np.ascontiguousarray(LAYOUT[name](a) if name in LAYOUT else a)
        arrays[f"in_{name}"] = a
        ins[name] = nc.dram_tensor(f"in_{name}", a.shape, mybir.dt.from_np(a.dtype), kind="ExternalInput").ap()
    out = nc.dram_tensor("out", (NB, T, D), F32, kind="ExternalOutput").ap()
    program(nc, ins, out)
    return run(nc, [arrays], core_ids=[0]).results[0]["out"]
```
